# Optimizing a Trainium2 kernel written in Bass

```python
import numpy as np
import jax
import jax.numpy as jnp

def _softmax(x, axis=-1):
    return jax.nn.softmax(x, axis=axis)

def _gelu(x):
    return jax.nn.gelu(x, approximate=True)

def _silu(x):
    return jax.nn.silu(x)

def _sigmoid(x):
    return jax.nn.sigmoid(x)

def _layernorm(x, axis=-1, eps=1e-05):
    m = jnp.mean(x, axis=axis, keepdims=True)
    v = jnp.var(x, axis=axis, keepdims=True)
    return (x - m) / jnp.sqrt(v + eps)

def _scatter_add(tgt, idx, src, axis=0):
    return tgt.at[idx].add(src)

def _segment_sum(src, seg, n):
    return jax.ops.segment_sum(src, seg, n)
kernel_name = 'mk_gnn_resnorm_d4_gnn_r32_f0f7fb'

def setup_inputs(seed: int=0):
    np.random.seed(seed)
    _w = jnp.asarray

    def _rec_inputs():
        import jax
        import jax.numpy as jnp
        _gk = jax.random.key(seed)
        x = -0.0005121 + 1.001 * jax.random.normal(jax.random.fold_in(_gk, 1), (3125, 64), jnp.float32)
        _s = jax.random.randint(jax.random.fold_in(_gk, 2), (50000,), 0, 3125, jnp.int32)
        _d = jax.random.randint(jax.random.fold_in(_gk, 3), (50000,), 0, 3125, jnp.int32)
        _loop = jnp.arange(3125, dtype=jnp.int32)
        src = jnp.concatenate([_s, _d, _loop])
        dst = jnp.concatenate([_d, _s, _loop])
        _o = jnp.argsort(dst, stable=True)
        src = src[_o]
        dst = dst[_o]
        edge_attr_3 = 0.000438201 + 0.99985 * jax.random.normal(jax.random.fold_in(_gk, 12), (103125, 3), jnp.float32)
        edge_attr_32 = 0.000189758 + 1.00013 * jax.random.normal(jax.random.fold_in(_gk, 13), (103125, 32), jnp.float32)
        edge_attr_64 = -6.74381e-05 + 0.999835 * jax.random.normal(jax.random.fold_in(_gk, 14), (103125, 64), jnp.float32)
        edge_weight = jax.random.uniform(jax.random.fold_in(_gk, 16), (103125,), jnp.float32, 0.0, 0.999999)
        return (x, src, dst, edge_attr_3, edge_attr_32, edge_attr_64, edge_weight)
    x, src, dst, edge_attr_3, edge_attr_32, edge_attr_64, edge_weight = _rec_inputs()

    def _L0_gnn_setup():
        import jax, jax.numpy as jnp
        import numpy as np
        N_NODES = 50000
        N_EDGES = 15625
        FEAT = 64
        HEADS = 4
        key = jax.random.key(seed)
        ks = jax.random.split(key, 8)
        x = jax.random.normal(ks[0], (N_NODES, FEAT), jnp.float32)
        edge_index = jax.random.randint(ks[1], (2, N_EDGES), 0, N_NODES)
        edge_vec = jax.random.normal(ks[2], (N_EDGES, 3), jnp.float32)
        edge_len = jax.random.uniform(ks[3], (N_EDGES,), jnp.float32)
        w_proj = jax.random.normal(ks[4], (HEADS, FEAT, FEAT), jnp.float32) / np.float32(np.sqrt(FEAT))
        xav = np.float32(np.sqrt(6.0 / (HEADS + FEAT)))
        radial_score = jax.random.uniform(ks[5], (HEADS, FEAT), jnp.float32, -xav, xav)
        tangential_score = jax.random.uniform(ks[6], (HEADS, FEAT), jnp.float32, -xav, xav)
        radial_distance_scale = jnp.array(1.0, jnp.float32)
        w_out = jax.random.normal(ks[7], (FEAT, FEAT), jnp.float32) / np.float32(np.sqrt(FEAT))
        return {'x': x, 'edge_index': edge_index, 'edge_vec': edge_vec, 'edge_len': edge_len, 'w_proj': w_proj, 'radial_score': radial_score, 'tangential_score': tangential_score, 'radial_distance_scale': radial_distance_scale, 'w_out': w_out}
    _L0_gnn_all = _L0_gnn_setup()
    _L0_gnn_in = {k: v for k, v in _L0_gnn_all.items() if k in ('w_proj', 'radial_score', 'tangential_score', 'radial_distance_scale', 'w_out')}
    del _L0_gnn_all

    def _L1_gnn_setup():
        import jax, jax.numpy as jnp
        import numpy as np
        N, E, D = (3125, 50000, 64)
        L = 3
        EPS = 1e-05

        def _layer_norm(h, g, b):
            mu = jnp.mean(h, axis=-1, keepdims=True)
            var = jnp.var(h, axis=-1, keepdims=True)
            return (h - mu) * jax.lax.rsqrt(var + EPS) * g + b
        key = jax.random.key(seed)
        ks = jax.random.split(key, 8)
        s = 0.05
        return {'x': jax.random.normal(ks[0], (N, D), jnp.float32), 'edge_src': jax.random.randint(ks[1], (E,), 0, N, jnp.int32), 'edge_dst': jax.random.randint(ks[2], (E,), 0, N, jnp.int32), 'w_l': (jax.random.normal(ks[3], (L, D, D)) * s).astype(jnp.float32), 'b_l': jnp.zeros((L, D), jnp.float32), 'w_r': (jax.random.normal(ks[4], (L, D, D)) * s).astype(jnp.float32), 'gamma': jnp.ones((L, D), jnp.float32), 'beta': jnp.zeros((L, D), jnp.float32), 'w_res': (jax.random.normal(ks[5], (D, D)) * s).astype(jnp.float32), 'b_res': jnp.zeros((D,), jnp.float32), 'w_fc': (jax.random.normal(ks[6], (D, D)) * s).astype(jnp.float32), 'b_fc': jnp.zeros((D,), jnp.float32)}
    _L1_gnn_all = _L1_gnn_setup()
    _L1_gnn_in = {k: v for k, v in _L1_gnn_all.items() if k in ('w_l', 'b_l', 'w_r', 'gamma', 'beta', 'w_res', 'b_res', 'w_fc', 'b_fc')}
    del _L1_gnn_all

    def _L2_gnn_setup():
        import jax, jax.numpy as jnp
        import numpy as np
        import math
        N_NODES = 50000
        N_EDGES = 50000
        DIM = 64
        HEADS = 8
        EDGE_DIM = 32

        def graph_softmax(src, index, num_segments):
            smax = jax.ops.segment_max(src, index, num_segments=num_segments)
            smax = jnp.where(jnp.isfinite(smax), smax, 0.0)
            e = jnp.exp(src - smax[index])
            ssum = jax.ops.segment_sum(e, index, num_segments=num_segments) + 1e-12
            return e / ssum[index]
        key = jax.random.key(seed)
        ks = jax.random.split(key, 12)
        s = 1.0 / math.sqrt(DIM)
        se = 1.0 / math.sqrt(EDGE_DIM)
        return {'x': jax.random.normal(ks[0], (N_NODES, DIM), jnp.float32), 'edge_index': jax.random.randint(ks[1], (2, N_EDGES), 0, N_NODES), 'edge_attr': jax.random.normal(ks[2], (N_EDGES, EDGE_DIM), jnp.float32), 'WQ': jax.random.normal(ks[3], (DIM, DIM), jnp.float32) * s, 'bQ': jnp.zeros((DIM,), jnp.float32), 'WK': jax.random.normal(ks[4], (DIM, DIM), jnp.float32) * s, 'bK': jnp.zeros((DIM,), jnp.float32), 'WV': jax.random.normal(ks[5], (DIM, DIM), jnp.float32) * s, 'bV': jnp.zeros((DIM,), jnp.float32), 'WO': jax.random.normal(ks[6], (DIM, DIM), jnp.float32) * s, 'bO': jnp.zeros((DIM,), jnp.float32), 'We1': jax.random.normal(ks[7], (EDGE_DIM, EDGE_DIM), jnp.float32) * se, 'be1': jnp.zeros((EDGE_DIM,), jnp.float32), 'We2': jax.random.normal(ks[8], (EDGE_DIM, HEADS), jnp.float32) * se, 'be2': jnp.zeros((HEADS,), jnp.float32)}
    _L2_gnn_all = _L2_gnn_setup()
    _L2_gnn_in = {k: v for k, v in _L2_gnn_all.items() if k in ('WQ', 'bQ', 'WK', 'bK', 'WV', 'bV', 'WO', 'bO', 'We1', 'be1', 'We2', 'be2')}
    del _L2_gnn_all

    def _L3_gnn_setup():
        import jax, jax.numpy as jnp
        import numpy as np
        N_NODES = 50000
        N_EDGES = 1250000
        D_FEAT = 64
        key = jax.random.key(seed)
        k1, k2, k3 = jax.random.split(key, 3)
        x = jax.random.normal(k1, (N_NODES, D_FEAT), dtype=jnp.float32)
        edge_attr = jax.random.normal(k2, (N_EDGES, D_FEAT), dtype=jnp.float32)
        edge_index = jax.random.randint(k3, (2, N_EDGES), 0, N_NODES, dtype=jnp.int64)
        return {'x': x, 'edge_attr': edge_attr, 'edge_index': edge_index}
    _L3_gnn_all = _L3_gnn_setup()
    _L3_gnn_in = {k: v for k, v in _L3_gnn_all.items() if k in ()}
    del _L3_gnn_all
    return {'x': x, 'src': src, 'dst': dst, 'edge_attr_3': edge_attr_3, 'edge_attr_32': edge_attr_32, 'edge_attr_64': edge_attr_64, 'edge_weight': edge_weight, 'L0_gnn_w_proj': _L0_gnn_in['w_proj'], 'L0_gnn_radial_score': _L0_gnn_in['radial_score'], 'L0_gnn_tangential_score': _L0_gnn_in['tangential_score'], 'L0_gnn_radial_distance_scale': _L0_gnn_in['radial_distance_scale'], 'L0_gnn_w_out': _L0_gnn_in['w_out'], 'L1_gnn_w_l': _L1_gnn_in['w_l'], 'L1_gnn_b_l': _L1_gnn_in['b_l'], 'L1_gnn_w_r': _L1_gnn_in['w_r'], 'L1_gnn_gamma': _L1_gnn_in['gamma'], 'L1_gnn_beta': _L1_gnn_in['beta'], 'L1_gnn_w_res': _L1_gnn_in['w_res'], 'L1_gnn_b_res': _L1_gnn_in['b_res'], 'L1_gnn_w_fc': _L1_gnn_in['w_fc'], 'L1_gnn_b_fc': _L1_gnn_in['b_fc'], 'L2_gnn_WQ': _L2_gnn_in['WQ'], 'L2_gnn_bQ': _L2_gnn_in['bQ'], 'L2_gnn_WK': _L2_gnn_in['WK'], 'L2_gnn_bK': _L2_gnn_in['bK'], 'L2_gnn_WV': _L2_gnn_in['WV'], 'L2_gnn_bV': _L2_gnn_in['bV'], 'L2_gnn_WO': _L2_gnn_in['WO'], 'L2_gnn_bO': _L2_gnn_in['bO'], 'L2_gnn_We1': _L2_gnn_in['We1'], 'L2_gnn_be1': _L2_gnn_in['be1'], 'L2_gnn_We2': _L2_gnn_in['We2'], 'L2_gnn_be2': _L2_gnn_in['be2']}

def reference(x, src, dst, edge_attr_3, edge_attr_32, edge_attr_64, edge_weight, L0_gnn_w_proj, L0_gnn_radial_score, L0_gnn_tangential_score, L0_gnn_radial_distance_scale, L0_gnn_w_out, L1_gnn_w_l, L1_gnn_b_l, L1_gnn_w_r, L1_gnn_gamma, L1_gnn_beta, L1_gnn_w_res, L1_gnn_b_res, L1_gnn_w_fc, L1_gnn_b_fc, L2_gnn_WQ, L2_gnn_bQ, L2_gnn_WK, L2_gnn_bK, L2_gnn_WV, L2_gnn_bV, L2_gnn_WO, L2_gnn_bO, L2_gnn_We1, L2_gnn_be1, L2_gnn_We2, L2_gnn_be2):
    import jax
    import jax.numpy as jnp

    def _L0_gnn_ref(x, edge_index, edge_vec, edge_len, w_proj, radial_score, tangential_score, radial_distance_scale, w_out):
        import jax, jax.numpy as jnp
        import numpy as np
        N_NODES = 50000
        N_EDGES = 15625
        FEAT = 64
        HEADS = 4
        sender, receiver = (edge_index[0], edge_index[1])
        num_nodes = x.shape[0]
        proj = jnp.einsum('nf,hfg->nhg', x, w_proj)
        delta = proj[sender] - proj[receiver]
        radial_logits = jnp.einsum('ehf,hf->eh', delta, radial_score) - radial_distance_scale * edge_len[:, None]
        tangential_logits = jnp.einsum('ehf,hf->eh', delta, tangential_score)

        def seg_softmax_msg(logits):
            m = jax.ops.segment_max(logits, receiver, num_segments=num_nodes)
            e = jnp.exp(logits - m[receiver])
            s = jax.ops.segment_sum(e, receiver, num_segments=num_nodes)
            alpha = e / s[receiver]
            return jax.ops.segment_sum(alpha[:, :, None] * delta, receiver, num_segments=num_nodes)
        out = seg_softmax_msg(radial_logits) + seg_softmax_msg(tangential_logits)
        out = out.mean(axis=1)
        out = jnp.nan_to_num(out)
        return x + out @ w_out

    def _L1_gnn_ref(x, edge_src, edge_dst, w_l, b_l, w_r, gamma, beta, w_res, b_res, w_fc, b_fc):
        import jax, jax.numpy as jnp
        import numpy as np
        N, E, D = (3125, 50000, 64)
        L = 3
        EPS = 1e-05

        def _layer_norm(h, g, b):
            mu = jnp.mean(h, axis=-1, keepdims=True)
            var = jnp.var(h, axis=-1, keepdims=True)
            return (h - mu) * jax.lax.rsqrt(var + EPS) * g + b
        n = x.shape[0]
        deg = jax.ops.segment_sum(jnp.ones(edge_dst.shape, x.dtype), edge_dst, num_segments=n)
        inv_deg = jnp.where(deg > 0, 1.0 / jnp.maximum(deg, 1.0), 0.0)[:, None]
        for i in range(L):
            residual = x @ w_res + b_res if i == 0 else x
            agg = jax.ops.segment_sum(x[edge_src], edge_dst, num_segments=n) * inv_deg
            h = agg @ w_l[i] + b_l[i] + x @ w_r[i]
            h = jax.nn.relu(_layer_norm(h, gamma[i], beta[i]))
            x = h + residual
        return x @ w_fc + b_fc

    def _L2_gnn_ref(x, edge_index, edge_attr, WQ, bQ, WK, bK, WV, bV, WO, bO, We1, be1, We2, be2):
        import jax, jax.numpy as jnp
        import numpy as np
        import math
        N_NODES = 50000
        N_EDGES = 50000
        DIM = 64
        HEADS = 8
        EDGE_DIM = 32

        def graph_softmax(src, index, num_segments):
            smax = jax.ops.segment_max(src, index, num_segments=num_segments)
            smax = jnp.where(jnp.isfinite(smax), smax, 0.0)
            e = jnp.exp(src - smax[index])
            ssum = jax.ops.segment_sum(e, index, num_segments=num_segments) + 1e-12
            return e / ssum[index]
        num_nodes = x.shape[0]
        d_k = DIM // HEADS
        i, j = (edge_index[0], edge_index[1])
        Q = (x @ WQ + bQ).reshape(num_nodes, HEADS, d_k)
        K = (x @ WK + bK).reshape(num_nodes, HEADS, d_k)
        V = (x @ WV + bV).reshape(num_nodes, HEADS, d_k)
        query = Q[j]
        key = K[i]
        value = V[i]
        h = jax.nn.silu(edge_attr @ We1 + be1)
        bias = h @ We2 + be2
        scores = jnp.sum(query * key, axis=-1) / math.sqrt(d_k) + bias
        alpha = graph_softmax(scores, j, num_nodes)
        weighted = (alpha[..., None] * value).reshape(-1, DIM)
        attn_out = jax.ops.segment_sum(weighted, j, num_segments=num_nodes)
        return attn_out @ WO + bO

    def _L3_gnn_ref(x, edge_attr, edge_index):
        import jax, jax.numpy as jnp
        import numpy as np
        N_NODES = 50000
        N_EDGES = 1250000
        D_FEAT = 64
        src = edge_index[0]
        dst = edge_index[1]
        messages = x[src] + x[dst] + edge_attr
        out = jax.ops.segment_sum(messages, dst, num_segments=x.shape[0])
        return out
    edge_index = jnp.stack([src, dst])
    x = _layernorm(x + _L0_gnn_ref(x, edge_index, edge_attr_3, edge_weight, L0_gnn_w_proj, L0_gnn_radial_score, L0_gnn_tangential_score, L0_gnn_radial_distance_scale, L0_gnn_w_out), axis=-1)
    x = _layernorm(x + _L1_gnn_ref(x, src, dst, L1_gnn_w_l, L1_gnn_b_l, L1_gnn_w_r, L1_gnn_gamma, L1_gnn_beta, L1_gnn_w_res, L1_gnn_b_res, L1_gnn_w_fc, L1_gnn_b_fc), axis=-1)
    x = _layernorm(x + _L2_gnn_ref(x, edge_index, edge_attr_32, L2_gnn_WQ, L2_gnn_bQ, L2_gnn_WK, L2_gnn_bK, L2_gnn_WV, L2_gnn_bV, L2_gnn_WO, L2_gnn_bO, L2_gnn_We1, L2_gnn_be1, L2_gnn_We2, L2_gnn_be2), axis=-1)
    x = _layernorm(x + _L3_gnn_ref(x, edge_attr_64, edge_index), axis=-1)
    return x

_drawn_inputs = setup_inputs


def setup_inputs(seed=0):
    import zlib

    import numpy as np

    out = dict(_drawn_inputs(seed))
    spreads = {'L1_gnn_b_l': (0.0, 0.1),
     'L1_gnn_gamma': (1.0, 0.2),
     'L1_gnn_beta': (0.0, 0.1),
     'L1_gnn_b_res': (0.0, 0.1),
     'L1_gnn_b_fc': (0.0, 0.1),
     'L2_gnn_bQ': (0.0, 0.383),
     'L2_gnn_bK': (0.0, 0.8),
     'L2_gnn_bV': (0.0, 0.1),
     'L2_gnn_bO': (0.0, 0.1),
     'L2_gnn_be1': (0.0, 0.8),
     'L2_gnn_be2': (0.0, 0.8)}
    factors = {'edge_weight': 4.485}
    for name, (base, spread) in spreads.items():
        noise = np.random.default_rng([zlib.crc32(name.encode()), seed]).standard_normal(out[name].shape)
        drawn = base * np.exp(spread * noise) if base else spread * noise
        out[name] = jnp.asarray(drawn.astype(out[name].dtype))
    for name, factor in factors.items():
        out[name] = (out[name] * factor).astype(out[name].dtype)
    return out
```

```python
import concourse.bass as bass
from concourse import mybir
from contextlib import ExitStack, contextmanager

F32 = mybir.dt.float32
BF16 = mybir.dt.bfloat16
F16 = mybir.dt.float16
I32 = mybir.dt.int32
ALU = mybir.AluOpType
ACT = mybir.ActivationFunctionType
AX = mybir.AxisListType.X
RMAX = bass.bass_isa.ReduceOp.max

P = 128
N, E, F = 3125, 103125, 64
WN = 125
NW = N // WN
T = 8
H = 4
GE = P * T
NG = -(-E // GE)
LAST = E - GE
DUP = NG * GE - E
HEADS0, HEADS2, DK = 4, 8, 8
A0 = 2 * HEADS0
ROW0 = F + A0
ED = 32
U = 5
TINY = 1e-30
EPS = 1e-5
BANK = 512


class Phase:

    def __init__(self, nc, name):
        self.nc, self.name, self.ctx, self.sems = nc, name, ExitStack(), []

    def __enter__(self):
        self.ctx.__enter__()
        return self

    def __exit__(self, *a):
        done = self.ctx.__exit__(*a)
        if self.sems and a[0] is None:
            self.nc.clear_and_free_semaphores(self.sems)
            self.nc.all_engine_barrier()
        return done

    def sb(self, name, shape, dt=F32):
        return self.ctx.enter_context(self.nc.sbuf_tensor(f"{self.name}_{name}", shape, dt))

    def ps(self, name, shape, dt=F32):
        return self.ctx.enter_context(self.nc.psum_tensor(f"{self.name}_{name}", shape, dt))

    def sem(self, name):
        self.sems.append(self.nc.alloc_semaphore(f"{self.name}_{name}"))
        return self.sems[-1]



class Chain:

    def __init__(self, eng, sem, base=0):
        self.eng, self.sem, self.n, self.base = eng, sem, 0, base

    def __call__(self, ins):
        ins.then_inc(self.sem, 1)
        self.n += 1
        self.eng.wait_ge(self.sem, self.base + self.n)
        return ins


def grouped(a):
    return a[0:(NG - 1) * GE].rearrange("(g p j) -> p g j", p=P, j=T)


def node_linear(nc, tag, src, chunks, weights, fout, bias, dst, scale=None):
    with Phase(nc, tag) as ph:
        nk = len(chunks)
        width = max(c for _, c in chunks)
        fin = sum(c for _, c in chunks)
        turns = NW // U
        staged = ph.sb("staged", [WN, U, fin])
        turned = ph.sb("turned", [P, U, nk, P])
        turned_ps = ph.ps("turned_ps", [P, 8, nk, P])
        out_ps = ph.ps("out_ps", [WN, 6, 256])
        s_go = ph.sem("s_go")
        s_staged, s_turned_ps, s_turned, s_out_ps, s_out = (
            ph.sem(n) for n in ("s_staged", "s_turned_ps", "s_turned", "s_out_ps", "s_out"))
        block = ph.ctx.enter_context(nc.Block())

        @block.gpsimd
        def _(pool):
            with pool.Fori(0, turns) as i:
                pool.wait_ge(s_turned_ps, i + 1)
                pool.tensor_copy(staged[:, :, :], src[:, bass.ds(i * U, U), 0:fin]).then_inc(s_staged, 1)

        @block.tensor
        def _(pe):
            pe.sem_inc(s_turned_ps, 1)
            with pe.Fori(0, turns) as i:
                pe.wait_ge(s_staged, i + 1)
                pe.wait_ge(s_turned, i + 1)
                pe.sem_inc(s_go, 1)
                for u in range(U):
                    for k, (c0, cw) in enumerate(chunks):
                        last = nc.tensor.transpose(turned_ps[0:cw, u, k, 0:WN], staged[:, u, c0:c0 + cw],
                                                   nc_ident(nc)[0:WN, 0:WN])
                last.then_inc(s_turned_ps, 1)
                pe.wait_ge(s_turned, i + 2)
                pe.wait_ge(s_out, i + 1)
                for u in range(U):
                    for k, (c0, cw) in enumerate(chunks):
                        last = nc.tensor.matmul(out_ps[:, u, 0:fout], turned[0:cw, u, k, 0:WN], weights(k),
                                                start=(k == 0), stop=(k == nk - 1))
                last.then_inc(s_out_ps, 1)

        @block.scalar
        def _(act):
            act.sem_inc(s_turned, 1)
            act.sem_inc(s_out_ps, 1)
            with act.Fori(0, turns) as i:
                act.wait_ge(s_turned_ps, i + 2)
                act.wait_ge(s_out_ps, i + 1)
                act.copy(turned[0:width, :, :, 0:WN], turned_ps[0:width, 0:U, :, 0:WN]).then_inc(s_turned, 1)

        @block.vector
        def _(dve):
            dve.sem_inc(s_out, 1)
            with dve.Fori(0, turns) as i:
                dve.wait_ge(s_out_ps, i + 2)
                to, by = dst[:, bass.ds(i * U, U), 0:fout], 1.0 if scale is None else scale
                if bias is None:
                    dve.tensor_scalar(to, out_ps[:, 0:U, 0:fout], by, None, ALU.mult).then_inc(s_out, 1)
                else:
                    dve.scalar_tensor_tensor(to, out_ps[:, 0:U, 0:fout], by,
                                             bias.unsqueeze(1).broadcast_to([WN, U, fout]),
                                             ALU.mult, ALU.add).then_inc(s_out, 1)


_IDENT = {}


def nc_ident(nc):
    return _IDENT["ident"]


def over(ap, n):
    return ap.unsqueeze(2).broadcast_to([ap.shape[0], ap.shape[1], n])


class Norm:

    def __init__(self, ph, name, stat, minus_half):
        self.stat, self.minus_half = stat, minus_half
        self.s_var, self.s_rstd = ph.sem(f"{name}_s_var"), ph.sem(f"{name}_s_rstd")

    def on_gpsimd(self, pool):
        pool.wait_ge(self.s_var, 1)
        pool.tensor_tensor(self.stat[:, 0, :], self.stat[:, 1, :], self.minus_half[0:WN, 0:NW], ALU.pow).then_inc(self.s_rstd, 1)

    def on_vector(self, step, dve, y, out, tmp):
        stat = self.stat
        step(dve.tensor_reduce(stat[:, 0, :], y, AX, ALU.add))
        step(dve.tensor_scalar(stat[:, 1, :], stat[:, 0, :], 1.0 / F, None, ALU.mult))
        step(dve.tensor_tensor(y, y, over(stat[:, 1, :], F), ALU.subtract))
        step(dve.tensor_tensor(tmp, y, y, ALU.mult))
        step(dve.tensor_reduce(stat[:, 0, :], tmp, AX, ALU.add))
        dve.tensor_scalar(stat[:, 1, :], stat[:, 0, :], 1.0 / F, EPS, ALU.mult, ALU.add).then_inc(self.s_var, 1)
        dve.wait_ge(self.s_rstd, 1)
        step(dve.tensor_tensor(out, y, over(stat[:, 0, :], F), ALU.mult))


def build(nc, a, out, stop=99):
    with Phase(nc, "all") as whole:
        sb, sem = whole.sb, whole.sem
        table0 = nc.dram_tensor("table0", [N, ROW0], F32).ap()
        table_kv = nc.dram_tensor("table_kv", [N, 2 * F], F32).ap()
        edge_sum = nc.dram_tensor("edge_sum", [WN, NW, F], F32).ap()
        counts_t = nc.dram_tensor("counts_t", [NW, WN, NW * WN], BF16).ap()

        ident = sb("ident", [P, P])
        _IDENT["ident"] = ident
        ident16 = sb("ident16", [P, P], BF16)
        iota_n = sb("iota_n", [P, WN])
        window_start = sb("window_start", [P, NW])
        x = sb("x", [WN, NW, F])
        src_i = sb("src_i", [P, NG, T], I32)
        dst_f = sb("dst_f", [P, NG, T])
        visits = sb("visits", [P, 3, NW], I32)
        starts = sb("starts", [P, NG], I32)
        deg = sb("deg", [WN, NW])
        stat = sb("stat", [WN, 2, NW])
        minus_half = sb("minus_half", [P, NW])
        half = sb("half", [P, HEADS2])

        def loop_windows(eng, body, before=None, after=None):
            with eng.Fori(0, NW) as w:
                lo = eng.value_load(visits[0:1, 0, bass.ds(w, 1)], min_val=0, max_val=NG - 1)
                end = eng.value_load(visits[0:1, 1, bass.ds(w, 1)], min_val=1, max_val=NW * NG)
                cum = eng.value_load(visits[0:1, 2, bass.ds(w, 1)], min_val=0, max_val=NW * NG)
                if before:
                    before(w)
                with eng.Fori(cum, end) as v:
                    body(w, nc.s_assert_within(eng.snap(v - cum + lo), 0, NG - 1, skip_runtime_bounds_check_because=
                                                "each window's visits are groups that exist"), v)
                if after:
                    after(w, end)

        with Phase(nc, "plan") as ph:
            dst_i = ph.sb("dst_i", [P, NG, T], I32)
            ramp = ph.sb("ramp", [P, NG * 2], I32)
            ramp_f = ph.sb("ramp_f", [P, NG * 2])
            dup = ph.sb("dup", [P, 3, T])
            ends = ph.sb("ends", [P, 2, NG])
            ends_all = ph.sb("ends_all", [P, 2, NG])
            touch = ph.sb("touch", [P, 3, NW, NG])
            wf = ph.sb("wf", [P, 6, NW])
            ones = ph.sb("ones", [P, NW])
            s_ld, s_pool, s_ch = ph.sem("s_ld"), ph.sem("s_pool"), ph.sem("s_ch")
            s_ends = ph.sem("s_ends")
            s_all = ph.sem("s_all")
            block = ph.ctx.enter_context(nc.Block())

            @block.sync
            def _(sp):
                with nc.allow_non_contiguous_dma("runs of eight edges"):
                    for to, fro in ((src_i, a["src"]), (dst_i, a["dst"])):
                        sp.dma_start(to[:, 0:NG - 1, :], grouped(fro)).then_inc(s_ld, 16)
                        sp.dma_start(to[:, NG - 1, :], fro[LAST:E].rearrange("(p j) -> p j", j=T)).then_inc(s_ld, 16)
                    sp.dma_start(x[:, :, :], a["x"].rearrange("(w p) f -> p w f", p=WN)).then_inc(s_ld, 16)
                sp.wait_ge(s_ld, 80)

            @block.gpsimd
            def _(pool):
                step = Chain(pool, s_pool)
                step(pool.memset(ident[:, :], 0.0))
                step(pool.affine_select(out=ident[:, :], in_=ident[:, :], compare_op=ALU.not_equal, fill=1.0,
                                        base=0, pattern=[[-1, P]], channel_multiplier=1))
                step(pool.tensor_copy(ident16[:, :], ident[:, :]))
                step(pool.iota(ramp[:, :], [[1, 2 * NG]], base=0, channel_multiplier=0))
                step(pool.tensor_copy(ramp_f[:, :], ramp[:, :]))
                step(pool.tensor_copy(iota_n[:, :], ramp_f[:, 0:WN]))
                step(pool.tensor_scalar(window_start[:, :], ramp_f[:, 0:NW], float(WN), None, ALU.mult))
                step(pool.iota(ramp[:, 0:T], [[1, T]], base=0, channel_multiplier=T))
                step(pool.tensor_copy(dup[:, 0, :], ramp[:, 0:T]))
                pool.memset(minus_half[:, :], -0.5)
                pool.memset(half[:, :], 0.5)
                pool.wait_ge(s_ends, 1)
                pool.partition_all_reduce(ends_all[:, :, :].rearrange("p a g -> p (a g)"),
                                          ends[:, :, :].rearrange("p a g -> p (a g)"), P, RMAX).then_inc(s_all, 1)

            @block.vector
            def _(dve):
                step = Chain(dve, s_ch)
                dve.wait_ge(s_ld, 80)
                dve.wait_ge(s_pool, 9)
                step(dve.memset(ones[:, :], 1.0))
                step(dve.tensor_copy(dst_f[:, :, :], dst_i[:, :, :]))
                last = dst_f[:, NG - 1, :]
                step(dve.tensor_scalar(dup[:, 1, :], dup[:, 0, :], float(DUP), None, ALU.is_ge))
                step(dve.tensor_scalar(last, last, 1.0, None, ALU.add))
                step(dve.tensor_tensor(last, last, dup[:, 1, :], ALU.mult))
                step(dve.tensor_scalar(last, last, -1.0, None, ALU.add))
                step(dve.tensor_reduce(ends[:, 0, :], dst_f[:, :, :], AX, ALU.max))
                step(dve.tensor_reduce(ends[:, 1, :], dst_f[:, :, :], AX, ALU.min))
                step(dve.tensor_scalar(dup[:, 2, :], dup[:, 1, :], -2.0 * N, 2.0 * N, ALU.mult, ALU.add))
                step(dve.tensor_tensor(dup[:, 2, :], dup[:, 2, :], last, ALU.add))
                step(dve.tensor_reduce(ends[:, 1, NG - 1:NG], dup[:, 2, :], AX, ALU.min))
                dve.tensor_scalar(ends[:, 1, :], ends[:, 1, :], -1.0, None, ALU.mult).then_inc(s_ends, 1)
                dve.wait_ge(s_all, 1)
                step(dve.tensor_scalar(ends[:, 1, :], ends_all[:, 1, :], -1.0, None, ALU.mult))
                step(dve.tensor_scalar(wf[:, 5, :], window_start[:, :], float(WN - 1), None, ALU.add))

                def by_window(ap):
                    return ap.unsqueeze(1).broadcast_to([P, NW, NG])

                step(dve.tensor_tensor(touch[:, 0], by_window(ends_all[:, 0, :]), over(window_start[:, :], NG), ALU.is_ge))
                step(dve.tensor_tensor(touch[:, 1], by_window(ends[:, 1, :]), over(wf[:, 5, :], NG), ALU.is_le))
                step(dve.tensor_tensor(touch[:, 0], touch[:, 0], touch[:, 1], ALU.mult))
                step(dve.tensor_tensor(touch[:, 1], touch[:, 0], by_window(ramp_f[:, 1:NG + 1]), ALU.mult))
                step(dve.tensor_reduce(wf[:, 0, :], touch[:, 1], AX, ALU.max))
                step(dve.tensor_scalar(wf[:, 0, :], wf[:, 0, :], 1.0, None, ALU.max))
                step(dve.tensor_scalar(ends[:, 0, :], ramp_f[:, 0:NG], -1.0, float(NG), ALU.mult, ALU.add))
                step(dve.tensor_tensor(touch[:, 1], touch[:, 0], by_window(ends[:, 0, :]), ALU.mult))
                step(dve.tensor_reduce(wf[:, 1, :], touch[:, 1], AX, ALU.max))
                step(dve.tensor_scalar(wf[:, 1, :], wf[:, 1, :], -1.0, float(NG), ALU.mult, ALU.add))
                step(dve.tensor_scalar(wf[:, 2, :], wf[:, 0, :], -1.0, None, ALU.add))
                step(dve.tensor_tensor(wf[:, 1, :], wf[:, 1, :], wf[:, 2, :], ALU.min))
                step(dve.tensor_tensor(wf[:, 2, :], wf[:, 0, :], wf[:, 1, :], ALU.subtract))
                step(dve.tensor_tensor_scan(wf[:, 3, :], ones[:, :], wf[:, 2, :], 0.0, ALU.mult, ALU.add))
                step(dve.tensor_tensor(wf[:, 3, :], wf[:, 3, :], wf[:, 2, :], ALU.subtract))
                step(dve.tensor_tensor(wf[:, 2, :], wf[:, 3, :], wf[:, 2, :], ALU.add))
                step(dve.tensor_copy(visits[:, :, :], wf[:, 1:4, :]))
                step(dve.tensor_scalar(ends[:, 0, :], ramp_f[:, 0:NG], float(GE), float(LAST), ALU.mult, ALU.min))
                step(dve.tensor_copy(starts[:, :], ends[:, 0, :]))


        with Phase(nc, "first") as first:
            edge_term = first.sb("edge_term", [P, NG * T, A0])
            with Phase(nc, "table") as ph:
                w_proj = ph.sb("w_proj", [F, HEADS0, F])
                score = ph.sb("score", [F, 2, HEADS0, F])
                prod = ph.sb("prod", [F, HEADS0, F])
                u = ph.sb("u", [F, A0])
                neg_c = ph.sb("neg_c", [P, 1])
                lens = ph.sb("lens", [P, NG, T])
                logits = ph.sb("logits", [WN, NW, A0])
                top = ph.sb("top", [P, A0 + 1])
                top_all = ph.sb("top_all", [P, A0 + 1])
                s_ld, s_ch = ph.sem("s_ld"), ph.sem("s_ch")
                s_top, s_all, s_st, s_neg = ph.sem("s_top"), ph.sem("s_all"), ph.sem("s_st"), ph.sem("s_neg")
                with nc.Block() as block:

                    @block.sync
                    def _(sp):
                        with nc.allow_non_contiguous_dma("runs of eight edges"):
                            ew = a["edge_weight"]
                            sp.dma_start(lens[:, 0:NG - 1, :], grouped(ew)).then_inc(s_ld, 16)
                            sp.dma_start(lens[:, NG - 1, :], ew[LAST:E].rearrange("(p j) -> p j", j=T)).then_inc(s_ld, 16)
                            sp.dma_start(w_proj[:, :, :], a["L0_gnn_w_proj"].rearrange("h f g -> f h g")).then_inc(s_ld, 16)
                            for n, name in enumerate(("L0_gnn_radial_score", "L0_gnn_tangential_score")):
                                sp.dma_start(score[:, n], a[name].partition_broadcast(F)).then_inc(s_ld, 16)
                            sp.dma_start(neg_c[:, :], a["L0_gnn_radial_distance_scale"].partition_broadcast(P)).then_inc(s_ld, 16)
                        sp.wait_ge(s_ld, 96)

                    @block.vector
                    def _(dve):
                        step = Chain(dve, s_ch)
                        dve.wait_ge(s_ld, 96)
                        for n in range(2):
                            step(dve.tensor_tensor(prod[:, :, :], w_proj[:, :, :], score[:, n], ALU.mult))
                            step(dve.tensor_reduce(u[:, n * HEADS0:(n + 1) * HEADS0], prod[:, :, :], AX, ALU.add))
                        step(dve.tensor_scalar(neg_c[:, :], neg_c[:, :], -1.0, None, ALU.mult))
                        step(dve.tensor_scalar(lens[:, :, :], lens[:, :, :], neg_c[:, 0:1], None, ALU.mult))

                node_linear(nc, "l0", x, [(0, F)], lambda k: u[:, :], A0, None, logits)

                with nc.Block() as block:

                    @block.sync
                    def _(sp):
                        t = table0.rearrange("(w p) c -> p w c", p=WN)
                        with nc.allow_non_contiguous_dma("table rows"):
                            sp.dma_start(t[:, :, 0:F], x[:, :, :]).then_inc(s_st, 16)
                            sp.dma_start(t[:, :, F:ROW0], logits[:, :, :]).then_inc(s_st, 16)
                        sp.wait_ge(s_st, 32)

                    @block.gpsimd
                    def _(pool):
                        pool.wait_ge(s_top, 1)
                        pool.partition_all_reduce(top_all[:, :], top[:, :], P, RMAX).then_inc(s_all, 1)

                    @block.vector
                    def _(dve):
                        step = Chain(dve, s_neg)
                        flat = lens[:, :, :].rearrange("p g j -> p (g j)")
                        step(dve.memset(top[:, :], -3e38))
                        step(dve.tensor_reduce(top[0:WN, 0:A0], logits[:, :, :].rearrange("p w h -> p h w"), AX, ALU.max))
                        dve.tensor_reduce(top[:, A0:A0 + 1], flat, AX, ALU.max).then_inc(s_top, 1)
                        dve.wait_ge(s_all, 1)
                        step(dve.tensor_scalar(top_all[:, 0:HEADS0], top_all[:, 0:HEADS0], top_all[:, A0:A0 + 1], None, ALU.add))
                        shift = top_all[:, 0:A0].unsqueeze(1).broadcast_to([P, NG * T, A0])
                        step(dve.memset(edge_term[:, :, HEADS0:A0], 0.0))
                        step(dve.tensor_copy(edge_term[:, :, 0:HEADS0], over(flat, HEADS0)))
                        step(dve.tensor_tensor(edge_term[:, :, :], edge_term[:, :, :], shift, ALU.subtract))

            NUM, EA, DEN, DEG, RAW = 0, A0 * F, A0 * F + F, A0 * F + F + A0, A0 * F + F + A0 + 1
            raw = first.sb("raw", [WN, NW, RAW])
            with Phase(nc, "edges0") as ph:
                zeros = ph.sb("zeros", [P, BANK], BF16)
                node_ids = ph.sb("node_ids", [P, N], F16)
                src_f = ph.sb("src_f", [P, NG * T])
                idx = ph.sb("idx", [P, 2, H], I32)
                rows = ph.sb("rows", [P, 2, H, ROW0])
                dst_rel = ph.sb("dst_rel", [P, 2, H])
                into = ph.sb("into", [P, 2, H, WN])
                into16 = ph.sb("into16", [P, 2, H, WN], BF16)
                fro = ph.sb("fro", [P, H, N], BF16)
                logit = ph.sb("logit", [P, 2, H, A0])
                prob = ph.sb("prob", [P, 2, H, A0 + 1])
                weighted = ph.sb("weighted", [P, 2, H, A0, F])
                ea = ph.sb("ea", [P, 2, H, F])
                counts = ph.sb("counts", [WN, N], BF16)
                turned = ph.sb("turned", [WN, NW, WN], BF16)
                acc = ph.ps("acc", [P, 8 * BANK])
                TAIL = N
                NUM_PS = 7 * BANK
                turned_ps = acc[:, 0:4 * BANK].bitcast(BF16).rearrange("p (c n) -> p c n", n=P)
                s_idx, s_m, s_half, s_tile = (ph.sem(n) for n in ("s_idx", "s_weighted", "s_half_done", "s_tile_done"))
                s_rows = [ph.sem(f"s_rows{h}") for h in range(2)]
                s_ea = [ph.sem(f"s_ea{h}") for h in range(2)]
                s_rel, s_into, s_into16, s_logit, s_prob, s_fro = (
                    ph.sem(n) for n in ("s_rel", "s_into", "s_into16", "s_logit", "s_prob", "s_fro"))
                s_free, s_counts, s_trps, s_turned, s_ctd, s_ctfree, s_init, s_iota, s_seen = (
                    ph.sem(n) for n in ("s_acc_free", "s_counts", "s_turned_ps", "s_turned", "s_counts_stored",
                                        "s_turned_free", "s_init", "s_iota", "s_seen"))
                with nc.Block() as block:

                    @block.sync
                    def _(sp):
                        def body(w, g, v):
                            e0 = sp.value_load(starts[0:1, bass.ds(g, 1)], min_val=0, max_val=LAST)
                            both = a["edge_attr_64"][bass.ds(e0, GE), :].rearrange("(p j) f -> p j f", j=T)
                            for h in range(2):
                                sp.wait_ge(s_half, 2 * v + h + 1)
                                sp.dma_start(ea[:, h], both[:, h * H:(h + 1) * H, :]).then_inc(s_ea[h], 16)

                        def after(w, end):
                            sp.wait_ge(s_turned, w * 4 + 4)
                            sp.dma_start(counts_t[bass.ds(w, 1)].squeeze(0),
                                         turned[:, :, :].rearrange("p c n -> p (c n)")).then_inc(s_ctd, 16)
                            sp.wait_ge(s_ctd, w * 16 + 16)
                            sp.sem_inc(s_ctfree, 1)

                        loop_windows(sp, body, after=after)

                    @block.gpsimd
                    def _(pool):
                        pool.iota(node_ids[:, :], [[1, N]], base=-(N // 2), channel_multiplier=0,
                                  allow_small_or_imprecise_dtypes=True).then_inc(s_iota, 1)

                        def body(w, g, v):
                            for h in range(2):
                                pool.wait_ge(s_m, 2 * v + h + 1)
                                pool.tensor_copy(idx[:, h, :], src_i[:, bass.ds(g, 1), h * H:(h + 1) * H].squeeze(1)).then_inc(s_idx, 1)
                                pool.wait_ge(s_idx, 2 * v + h + 1)
                                pool.sem_inc(s_seen, 1)
                                for j in range(H):
                                    pool.indirect_dma_start(rows[:, h, j, :], None, table0,
                                                            bass.IndirectOffsetOnAxis(ap=idx[:, h, j:j + 1], axis=0)).then_inc(s_rows[h], 16)

                        loop_windows(pool, body)

                    @block.vector
                    def _(dve):
                        dve.memset(zeros[:, :], 0.0).then_inc(s_init, 1)
                        dve.memset(prob[:, :, :, A0:A0 + 1], 1.0).then_inc(s_init, 1)
                        dve.tensor_scalar(src_f[:, :], src_i[:, :, :].rearrange("p g j -> p (g j)"), -float(N // 2), None,
                                          ALU.add).then_inc(s_init, 1)
                        dve.sem_inc(s_m, 2)
                        dve.wait_ge(s_init, 3)
                        dve.wait_ge(s_iota, 1)

                        def body(w, g, v):
                            for h in range(2):
                                k = 2 * v + h + 1
                                dve.wait_ge(s_half, k)
                                dve.tensor_scalar(dst_rel[:, h], dst_f[:, bass.ds(g, 1), h * H:(h + 1) * H].squeeze(1),
                                                  window_start[:, bass.ds(w, 1)], None, ALU.subtract).then_inc(s_rel, 1)
                                dve.wait_ge(s_rel, k)
                                dve.tensor_tensor(into[:, h], iota_n[:, :].unsqueeze(1).broadcast_to([P, H, WN]),
                                                  over(dst_rel[:, h], WN), ALU.is_equal).then_inc(s_into, 1)
                                dve.wait_ge(s_rows[h], 16 * H * (v + 1))
                                dve.tensor_tensor(logit[:, h], rows[:, h, :, F:ROW0],
                                                  edge_term[:, bass.ds(g * T + h * H, H), :], ALU.add).then_inc(s_logit, 1)
                                for j in range(H):
                                    dve.wait_ge(s_tile, v * T + h * H + j + 1)
                                    dve.tensor_scalar(fro[:, j, :], node_ids[:, :], src_f[:, bass.ds(g * T + h * H + j, 1)], None,
                                                      ALU.is_equal).then_inc(s_fro, 1)
                                dve.wait_ge(s_prob, k)
                                dve.tensor_tensor(weighted[:, h], rows[:, h, :, 0:F].unsqueeze(2).broadcast_to([P, H, A0, F]),
                                                  prob[:, h, :, 0:A0].unsqueeze(3).broadcast_to([P, H, A0, F]),
                                                  ALU.mult).then_inc(s_m, 1)

                        loop_windows(dve, body)

                    @block.scalar
                    def _(act):
                        act.sem_inc(s_free, 1)
                        act.wait_ge(s_init, 3)

                        def body(w, g, v):
                            for h in range(2):
                                k = 2 * v + h + 1
                                act.wait_ge(s_into, k)
                                act.copy(into16[:, h], into[:, h]).then_inc(s_into16, 1)
                                act.wait_ge(s_logit, k)
                                act.activation(prob[:, h, :, 0:A0], logit[:, h], ACT.Exp).then_inc(s_prob, 1)

                        def after(w, end):
                            act.wait_ge(s_half, 2 * end + 2)
                            act.copy(raw[:, bass.ds(w, 1), EA:RAW].squeeze(1), acc[0:WN, TAIL:TAIL + RAW - EA])
                            act.copy(raw[:, bass.ds(w, 1), NUM:EA].squeeze(1), acc[0:WN, NUM_PS:NUM_PS + EA])
                            act.copy(counts[:, :], acc[0:WN, 0:N]).then_inc(s_counts, 1)
                            act.wait_ge(s_ctfree, w + 1)
                            for b in range(4):
                                c0, c1 = 8 * b, min(8 * b + 8, NW)
                                act.wait_ge(s_trps, w * 4 + b + 1)
                                act.copy(turned[:, c0:c1, :], turned_ps[0:WN, c0:c1, 0:WN]).then_inc(s_turned, 1)
                            act.wait_ge(s_turned, w * 4 + 4)
                            act.sem_inc(s_free, 1)

                        act.sem_inc(s_ctfree, 1)
                        loop_windows(act, body, after=after)

                    @block.tensor
                    def _(pe):
                        pe.sem_inc(s_half, 2)
                        pe.sem_inc(s_tile, H)
                        pe.wait_ge(s_init, 3)

                        def before(w):
                            pe.wait_ge(s_free, w + 1)
                            for b in range(8):
                                nc.tensor.matmul(acc[0:WN, b * BANK:(b + 1) * BANK], zeros[:, 0:WN], zeros[:, :],
                                                 start=True, stop=True)

                        def add(to, lhsT, rhs):
                            return nc.tensor.matmul(to, lhsT, rhs, start=False, stop=True, skip_group_check=True)

                        def body(w, g, v):
                            for h in range(2):
                                k = 2 * v + h + 1
                                pe.wait_ge(s_into16, k)
                                for j in range(H):
                                    pe.wait_ge(s_fro, v * T + h * H + j + 1)
                                    for c in range(0, N, BANK):
                                        last = add(acc[0:WN, c:min(c + BANK, N)], into16[:, h, j, :], fro[:, j, c:min(c + BANK, N)])
                                    last.then_inc(s_tile, 1)
                                pe.wait_ge(s_ea[h], 16 * (v + 1))
                                pe.wait_ge(s_m, 2 + k)
                                for j in range(H):
                                    add(acc[0:WN, TAIL:TAIL + F], into[:, h, j, :], ea[:, h, j, :])
                                    add(acc[0:WN, TAIL + F:TAIL + RAW - EA], into[:, h, j, :], prob[:, h, j, :])
                                    last = add(acc[0:WN, NUM_PS:NUM_PS + EA], into[:, h, j, :],
                                               weighted[:, h, j].rearrange("p h f -> p (h f)"))
                                last.then_inc(s_half, 1)

                        def after(w, end):
                            pe.wait_ge(s_counts, w + 1)
                            for c in range(NW):
                                last = nc.tensor.transpose(turned_ps[0:WN, c, 0:WN], counts[:, c * WN:(c + 1) * WN],
                                                           ident16[0:WN, 0:WN])
                                if c % 8 == 7 or c == NW - 1:
                                    last.then_inc(s_trps, 1)

                        loop_windows(pe, body, before, after)

            with Phase(nc, "nodes0") as ph:
                rden = ph.sb("rden", [WN, NW, A0])
                twice = ph.sb("twice", [WN, NW, F])
                w_heads = ph.sb("w_heads", [P, 2, F])
                w_out = ph.sb("w_out", [F, F])
                mean = ph.sb("mean", [WN, NW, F])
                y = ph.sb("y", [WN, NW, F])
                s_ld, s_ch, s_ch2, s_ch3 = ph.sem("s_ld"), ph.sem("s_ch"), ph.sem("s_ch2"), ph.sem("s_ch3")
                msg = raw[:, :, 0:HEADS0 * F]
                with nc.Block() as block:

                    @block.sync
                    def _(sp):
                        wh = a["L0_gnn_w_proj"].rearrange("h f g -> (h f) g").rearrange("(k p) g -> p k g", p=P)
                        sp.dma_start(w_heads[:, :, :], wh).then_inc(s_ld, 16)
                        sp.dma_start(w_out[:, :], a["L0_gnn_w_out"]).then_inc(s_ld, 16)
                        with nc.allow_non_contiguous_dma("rows"):
                            sp.dma_start(edge_sum, raw[:, :, EA:DEN]).then_inc(s_ld, 16)
                        sp.wait_ge(s_ld, 48)

                    @block.vector
                    def _(dve):
                        step = Chain(dve, s_ch)
                        step(dve.tensor_copy(deg[:, :], raw[:, :, DEG:RAW].squeeze(2)))
                        step(dve.tensor_scalar(rden[:, :, :], raw[:, :, DEN:DEG], TINY, None, ALU.max))
                        step(dve.reciprocal(rden[:, :, :], rden[:, :, :]))
                        for k in range(A0):
                            part = raw[:, :, k * F:(k + 1) * F]
                            step(dve.tensor_tensor(part, part, over(rden[:, :, k], F), ALU.mult))
                        step(dve.tensor_tensor(msg, msg, raw[:, :, HEADS0 * F:A0 * F], ALU.add))
                        step(dve.tensor_scalar(stat[:, 0, :], deg[:, :], 1.0, 2.0, ALU.min, ALU.mult))
                        step(dve.tensor_tensor(twice[:, :, :], x[:, :, :], over(stat[:, 0, :], F), ALU.mult))
                        for k in range(HEADS0):
                            part = raw[:, :, k * F:(k + 1) * F]
                            step(dve.tensor_tensor(part, part, twice[:, :, :], ALU.subtract))

                node_linear(nc, "heads", raw, [(0, P), (P, P)], lambda k: w_heads[:, k, :], F, None, mean, 1.0 / HEADS0)
                with nc.Block() as block:

                    @block.vector
                    def _(dve):
                        step = Chain(dve, s_ch2)
                        step(dve.tensor_tensor(twice[:, :, :], mean[:, :, :], mean[:, :, :], ALU.is_equal))
                        step(dve.memset(y[:, :, :], 0.0))
                        step(dve.copy_predicated(y[:, :, :], twice[:, :, :].bitcast(I32), mean[:, :, :]))
                        step(dve.tensor_scalar(mean[:, :, :], y[:, :, :], 3.4028234e38, -3.4028234e38, ALU.min, ALU.max))

                node_linear(nc, "out0", mean, [(0, F)], lambda k: w_out[:, :], F, None, y)
                norm = Norm(ph, "norm", stat, minus_half)
                with nc.Block() as block:

                    @block.gpsimd
                    def _(pool):
                        norm.on_gpsimd(pool)

                    @block.vector
                    def _(dve):
                        step = Chain(dve, s_ch3)
                        step(dve.tensor_tensor(y[:, :, :], y[:, :, :], x[:, :, :], ALU.add))
                        step(dve.tensor_tensor(y[:, :, :], y[:, :, :], x[:, :, :], ALU.add))
                        norm.on_vector(step, dve, y[:, :, :], x[:, :, :], twice[:, :, :])

        def dense_sum(tag, counts_sb, parts, dst):
            with Phase(nc, tag) as ph:
                sum_ps = ph.ps("sum_ps", [WN, U, BANK])
                s_sum, s_out = ph.sem("s_sum"), ph.sem("s_out")
                with nc.Block() as block:

                    @block.tensor
                    def _(pe):
                        with pe.Fori(0, NW // U) as i:
                            for u in range(U):
                                w = i * U + u
                                pe.wait_ge(s_out, w + 1)
                                for c in range(NW):
                                    last = nc.tensor.matmul(sum_ps[:, u, 0:3 * F],
                                                            counts_sb[:, bass.ds(w, 1), c * WN:(c + 1) * WN].squeeze(1),
                                                            parts[:, c, :, :].rearrange("p k f -> p (k f)"),
                                                            start=(c == 0), stop=(c == NW - 1))
                                last.then_inc(s_sum, 1)

                    @block.vector
                    def _(dve):
                        dve.sem_inc(s_out, U)
                        with dve.Fori(0, NW // U) as i:
                            for u in range(U):
                                w = i * U + u
                                dve.wait_ge(s_sum, w + 1)
                                dve.tensor_reduce(dst[:, bass.ds(w, 1), 0:F].squeeze(1),
                                                  sum_ps[:, u, 0:3 * F].rearrange("p (k f) -> p f k", k=3),
                                                  AX, ALU.add).then_inc(s_out, 1)

        def split3(step, dve, parts, rest, src):
            step(dve.tensor_copy(parts[:, :, 0, :], src))
            step(dve.tensor_tensor(rest, src, parts[:, :, 0, :], ALU.subtract))
            step(dve.tensor_copy(parts[:, :, 1, :], rest))
            step(dve.tensor_tensor(rest, rest, parts[:, :, 1, :], ALU.subtract))
            step(dve.tensor_copy(parts[:, :, 2, :], rest))

        with Phase(nc, "rounds") as ph:
            counts_sb = ph.sb("counts_sb", [WN, NW, N], BF16)
            parts = ph.sb("parts", [WN, NW, 3, F], BF16)
            cat = ph.sb("cat", [WN, NW, 2 * F])
            w_lr = ph.sb("w_lr", [P, 3, F])
            w_one = ph.sb("w_one", [F, 2, F])
            vecs = ph.sb("vecs", [WN, 11, F])
            inv_deg = ph.sb("inv_deg", [WN, NW])
            y = ph.sb("y", [WN, NW, F])
            h_in = cat[:, :, F:2 * F]
            s_ld, s_ct = ph.sem("s_ld"), ph.sem("s_ct")
            with nc.Block() as block:

                @block.sync
                def _(sp):
                    for w in range(NW):
                        sp.dma_start(counts_sb[:, w, :], counts_t[w]).then_inc(s_ct, 16)
                    sp.wait_ge(s_ct, 16 * NW)

                @block.scalar
                def _(act):
                    with nc.allow_non_contiguous_dma("weights"):
                        act.dma_start(w_lr[0:F, :, :], a["L1_gnn_w_l"].rearrange("l f g -> f l g")).then_inc(s_ld, 16)
                        act.dma_start(w_lr[F:P, :, :], a["L1_gnn_w_r"].rearrange("l f g -> f l g")).then_inc(s_ld, 16)
                    act.dma_start(w_one[:, 0, :], a["L1_gnn_w_res"]).then_inc(s_ld, 16)
                    act.dma_start(w_one[:, 1, :], a["L1_gnn_w_fc"]).then_inc(s_ld, 16)
                    for n, name in enumerate(("L1_gnn_b_l", "L1_gnn_gamma", "L1_gnn_beta")):
                        act.dma_start(vecs[:, 3 * n:3 * n + 3, :], a[name].partition_broadcast(WN)).then_inc(s_ld, 16)
                    act.dma_start(vecs[:, 9, :], a["L1_gnn_b_res"].partition_broadcast(WN)).then_inc(s_ld, 16)
                    act.dma_start(vecs[:, 10, :], a["L1_gnn_b_fc"].partition_broadcast(WN)).then_inc(s_ld, 16)
                    act.wait_ge(s_ld, 16 * 9)

                s_ch = ph.sem("s_prep")

                @block.vector
                def _(dve):
                    step = Chain(dve, s_ch)
                    step(dve.tensor_scalar(inv_deg[:, :], deg[:, :], 1.0, None, ALU.max))
                    step(dve.reciprocal(inv_deg[:, :], inv_deg[:, :]))
                    step(dve.tensor_scalar(stat[:, 0, :], deg[:, :], 1.0, None, ALU.min))
                    step(dve.tensor_tensor(inv_deg[:, :], inv_deg[:, :], stat[:, 0, :], ALU.mult))
                    step(dve.tensor_copy(h_in, x[:, :, :]))
                    split3(step, dve, parts, y[:, :, :], x[:, :, :])

            for r in range(3):
                dense_sum(f"r{r}", counts_sb, parts, cat)
                s_ch = ph.sem(f"s_mean{r}")
                with nc.Block() as block:

                    @block.vector
                    def _(dve):
                        step = Chain(dve, s_ch)
                        step(dve.tensor_tensor(cat[:, :, 0:F], cat[:, :, 0:F], over(inv_deg[:, :], F), ALU.mult))

                node_linear(nc, f"lr{r}", cat, [(0, P)], lambda k: w_lr[:, r, :], F, vecs[:, r, :], y)
                s_ch = ph.sem(f"s_round{r}")
                norm = Norm(ph, f"norm{r}", stat, minus_half)
                with nc.Block() as block:

                    @block.gpsimd
                    def _(pool):
                        norm.on_gpsimd(pool)

                    @block.vector
                    def _(dve):
                        def each(n):
                            return vecs[:, n, :].unsqueeze(1).broadcast_to([WN, NW, F])
                        step = Chain(dve, s_ch)
                        norm.on_vector(step, dve, y[:, :, :], y[:, :, :], cat[:, :, 0:F])
                        step(dve.tensor_tensor(y[:, :, :], y[:, :, :], each(3 + r), ALU.mult))
                        step(dve.tensor_tensor(y[:, :, :], y[:, :, :], each(6 + r), ALU.add))
                        step(dve.tensor_scalar(y[:, :, :], y[:, :, :], 0.0, None, ALU.max))

                residual = h_in
                if r == 0:
                    residual = cat[:, :, 0:F]
                    node_linear(nc, "res", x, [(0, F)], lambda k: w_one[:, 0, :], F, vecs[:, 9, :], cat)
                s_ch = ph.sem(f"s_sum{r}")
                with nc.Block() as block:

                    @block.vector
                    def _(dve):
                        step = Chain(dve, s_ch)
                        step(dve.tensor_tensor(h_in, y[:, :, :], residual, ALU.add))
                        if r < 2:
                            split3(step, dve, parts, y[:, :, :], h_in)

            node_linear(nc, "fc", h_in, [(0, F)], lambda k: w_one[:, 1, :], F, vecs[:, 10, :], y)
            s_ch = ph.sem("s_norm1")
            norm = Norm(ph, "norm", stat, minus_half)
            with nc.Block() as block:

                @block.gpsimd
                def _(pool):
                    norm.on_gpsimd(pool)

                @block.vector
                def _(dve):
                    step = Chain(dve, s_ch)
                    step(dve.tensor_tensor(y[:, :, :], y[:, :, :], x[:, :, :], ALU.add))
                    norm.on_vector(step, dve, y[:, :, :], x[:, :, :], cat[:, :, 0:F])

        with Phase(nc, "attention") as layer:
            bias = layer.sb("bias", [P, NG, T * HEADS2])
            q = layer.sb("q", [WN, NW, F])
            attn = layer.sb("attn", [WN, NW, F + HEADS2])
            w_sq = layer.sb("w_sq", [F, 4, F])
            b_sq = layer.sb("b_sq", [WN, 4, F])
            QUADS = 2
            with Phase(nc, "bias") as ph:
                attr = ph.sb("attr", [P, 4, T, ED])
                attr_t = ph.sb("attr_t", [P, 4, P])
                hidden = ph.sb("hidden", [P, 4, P])
                w1 = ph.sb("w1", [P, P])
                w2 = ph.sb("w2", [P, H * HEADS2])
                b1 = ph.sb("b1", [P, 1])
                b2 = ph.sb("b2", [P, T, HEADS2])
                t_ps = ph.ps("t_ps", [P, 4, BANK])
                h_ps = ph.ps("h_ps", [P, 2, BANK])
                b_ps = ph.ps("b_ps", [P, 2, BANK])
                s_ld, s_zero, s_w = ph.sem("s_ld"), ph.sem("s_zero"), ph.sem("s_w")
                with nc.Block() as block:

                    @block.gpsimd
                    def _(pool):
                        pool.memset(w1[:, :], 0.0).then_inc(s_zero, 1)
                        pool.memset(w2[:, :], 0.0).then_inc(s_zero, 1)

                    @block.sync
                    def _(sp):
                        sp.wait_ge(s_zero, 2)
                        n = 0
                        with nc.allow_non_contiguous_dma("weights"):
                            for k in range(H):
                                r = slice(k * ED, (k + 1) * ED)
                                sp.dma_start(w1[r, r], a["L2_gnn_We1"]).then_inc(s_w, 16)
                                sp.dma_start(w2[r, k * HEADS2:(k + 1) * HEADS2], a["L2_gnn_We2"]).then_inc(s_w, 16)
                                sp.dma_start(b1[r, :], a["L2_gnn_be1"].rearrange("(f a) -> f a", a=1)).then_inc(s_w, 16)
                            for j in range(T):
                                sp.dma_start(b2[:, j, :], a["L2_gnn_be2"].partition_broadcast(P)).then_inc(s_w, 16)
                            for n, name in enumerate("QKVO"):
                                sp.dma_start(w_sq[:, n, :], a["L2_gnn_W" + name]).then_inc(s_w, 16)
                                sp.dma_start(b_sq[:, n, :], a["L2_gnn_b" + name].partition_broadcast(WN)).then_inc(s_w, 16)
                        sp.wait_ge(s_w, 16 * (3 * H + T + 8))

                s_attr = [ph.sem(f"s_attr{n}") for n in range(4)]
                s_t, s_tc, s_h, s_hc, s_b, s_bc = (ph.sem(n) for n in ("s_t", "s_tc", "s_h", "s_hc", "s_b", "s_bc"))
                GROUPS = 101

                def bias_stage(groups, g_of, ring):
                    pass

                s_sig, s_lin = ph.sem("s_sig"), ph.sem("s_lin")
                with nc.Block() as block:

                    @block.sync
                    def _(sp):
                        with sp.Fori(0, NG) as g:
                            e0 = sp.value_load(starts[0:1, bass.ds(g, 1)], min_val=0, max_val=LAST)
                            sp.wait_ge(s_t, 2 * g + 2)
                            sp.dma_start(attr[:, 0], a["edge_attr_32"][bass.ds(e0, GE), :].rearrange("(p j) f -> p j f", j=T)).then_inc(s_attr[0], 16)

                    @block.tensor
                    def _(pe):
                        pe.sem_inc(s_t, 2)
                        pe.sem_inc(s_h, 2)
                        pe.sem_inc(s_b, 2)
                        with pe.Fori(0, NG) as g:
                            pe.wait_ge(s_attr[0], 16 * (g + 1))
                            for h in range(2):
                                pe.wait_ge(s_tc, 2 * g + h + 1)
                                nc.tensor.transpose(t_ps[:, h, 0:P], attr[:, 0, h * H:(h + 1) * H, :].rearrange("p j f -> p (j f)"),
                                                    ident[:, :]).then_inc(s_t, 1)
                            for h in range(2):
                                pe.wait_ge(s_tc, 2 + 2 * g + h + 1)
                                pe.wait_ge(s_hc, 2 * g + h + 1)
                                nc.tensor.matmul(h_ps[:, h, 0:P], w1[:, :], attr_t[:, h, :], start=True, stop=True).then_inc(s_h, 1)
                            for h in range(2):
                                pe.wait_ge(s_hc, 2 + 2 * g + h + 1)
                                pe.wait_ge(s_bc, 2 * g + h + 1)
                                nc.tensor.matmul(b_ps[:, h, 0:H * HEADS2], hidden[:, h, :], w2[:, :], start=True, stop=True).then_inc(s_b, 1)

                    @block.scalar
                    def _(act):
                        act.sem_inc(s_hc, 2)
                        with act.Fori(0, NG) as g:
                            for h in range(2):
                                act.wait_ge(s_h, 2 + 2 * g + h + 1)
                                act.wait_ge(s_b, 2 * g + h + 1)
                                act.activation(hidden[:, h, :], h_ps[:, h, 0:P], ACT.Silu, bias=b1[:, 0:1]).then_inc(s_hc, 1)

                    @block.vector
                    def _(dve):
                        dve.sem_inc(s_tc, 2)
                        dve.sem_inc(s_bc, 2)
                        with dve.Fori(0, NG) as g:
                            for h in range(2):
                                dve.wait_ge(s_t, 2 + 2 * g + h + 1)
                                dve.wait_ge(s_h, 2 * g + h + 1)
                                dve.tensor_copy(attr_t[:, h, :], t_ps[:, h, 0:P]).then_inc(s_tc, 1)
                            for h in range(2):
                                dve.wait_ge(s_b, 2 + 2 * g + h + 1)
                                dve.tensor_tensor(bias[:, bass.ds(g, 1), h * H * HEADS2:(h + 1) * H * HEADS2].squeeze(1),
                                                  b_ps[:, h, 0:H * HEADS2],
                                                  b2[:, 0:H, :].rearrange("p j h -> p (j h)"), ALU.add).then_inc(s_bc, 1)

            with Phase(nc, "kvq") as ph:
                kv = ph.sb("kv", [WN, NW, 2 * F])
                sq = ph.sb("sq", [WN, NW, F])
                norms = ph.sb("norms", [WN, NW, HEADS2])
                top = ph.sb("top", [P, 3 * HEADS2])
                top_all = ph.sb("top_all", [P, 3 * HEADS2])
                bound = ph.sb("bound", [P, HEADS2])
                node_linear(nc, "q", x, [(0, F)], lambda k: w_sq[:, 0, :], F, b_sq[:, 0, :], q)
                node_linear(nc, "kv", x, [(0, F)], lambda k: w_sq[:, 1:3, :].rearrange("p a f -> p (a f)"), 2 * F,
                            b_sq[:, 1:3, :].rearrange("p a f -> p (a f)"), kv)
                s_st, s_ch, s_top, s_all = ph.sem("s_st"), ph.sem("s_ch"), ph.sem("s_top"), ph.sem("s_all")
                s_bound, s_root = ph.sem("s_bound"), ph.sem("s_root")
                with nc.Block() as block:

                    @block.sync
                    def _(sp):
                        with nc.allow_non_contiguous_dma("table rows"):
                            sp.dma_start(table_kv.rearrange("(w p) c -> p w c", p=WN), kv[:, :, :]).then_inc(s_st, 16)
                        sp.wait_ge(s_st, 16)

                    @block.gpsimd
                    def _(pool):
                        pool.wait_ge(s_top, 1)
                        pool.partition_all_reduce(top_all[:, :], top[:, :], P, RMAX).then_inc(s_all, 1)
                        pool.wait_ge(s_bound, 1)
                        pool.tensor_tensor(bound[:, :], bound[:, :], half[:, :], ALU.pow).then_inc(s_root, 1)

                    @block.vector
                    def _(dve):
                        step = Chain(dve, s_ch)
                        step(dve.tensor_scalar(q[:, :, :], q[:, :, :], float(DK) ** -0.5, None, ALU.mult))
                        step(dve.memset(top[:, :], -3e38))
                        for n, of in enumerate((q[:, :, :], kv[:, :, 0:F])):
                            step(dve.tensor_tensor(sq[:, :, :], of, of, ALU.mult))
                            step(dve.tensor_reduce(norms[:, :, :], sq[:, :, :].rearrange("p w (h d) -> p w h d", d=DK), AX, ALU.add))
                            step(dve.tensor_reduce(top[0:WN, n * HEADS2:(n + 1) * HEADS2],
                                                   norms[:, :, :].rearrange("p w h -> p h w"), AX, ALU.max))
                        by_head = bias[:, :, :].rearrange("p g (j h) -> p (g j) h", h=HEADS2)
                        dve.tensor_reduce(top[:, 2 * HEADS2:3 * HEADS2], by_head.rearrange("p e h -> p h e"), AX,
                                          ALU.max).then_inc(s_top, 1)
                        dve.wait_ge(s_all, 1)
                        dve.tensor_tensor(bound[:, :], top_all[:, 0:HEADS2], top_all[:, HEADS2:2 * HEADS2],
                                          ALU.mult).then_inc(s_bound, 1)
                        dve.wait_ge(s_root, 1)
                        step(dve.tensor_tensor(bound[:, :], bound[:, :], top_all[:, 2 * HEADS2:3 * HEADS2], ALU.add))
                        step(dve.tensor_tensor(by_head, by_head, bound[:, :].unsqueeze(1).broadcast_to([P, NG * T, HEADS2]),
                                               ALU.subtract))

            with Phase(nc, "edges2") as ph:
                zeros = ph.sb("zeros", [P, P])
                idx = ph.sb("idx", [P, 2, H], I32)
                rows = ph.sb("rows", [P, 2, H, 2 * F])
                dst_rel = ph.sb("dst_rel", [P, 2, H])
                into = ph.sb("into", [P, 2, H, WN])
                into_t = ph.sb("into_t", [WN, 2, H, P])
                q_w = ph.sb("q_w", [WN, F])
                prod = ph.sb("prod", [P, 2, H, F])
                score = ph.sb("score", [P, 2, H, HEADS2])
                weighted = ph.sb("weighted", [P, 2, H, F + HEADS2])
                t_ps = ph.ps("t_ps", [P, 2, H, P])
                q_ps = ph.ps("q_ps", [P, 2, H, P])
                acc = ph.ps("acc", [P, BANK])
                s_idx, s_rel, s_into, s_t, s_tc, s_q, s_prod, s_score, s_sb, s_exp, s_m, s_half, s_free, s_seen, s_init, s_qw = (
                    ph.sem(n) for n in ("s_idx", "s_rel", "s_into", "s_turned_ps", "s_turned", "s_query", "s_prod",
                                        "s_dot", "s_score", "s_exp", "s_weighted", "s_half_done", "s_acc_free", "s_seen", "s_init", "s_qw"))
                s_rows = [ph.sem(f"s_rows{h}") for h in range(2)]
                with nc.Block() as block:

                    @block.gpsimd
                    def _(pool):
                        def body(w, g, v):
                            for h in range(2):
                                pool.wait_ge(s_m, 2 * v + h + 1)
                                pool.tensor_copy(idx[:, h, :], src_i[:, bass.ds(g, 1), h * H:(h + 1) * H].squeeze(1)).then_inc(s_idx, 1)
                                pool.wait_ge(s_idx, 2 * v + h + 1)
                                pool.sem_inc(s_seen, 1)
                                for j in range(H):
                                    pool.indirect_dma_start(rows[:, h, j, :], None, table_kv,
                                                            bass.IndirectOffsetOnAxis(ap=idx[:, h, j:j + 1], axis=0)).then_inc(s_rows[h], 16)

                        loop_windows(pool, body)

                    @block.vector
                    def _(dve):
                        dve.memset(zeros[:, :], 0.0).then_inc(s_init, 1)
                        dve.sem_inc(s_m, 2)

                        def body(w, g, v):
                            for h in range(2):
                                k = 2 * v + h + 1
                                dve.wait_ge(s_half, k)
                                dve.tensor_scalar(dst_rel[:, h], dst_f[:, bass.ds(g, 1), h * H:(h + 1) * H].squeeze(1),
                                                  window_start[:, bass.ds(w, 1)], None, ALU.subtract).then_inc(s_rel, 1)
                                dve.wait_ge(s_rel, k)
                                dve.tensor_tensor(into[:, h], iota_n[:, :].unsqueeze(1).broadcast_to([P, H, WN]),
                                                  over(dst_rel[:, h], WN), ALU.is_equal).then_inc(s_into, 1)
                                dve.wait_ge(s_rows[h], 16 * H * (v + 1))
                                dve.wait_ge(s_q, k)
                                dve.tensor_tensor(prod[:, h], rows[:, h, :, 0:F], q_ps[:, h, :, 0:F], ALU.mult).then_inc(s_prod, 1)
                                dve.wait_ge(s_prod, k)
                                dve.tensor_reduce(score[:, h], prod[:, h].rearrange("p j (h d) -> p j h d", d=DK), AX,
                                                  ALU.add).then_inc(s_score, 1)
                                dve.wait_ge(s_score, k)
                                dve.tensor_tensor(score[:, h], score[:, h],
                                                  bias[:, bass.ds(g, 1), h * H * HEADS2:(h + 1) * H * HEADS2].squeeze(1)
                                                  .rearrange("p (j h) -> p j h", h=HEADS2), ALU.add).then_inc(s_sb, 1)
                                dve.wait_ge(s_exp, k)
                                dve.tensor_tensor(weighted[:, h, :, 0:F].rearrange("p j (h d) -> p j h d", d=DK),
                                                  rows[:, h, :, F:2 * F].rearrange("p j (h d) -> p j h d", d=DK),
                                                  weighted[:, h, :, F:F + HEADS2].unsqueeze(3).broadcast_to([P, H, HEADS2, DK]),
                                                  ALU.mult).then_inc(s_m, 1)

                        loop_windows(dve, body)

                    @block.scalar
                    def _(act):
                        act.sem_inc(s_free, 1)

                        def before(w):
                            act.wait_ge(s_free, w + 1)
                            act.copy(q_w[:, :], q[:, bass.ds(w, 1), :].squeeze(1)).then_inc(s_qw, 1)

                        def body(w, g, v):
                            for h in range(2):
                                k = 2 * v + h + 1
                                act.wait_ge(s_t, k)
                                act.copy(into_t[:, h], t_ps[0:WN, h]).then_inc(s_tc, 1)
                                act.wait_ge(s_sb, k)
                                act.activation(weighted[:, h, :, F:F + HEADS2], score[:, h], ACT.Exp).then_inc(s_exp, 1)

                        def after(w, end):
                            act.wait_ge(s_half, 2 * end + 2)
                            act.copy(attn[:, bass.ds(w, 1), :].squeeze(1), acc[0:WN, 0:F + HEADS2]).then_inc(s_free, 1)

                        loop_windows(act, body, before, after)

                    @block.tensor
                    def _(pe):
                        pe.sem_inc(s_half, 2)
                        pe.wait_ge(s_init, 1)

                        def before(w):
                            pe.wait_ge(s_free, w + 1)
                            pe.wait_ge(s_qw, w + 1)
                            nc.tensor.matmul(acc[0:WN, 0:P], zeros[:, 0:WN], zeros[:, :], start=True, stop=True)

                        def body(w, g, v):
                            for h in range(2):
                                k = 2 * v + h + 1
                                pe.wait_ge(s_into, k)
                                for j in range(H):
                                    last = nc.tensor.transpose(t_ps[0:WN, h, j, :], into[:, h, j, :], ident[:, :])
                                last.then_inc(s_t, 1)
                                pe.wait_ge(s_tc, k)
                                for j in range(H):
                                    last = nc.tensor.matmul(q_ps[:, h, j, 0:F], into_t[:, h, j, :], q_w[:, :], start=True, stop=True)
                                last.then_inc(s_q, 1)
                                pe.wait_ge(s_m, 2 + k)
                                for j in range(H):
                                    last = nc.tensor.matmul(acc[0:WN, 0:F + HEADS2], into[:, h, j, :], weighted[:, h, j, :],
                                                            start=False, stop=True, skip_group_check=True)
                                last.then_inc(s_half, 1)

                        loop_windows(pe, body, before)

            with Phase(nc, "nodes2") as ph:
                rden = ph.sb("rden", [WN, NW, HEADS2])
                y = ph.sb("y", [WN, NW, F])
                tmp = ph.sb("tmp", [WN, NW, F])
                s_ch, s_ch2 = ph.sem("s_ch"), ph.sem("s_ch2")
                with nc.Block() as block:

                    @block.vector
                    def _(dve):
                        step = Chain(dve, s_ch)
                        step(dve.tensor_scalar(rden[:, :, :], attn[:, :, F:F + HEADS2], TINY, None, ALU.max))
                        step(dve.reciprocal(rden[:, :, :], rden[:, :, :]))
                        for h in range(HEADS2):
                            part = attn[:, :, h * DK:(h + 1) * DK]
                            step(dve.tensor_tensor(part, part, over(rden[:, :, h], DK), ALU.mult))

                node_linear(nc, "wo", attn, [(0, F)], lambda k: w_sq[:, 3, :], F, b_sq[:, 3, :], y)
                norm = Norm(ph, "norm", stat, minus_half)
                with nc.Block() as block:

                    @block.gpsimd
                    def _(pool):
                        norm.on_gpsimd(pool)

                    @block.vector
                    def _(dve):
                        step = Chain(dve, s_ch2)
                        step(dve.tensor_tensor(y[:, :, :], y[:, :, :], x[:, :, :], ALU.add))
                        norm.on_vector(step, dve, y[:, :, :], x[:, :, :], tmp[:, :, :])

        with Phase(nc, "last") as ph:
            counts_sb = ph.sb("counts_sb", [WN, NW, N], BF16)
            parts = ph.sb("parts", [WN, NW, 3, F], BF16)
            y = ph.sb("y", [WN, NW, F])
            tmp = ph.sb("tmp", [WN, NW, F])
            sums = ph.sb("sums", [WN, NW, F])
            s_ct, s_ch, s_ch2, s_out = ph.sem("s_ct"), ph.sem("s_ch"), ph.sem("s_ch2"), ph.sem("s_out")
            with nc.Block() as block:

                @block.sync
                def _(sp):
                    for w in range(NW):
                        sp.dma_start(counts_sb[:, w, :], counts_t[w]).then_inc(s_ct, 16)
                    sp.dma_start(sums[:, :, :], edge_sum).then_inc(s_ct, 16)
                    sp.wait_ge(s_ct, 16 * NW + 16)

                @block.vector
                def _(dve):
                    step = Chain(dve, s_ch)
                    split3(step, dve, parts, y[:, :, :], x[:, :, :])

            dense_sum("neighbours", counts_sb, parts, y)
            s_res = ph.sem("s_res")
            norm = Norm(ph, "norm", stat, minus_half)
            with nc.Block() as block:

                @block.gpsimd
                def _(pool):
                    norm.on_gpsimd(pool)

                @block.vector
                def _(dve):
                    step = Chain(dve, s_ch2)
                    step(dve.tensor_tensor(y[:, :, :], y[:, :, :], sums[:, :, :], ALU.add))
                    step(dve.tensor_tensor(tmp[:, :, :], x[:, :, :], over(deg[:, :], F), ALU.mult))
                    step(dve.tensor_tensor(y[:, :, :], y[:, :, :], tmp[:, :, :], ALU.add))
                    step(dve.tensor_tensor(y[:, :, :], y[:, :, :], x[:, :, :], ALU.add))
                    norm.on_vector(step, dve, y[:, :, :], x[:, :, :], tmp[:, :, :])
                    dve.sem_inc(s_res, 1)

                @block.sync
                def _(sp):
                    sp.wait_ge(s_res, 1)
                    with nc.allow_non_contiguous_dma("rows"):
                        sp.dma_start(out.rearrange("(w p) f -> p w f", p=WN), x[:, :, :]).then_inc(s_out, 16)
                    sp.wait_ge(s_out, 16)


def kernel(**inputs):
    import numpy as np
    import concourse.bacc as bacc
    from concourse.bass_utils import run_bass_kernel_spmd

    nc = bacc.Bacc("TRN2", target_bir_lowering=False, num_devices=1)
    arrays, args = {}, {}
    for name in inputs:
        if name == "edge_attr_3":
            continue
        arr = np.ascontiguousarray(inputs[name])
        if arr.ndim == 0:
            arr = arr.reshape(1)
        arrays["in_" + name] = arr
        args[name] = nc.dram_tensor("in_" + name, arr.shape, mybir.dt.from_np(arr.dtype), kind="ExternalInput").ap()
    out = nc.dram_tensor("out", (N, F), F32, kind="ExternalOutput").ap()
    build(nc, args, out)
    got = run_bass_kernel_spmd(nc, [arrays], core_ids=[0])
    return got.results[0]["out"]
```

```python
import concourse.bass as bass
from concourse import mybir
from contextlib import ExitStack, contextmanager

F32 = mybir.dt.float32
BF16 = mybir.dt.bfloat16
F16 = mybir.dt.float16
I32 = mybir.dt.int32
ALU = mybir.AluOpType
ACT = mybir.ActivationFunctionType
AX = mybir.AxisListType.X
RMAX = bass.bass_isa.ReduceOp.max

P = 128
N, E, F = 3125, 103125, 64
WN = 125
NW = N // WN
T = 8
H = 4
GE = P * T
NG = -(-E // GE)
LAST = E - GE
DUP = NG * GE - E
HEADS0, HEADS2, DK = 4, 8, 8
A0 = 2 * HEADS0
ROW0 = F + A0
ED = 32
U = 5
Q, QN = 4, 32
TILES = -(-E // P)
TAIL0 = TILES * P - E
CH = -(-TILES // P)
STEP = 2
TURN_BIT, TILE_BIT = 14, 10
assert TILES % STEP == 0 and NW * TILES // STEP < 1 << TURN_BIT and TILES < 1 << TILE_BIT
CUM_BIT, END_BIT = 7, 19
assert NG < 1 << CUM_BIT and NW * NG < 1 << (END_BIT - CUM_BIT)
TINY = 1e-30
EPS = 1e-5
BANK = 512


class Phase:

    def __init__(self, nc, name):
        self.nc, self.name, self.ctx, self.sems = nc, name, ExitStack(), []

    def __enter__(self):
        self.ctx.__enter__()
        return self

    def __exit__(self, *a):
        done = self.ctx.__exit__(*a)
        if self.sems and a[0] is None:
            self.nc.clear_and_free_semaphores(self.sems)
            self.nc.all_engine_barrier()
        return done

    def sb(self, name, shape, dt=F32):
        return self.ctx.enter_context(self.nc.sbuf_tensor(f"{self.name}_{name}", shape, dt))

    def ps(self, name, shape, dt=F32):
        return self.ctx.enter_context(self.nc.psum_tensor(f"{self.name}_{name}", shape, dt))

    def sem(self, name):
        self.sems.append(self.nc.alloc_semaphore(f"{self.name}_{name}"))
        return self.sems[-1]



class Chain:

    def __init__(self, eng, sem, base=0):
        self.eng, self.sem, self.n, self.base = eng, sem, 0, base

    def __call__(self, ins):
        ins.then_inc(self.sem, 1)
        self.n += 1
        self.eng.wait_ge(self.sem, self.base + self.n)
        return ins


def grouped(a):
    return a[0:(NG - 1) * GE].rearrange("(g p j) -> p g j", p=P, j=T)


def node_linear(nc, tag, src, chunks, weights, fout, bias, dst, scale=None):
    with Phase(nc, tag) as ph:
        nk = len(chunks)
        width = max(c for _, c in chunks)
        fin = sum(c for _, c in chunks)
        turns = NW // U
        staged = ph.sb("staged", [WN, U, fin])
        turned = ph.sb("turned", [P, U, nk, P])
        turned_ps = ph.ps("turned_ps", [P, 8, nk, P])
        out_ps = ph.ps("out_ps", [WN, 6, 256])
        s_go = ph.sem("s_go")
        s_staged, s_turned_ps, s_turned, s_out_ps, s_out = (
            ph.sem(n) for n in ("s_staged", "s_turned_ps", "s_turned", "s_out_ps", "s_out"))
        block = ph.ctx.enter_context(nc.Block())

        @block.gpsimd
        def _(pool):
            with pool.Fori(0, turns) as i:
                pool.wait_ge(s_turned_ps, i + 1)
                pool.tensor_copy(staged[:, :, :], src[:, bass.ds(i * U, U), 0:fin]).then_inc(s_staged, 1)

        @block.tensor
        def _(pe):
            pe.sem_inc(s_turned_ps, 1)
            with pe.Fori(0, turns) as i:
                pe.wait_ge(s_staged, i + 1)
                pe.wait_ge(s_turned, i + 1)
                pe.sem_inc(s_go, 1)
                for u in range(U):
                    for k, (c0, cw) in enumerate(chunks):
                        last = nc.tensor.transpose(turned_ps[0:cw, u, k, 0:WN], staged[:, u, c0:c0 + cw],
                                                   nc_ident(nc)[0:WN, 0:WN])
                last.then_inc(s_turned_ps, 1)
                pe.wait_ge(s_turned, i + 2)
                pe.wait_ge(s_out, i + 1)
                for u in range(U):
                    for k, (c0, cw) in enumerate(chunks):
                        last = nc.tensor.matmul(out_ps[:, u, 0:fout], turned[0:cw, u, k, 0:WN], weights(k),
                                                start=(k == 0), stop=(k == nk - 1))
                last.then_inc(s_out_ps, 1)

        @block.scalar
        def _(act):
            act.sem_inc(s_turned, 1)
            act.sem_inc(s_out_ps, 1)
            with act.Fori(0, turns) as i:
                act.wait_ge(s_turned_ps, i + 2)
                act.wait_ge(s_out_ps, i + 1)
                act.copy(turned[0:width, :, :, 0:WN], turned_ps[0:width, 0:U, :, 0:WN]).then_inc(s_turned, 1)

        @block.vector
        def _(dve):
            dve.sem_inc(s_out, 1)
            with dve.Fori(0, turns) as i:
                dve.wait_ge(s_out_ps, i + 2)
                to, by = dst[:, bass.ds(i * U, U), 0:fout], 1.0 if scale is None else scale
                if bias is None:
                    dve.tensor_scalar(to, out_ps[:, 0:U, 0:fout], by, None, ALU.mult).then_inc(s_out, 1)
                else:
                    dve.scalar_tensor_tensor(to, out_ps[:, 0:U, 0:fout], by,
                                             bias.unsqueeze(1).broadcast_to([WN, U, fout]),
                                             ALU.mult, ALU.add).then_inc(s_out, 1)


_IDENT = {}


def nc_ident(nc):
    return _IDENT["ident"]


def over(ap, n):
    return ap.unsqueeze(2).broadcast_to([ap.shape[0], ap.shape[1], n])


class Norm:

    def __init__(self, ph, name, stat, minus_half):
        self.stat, self.minus_half = stat, minus_half
        self.s_var, self.s_rstd = ph.sem(f"{name}_s_var"), ph.sem(f"{name}_s_rstd")

    def on_gpsimd(self, pool):
        pool.wait_ge(self.s_var, 1)
        pool.tensor_tensor(self.stat[:, 0, :], self.stat[:, 1, :], self.minus_half[0:WN, 0:NW], ALU.pow).then_inc(self.s_rstd, 1)

    def on_vector(self, step, dve, y, out, tmp):
        stat = self.stat
        step(dve.tensor_reduce(stat[:, 0, :], y, AX, ALU.add))
        step(dve.tensor_scalar(stat[:, 1, :], stat[:, 0, :], 1.0 / F, None, ALU.mult))
        step(dve.tensor_tensor(y, y, over(stat[:, 1, :], F), ALU.subtract))
        step(dve.tensor_tensor(tmp, y, y, ALU.mult))
        step(dve.tensor_reduce(stat[:, 0, :], tmp, AX, ALU.add))
        dve.tensor_scalar(stat[:, 1, :], stat[:, 0, :], 1.0 / F, EPS, ALU.mult, ALU.add).then_inc(self.s_var, 1)
        dve.wait_ge(self.s_rstd, 1)
        step(dve.tensor_tensor(out, y, over(stat[:, 0, :], F), ALU.mult))


def build(nc, a, out, stop=99):
    with Phase(nc, "all") as whole:
        sb, sem = whole.sb, whole.sem
        table0 = nc.dram_tensor("table0", [N, ROW0], F32).ap()
        table_kv = nc.dram_tensor("table_kv", [N, 2 * F], F32).ap()
        edge_sum = nc.dram_tensor("edge_sum", [WN, NW, F], F32).ap()
        counts_t = nc.dram_tensor("counts_t", [NW, WN, NW * WN], BF16).ap()

        ident = sb("ident", [P, P])
        _IDENT["ident"] = ident
        ident16 = sb("ident16", [P, P], BF16)
        iota_n = sb("iota_n", [P, WN])
        window_start = sb("window_start", [P, NW + 1])
        x = sb("x", [WN, NW, F])
        src_i = sb("src_i", [P, NG, T], I32)
        dst_f = sb("dst_f", [P, NG, T])
        visits = sb("visits", [P, 4, NW + 1], I32)
        turns_of = sb("turns_of", [P, 3, NW], I32)
        starts = sb("starts", [P, NG], I32)
        deg = sb("deg", [WN, NW])
        stat = sb("stat", [WN, 2, NW])
        minus_half = sb("minus_half", [P, NW])
        half = sb("half", [P, HEADS2])

        def in_range(v, lo, hi, why):
            return nc.s_assert_within(v, lo, hi, skip_runtime_bounds_check_because=why)

        def loop_windows(eng, body, before=None, after=None):
            with eng.Fori(0, NW) as w:
                code = eng.value_load(visits[0:1, 0, bass.ds(w, 1)], min_val=0, max_val=(1 << 31) - 1)
                why = "packed so by the first stage"
                lo = in_range(eng.snap(code & ((1 << CUM_BIT) - 1)), 0, NG - 1, why)
                cum = in_range(eng.snap((code >> CUM_BIT) & ((1 << (END_BIT - CUM_BIT)) - 1)), 0, NW * NG, why)
                end = in_range(eng.snap(code >> END_BIT), 1, NW * NG, why)
                if before:
                    before(w)
                with eng.Fori(cum, end) as v:
                    body(w, in_range(eng.snap(v - cum + lo), 0, NG - 1, "visits go to groups that exist"), v, end)
                if after:
                    after(w, end)

        def loop_strips(eng, body, before=None, after=None):
            with eng.Fori(0, NW) as w:
                code = [eng.value_load(turns_of[0:1, n, bass.ds(w, 1)], min_val=0, max_val=(1 << 31) - 1) for n in range(3)]
                why, ones = "packed so by the first stage", (1 << TILE_BIT) - 1
                cum = in_range(eng.snap(code[0] & ((1 << TURN_BIT) - 1)), 0, NW * TILES // STEP, why)
                end = in_range(eng.snap(code[0] >> TURN_BIT), 1, NW * TILES // STEP, why)
                lo = [eng.snap(code[1] & ones), eng.snap((code[1] >> TILE_BIT) & ones),
                      eng.snap(code[1] >> 2 * TILE_BIT), code[2]]
                if before:
                    before(w)
                with eng.Fori(cum, end) as v:
                    done = eng.snap(STEP * (v - cum))

                    def tile(q, h):
                        return in_range(eng.snap(lo[q] + done + h), 0, TILES - 1, "strips stay within the tiles")

                    body(w, tile, v)
                if after:
                    after(w, end)

        with Phase(nc, "plan") as ph:
            dst_i = ph.sb("dst_i", [P, NG, T], I32)
            ramp = ph.sb("ramp", [P, NG * 2], I32)
            ramp_f = ph.sb("ramp_f", [P, NG * 2])
            dup = ph.sb("dup", [P, 3, T])
            ends = ph.sb("ends", [P, 2, NG])
            ends_all = ph.sb("ends_all", [P, 2, NG])
            touch = ph.sb("touch", [P, 3, NW, NG])
            wf = ph.sb("wf", [P, 6, NW])
            ones = ph.sb("ones", [P, NW])
            s_ld, s_pool, s_ch = ph.sem("s_ld"), ph.sem("s_pool"), ph.sem("s_ch")
            s_ends = ph.sem("s_ends")
            s_all = ph.sem("s_all")
            block = ph.ctx.enter_context(nc.Block())

            @block.sync
            def _(sp):
                with nc.allow_non_contiguous_dma("runs of eight edges"):
                    for to, fro in ((src_i, a["src"]), (dst_i, a["dst"])):
                        sp.dma_start(to[:, 0:NG - 1, :], grouped(fro)).then_inc(s_ld, 16)
                        sp.dma_start(to[:, NG - 1, :], fro[LAST:E].rearrange("(p j) -> p j", j=T)).then_inc(s_ld, 16)
                    sp.dma_start(x[:, :, :], a["x"].rearrange("(w p) f -> p w f", p=WN)).then_inc(s_ld, 16)
                sp.wait_ge(s_ld, 80)

            @block.gpsimd
            def _(pool):
                step = Chain(pool, s_pool)
                step(pool.memset(ident[:, :], 0.0))
                step(pool.affine_select(out=ident[:, :], in_=ident[:, :], compare_op=ALU.not_equal, fill=1.0,
                                        base=0, pattern=[[-1, P]], channel_multiplier=1))
                step(pool.tensor_copy(ident16[:, :], ident[:, :]))
                step(pool.iota(ramp[:, :], [[1, 2 * NG]], base=0, channel_multiplier=0))
                step(pool.tensor_copy(ramp_f[:, :], ramp[:, :]))
                step(pool.tensor_copy(iota_n[:, :], ramp_f[:, 0:WN]))
                step(pool.tensor_scalar(window_start[:, :], ramp_f[:, 0:NW + 1], float(WN), None, ALU.mult))
                step(pool.iota(ramp[:, 0:T], [[1, T]], base=0, channel_multiplier=T))
                step(pool.tensor_copy(dup[:, 0, :], ramp[:, 0:T]))
                pool.memset(minus_half[:, :], -0.5)
                pool.memset(half[:, :], 0.5)
                pool.wait_ge(s_ends, 1)
                pool.partition_all_reduce(ends_all[:, :, :].rearrange("p a g -> p (a g)"),
                                          ends[:, :, :].rearrange("p a g -> p (a g)"), P, RMAX).then_inc(s_all, 1)

            @block.vector
            def _(dve):
                step = Chain(dve, s_ch)
                dve.wait_ge(s_ld, 80)
                dve.wait_ge(s_pool, 9)
                step(dve.memset(ones[:, :], 1.0))
                step(dve.tensor_copy(dst_f[:, :, :], dst_i[:, :, :]))
                last = dst_f[:, NG - 1, :]
                step(dve.tensor_scalar(dup[:, 1, :], dup[:, 0, :], float(DUP), None, ALU.is_ge))
                step(dve.tensor_scalar(last, last, 1.0, None, ALU.add))
                step(dve.tensor_tensor(last, last, dup[:, 1, :], ALU.mult))
                step(dve.tensor_scalar(last, last, -1.0, None, ALU.add))
                step(dve.tensor_reduce(ends[:, 0, :], dst_f[:, :, :], AX, ALU.max))
                step(dve.tensor_reduce(ends[:, 1, :], dst_f[:, :, :], AX, ALU.min))
                step(dve.tensor_scalar(dup[:, 2, :], dup[:, 1, :], -2.0 * N, 2.0 * N, ALU.mult, ALU.add))
                step(dve.tensor_tensor(dup[:, 2, :], dup[:, 2, :], last, ALU.add))
                step(dve.tensor_reduce(ends[:, 1, NG - 1:NG], dup[:, 2, :], AX, ALU.min))
                dve.tensor_scalar(ends[:, 1, :], ends[:, 1, :], -1.0, None, ALU.mult).then_inc(s_ends, 1)
                dve.wait_ge(s_all, 1)
                step(dve.tensor_scalar(ends[:, 1, :], ends_all[:, 1, :], -1.0, None, ALU.mult))
                step(dve.tensor_scalar(wf[:, 5, :], window_start[:, 0:NW], float(WN - 1), None, ALU.add))

                def by_window(ap):
                    return ap.unsqueeze(1).broadcast_to([P, NW, NG])

                step(dve.tensor_tensor(touch[:, 0], by_window(ends_all[:, 0, :]), over(window_start[:, 0:NW], NG), ALU.is_ge))
                step(dve.tensor_tensor(touch[:, 1], by_window(ends[:, 1, :]), over(wf[:, 5, :], NG), ALU.is_le))
                step(dve.tensor_tensor(touch[:, 0], touch[:, 0], touch[:, 1], ALU.mult))
                step(dve.tensor_tensor(touch[:, 1], touch[:, 0], by_window(ramp_f[:, 1:NG + 1]), ALU.mult))
                step(dve.tensor_reduce(wf[:, 0, :], touch[:, 1], AX, ALU.max))
                step(dve.tensor_scalar(wf[:, 0, :], wf[:, 0, :], 1.0, None, ALU.max))
                step(dve.tensor_scalar(ends[:, 0, :], ramp_f[:, 0:NG], -1.0, float(NG), ALU.mult, ALU.add))
                step(dve.tensor_tensor(touch[:, 1], touch[:, 0], by_window(ends[:, 0, :]), ALU.mult))
                step(dve.tensor_reduce(wf[:, 1, :], touch[:, 1], AX, ALU.max))
                step(dve.tensor_scalar(wf[:, 1, :], wf[:, 1, :], -1.0, float(NG), ALU.mult, ALU.add))
                step(dve.tensor_scalar(wf[:, 2, :], wf[:, 0, :], -1.0, None, ALU.add))
                step(dve.tensor_tensor(wf[:, 1, :], wf[:, 1, :], wf[:, 2, :], ALU.min))
                step(dve.tensor_tensor(wf[:, 2, :], wf[:, 0, :], wf[:, 1, :], ALU.subtract))
                step(dve.tensor_tensor_scan(wf[:, 3, :], ones[:, :], wf[:, 2, :], 0.0, ALU.mult, ALU.add))
                step(dve.tensor_tensor(wf[:, 3, :], wf[:, 3, :], wf[:, 2, :], ALU.subtract))
                step(dve.tensor_tensor(wf[:, 2, :], wf[:, 3, :], wf[:, 2, :], ALU.add))
                step(dve.memset(visits[:, :, :], 0))
                step(dve.tensor_copy(visits[:, 1:4, 0:NW], wf[:, 1:4, :]))
                step(dve.tensor_scalar(visits[:, 2, :], visits[:, 2, :], END_BIT, None, ALU.logical_shift_left))
                step(dve.tensor_scalar(visits[:, 3, :], visits[:, 3, :], CUM_BIT, None, ALU.logical_shift_left))
                step(dve.tensor_tensor(visits[:, 2, :], visits[:, 2, :], visits[:, 3, :], ALU.bitwise_or))
                step(dve.tensor_tensor(visits[:, 0, :], visits[:, 1, :], visits[:, 2, :], ALU.bitwise_or))
                step(dve.tensor_scalar(ends[:, 0, :], ramp_f[:, 0:NG], float(GE), float(LAST), ALU.mult, ALU.min))
                step(dve.tensor_copy(starts[:, :], ends[:, 0, :]))

        with Phase(nc, "first") as first:
            edge_term = first.sb("edge_term", [P, CH * P, A0])
            src_t = first.sb("src_t", [P, CH * P], I32)
            dst_t = first.sb("dst_t", [P, CH * P])
            with Phase(nc, "tiles") as ph:
                lens = ph.sb("lens", [P, CH * P])
                with Phase(nc, "strips") as pt:
                    FULL = TILES // P * P
                    REST = TILES - FULL - 1
                    row_i = pt.sb("row_i", [P, 2, CH, P], I32)
                    row = pt.sb("row", [P, 3, CH, P])
                    late = pt.sb("late", [P, CH, P])
                    strip = pt.sb("strip", [P, 4, NW * Q])
                    ramp_i = pt.sb("ramp_i", [P, NW * Q], I32)
                    tile_i = pt.sb("tile_i", [P, CH], I32)
                    tile_f = pt.sb("tile_f", [P, 2, CH])
                    ends = pt.sb("ends", [P, 2, CH])
                    touch = pt.sb("touch", [P, 3, CH, NW * Q])
                    reach = pt.sb("reach", [P, 2, NW * Q])
                    reach_all = pt.sb("reach_all", [P, 2, NW * Q])
                    wf = pt.sb("wf", [P, 6, NW])
                    wi = pt.sb("wi", [P, 2, NW], I32)
                    lo_i = pt.sb("lo_i", [P, NW * Q], I32)
                    turn_ps = pt.ps("turn_ps", [P, 3, 2 * BANK])
                    s_zero, s_ld, s_pool, s_ch, s_f, s_turned, s_reach, s_all, s_copied = (
                        pt.sem(n) for n in ("s_zero", "s_ld", "s_pool", "s_ch", "s_floats", "s_turned", "s_reach", "s_all", "s_copied"))
                    with nc.Block() as block:

                        @block.sync
                        def _(sp):
                            sp.wait_ge(s_zero, 3)
                            for to, fro in ((row_i[:, 0], a["src"]), (row_i[:, 1], a["dst"]), (row[:, 2], a["edge_weight"])):
                                sp.dma_start(to[:, 0:CH - 1, :],
                                             fro[0:FULL * P].rearrange("(c r i) -> r c i", r=P, i=P)).then_inc(s_ld, 16)
                                sp.dma_start(to[0:REST, CH - 1, :],
                                             fro[FULL * P:(TILES - 1) * P].rearrange("(r i) -> r i", i=P)).then_inc(s_ld, 16)
                                sp.dma_start(to[REST:REST + 1, CH - 1, TAIL0:P],
                                             fro[(TILES - 1) * P:E].rearrange("(r i) -> r i", r=1)).then_inc(s_ld, 16)
                            sp.wait_ge(s_ld, 144)

                        @block.gpsimd
                        def _(pool):
                            step = Chain(pool, s_pool)
                            step(pool.iota(ramp_i[:, :], [[WN, NW], [QN, Q]], base=0, channel_multiplier=0))
                            step(pool.tensor_copy(strip[:, 0, :], ramp_i[:, :]))
                            step(pool.iota(tile_i[:, :], [[P, CH]], base=1, channel_multiplier=1))
                            step(pool.tensor_copy(tile_f[:, 0, :], tile_i[:, :]))
                            pool.wait_ge(s_reach, 1)
                            pool.partition_all_reduce(reach_all[:, :, :].rearrange("p a w -> p (a w)"),
                                                      reach[:, :, :].rearrange("p a w -> p (a w)"), P, RMAX).then_inc(s_all, 1)

                        @block.vector
                        def _(dve):
                            dve.memset(row_i[:, 0], 0).then_inc(s_zero, 1)
                            dve.memset(row_i[:, 1], -1).then_inc(s_zero, 1)
                            dve.memset(row[:, 2], 0.0).then_inc(s_zero, 1)
                            step = Chain(dve, s_ch)
                            dve.wait_ge(s_ld, 144)
                            dve.tensor_copy(row[:, 0:2], row_i[:, :, :, :]).then_inc(s_f, 1)
                            dve.wait_ge(s_f, 1)
                            step(dve.tensor_reduce(ends[:, 0, :], row[:, 1], AX, ALU.max))
                            step(dve.tensor_scalar(late[:, :, :], row[:, 1], 0.0, 4.0 * N, ALU.is_lt, ALU.mult))
                            step(dve.tensor_tensor(late[:, :, :], late[:, :, :], row[:, 1], ALU.add))
                            step(dve.tensor_reduce(ends[:, 1, :], late[:, :, :], AX, ALU.min))
                            dve.wait_ge(s_pool, 4)
                            step(dve.tensor_scalar(strip[:, 1, :], strip[:, 0, :], float(QN - 1), None, ALU.add))
                            step(dve.tensor_scalar(tile_f[:, 1, :], tile_f[:, 0, :], -1.0, float(TILES + 1), ALU.mult, ALU.add))

                            def by_tile(ap):
                                return ap.unsqueeze(1).broadcast_to([P, CH, NW * Q])

                            step(dve.tensor_tensor(touch[:, 0], over(ends[:, 0, :], NW * Q), by_tile(strip[:, 0, :]), ALU.is_ge))
                            step(dve.tensor_tensor(touch[:, 1], over(ends[:, 1, :], NW * Q), by_tile(strip[:, 1, :]), ALU.is_le))
                            step(dve.tensor_tensor(touch[:, 0], touch[:, 0], touch[:, 1], ALU.mult))
                            for n in range(2):
                                step(dve.tensor_tensor(touch[:, 1 + n], touch[:, 0], over(tile_f[:, n, :], NW * Q), ALU.mult))
                            step(dve.tensor_reduce(reach[:, 0, :], touch[:, 1].rearrange("p c w -> p w c"), AX, ALU.max))
                            dve.tensor_reduce(reach[:, 1, :], touch[:, 2].rearrange("p c w -> p w c"), AX, ALU.max).then_inc(s_reach, 1)
                            dve.wait_ge(s_all, 1)
                            lo = strip[:, 2, :]
                            step(dve.tensor_scalar(lo, reach_all[:, 1, :], -1.0, float(TILES), ALU.mult, ALU.add))
                            step(dve.tensor_tensor(strip[:, 3, :], reach_all[:, 0, :], lo, ALU.subtract))
                            step(dve.tensor_reduce(wf[:, 0, :], strip[:, 3, :].rearrange("p (w q) -> p w q", q=Q), AX, ALU.max))
                            step(dve.tensor_scalar(wf[:, 0, :], wf[:, 0, :], 1.0, 1.0, ALU.max, ALU.add))
                            step(dve.tensor_copy(wi[:, 0, :], wf[:, 0, :]))
                            step(dve.tensor_scalar(wi[:, 1, :], wi[:, 0, :], 1, None, ALU.logical_shift_right))
                            step(dve.tensor_copy(wf[:, 1, :], wi[:, 1, :]))
                            step(dve.tensor_scalar(wf[:, 2, :], wf[:, 1, :], -float(STEP), float(TILES), ALU.mult, ALU.add))
                            by_strip = lo.rearrange("p (w q) -> p w q", q=Q)
                            step(dve.tensor_tensor(by_strip, by_strip, over(wf[:, 2, :], Q), ALU.min))
                            step(dve.memset(wf[:, 3, :], 1.0))
                            step(dve.tensor_tensor_scan(wf[:, 4, :], wf[:, 3, :], wf[:, 1, :], 0.0, ALU.mult, ALU.add))
                            step(dve.tensor_tensor(wf[:, 5, :], wf[:, 4, :], wf[:, 1, :], ALU.subtract))
                            step(dve.tensor_copy(wi[:, :, :], wf[:, 4:6, :]))
                            step(dve.tensor_scalar(wi[:, 0, :], wi[:, 0, :], TURN_BIT, None, ALU.logical_shift_left))
                            step(dve.tensor_tensor(turns_of[:, 0, :], wi[:, 0, :], wi[:, 1, :], ALU.bitwise_or))
                            step(dve.tensor_copy(lo_i[:, :], lo))
                            los = lo_i[:, :].rearrange("p (w q) -> p q w", q=Q)
                            step(dve.tensor_copy(turns_of[:, 2, :], los[:, 3, :]))
                            for n in (1, 2):
                                step(dve.tensor_scalar(wi[:, 0, :], los[:, n, :], n * TILE_BIT, None, ALU.logical_shift_left))
                                step(dve.tensor_tensor(turns_of[:, 1, :], wi[:, 0, :],
                                                       los[:, 0, :] if n == 1 else turns_of[:, 1, :], ALU.bitwise_or))

                        @block.tensor
                        def _(pe):
                            pe.wait_ge(s_f, 1)
                            for n in range(3):
                                for c in range(CH):
                                    last = nc.tensor.transpose(turn_ps[:, n, c * P:(c + 1) * P], row[:, n, c, :], ident[:, :])
                            last.then_inc(s_turned, 1)

                        @block.scalar
                        def _(act):
                            act.wait_ge(s_turned, 1)
                            act.copy(src_t[:, :], turn_ps[:, 0, 0:CH * P]).then_inc(s_copied, 1)
                            act.copy(dst_t[:, :], turn_ps[:, 1, 0:CH * P]).then_inc(s_copied, 1)
                            act.copy(lens[:, :], turn_ps[:, 2, 0:CH * P]).then_inc(s_copied, 1)

                w_proj = ph.sb("w_proj", [F, HEADS0, F])
                score = ph.sb("score", [F, 2, HEADS0, F])
                prod = ph.sb("prod", [F, HEADS0, F])
                u = ph.sb("u", [F, A0])
                neg_c = ph.sb("neg_c", [P, 1])
                logits = ph.sb("logits", [WN, NW, A0])
                top = ph.sb("top", [P, A0 + 1])
                top_all = ph.sb("top_all", [P, A0 + 1])
                s_ld, s_ch = ph.sem("s_ld"), ph.sem("s_ch")
                s_top, s_all, s_st, s_neg = ph.sem("s_top"), ph.sem("s_all"), ph.sem("s_st"), ph.sem("s_neg")
                with nc.Block() as block:

                    @block.sync
                    def _(sp):
                        sp.dma_start(w_proj[:, :, :], a["L0_gnn_w_proj"].rearrange("h f g -> f h g")).then_inc(s_ld, 16)
                        for n, name in enumerate(("L0_gnn_radial_score", "L0_gnn_tangential_score")):
                            sp.dma_start(score[:, n], a[name].partition_broadcast(F)).then_inc(s_ld, 16)
                        sp.dma_start(neg_c[:, :], a["L0_gnn_radial_distance_scale"].partition_broadcast(P)).then_inc(s_ld, 16)
                        sp.wait_ge(s_ld, 64)

                    @block.vector
                    def _(dve):
                        step = Chain(dve, s_ch)
                        dve.wait_ge(s_ld, 64)
                        for n in range(2):
                            step(dve.tensor_tensor(prod[:, :, :], w_proj[:, :, :], score[:, n], ALU.mult))
                            step(dve.tensor_reduce(u[:, n * HEADS0:(n + 1) * HEADS0], prod[:, :, :], AX, ALU.add))
                        step(dve.tensor_scalar(neg_c[:, :], neg_c[:, :], -1.0, None, ALU.mult))
                        step(dve.tensor_scalar(lens[:, :], lens[:, :], neg_c[:, 0:1], None, ALU.mult))

                node_linear(nc, "l0", x, [(0, F)], lambda k: u[:, :], A0, None, logits)

                with nc.Block() as block:

                    @block.sync
                    def _(sp):
                        t = table0.rearrange("(w p) c -> p w c", p=WN)
                        with nc.allow_non_contiguous_dma("table rows"):
                            sp.dma_start(t[:, :, 0:F], x[:, :, :]).then_inc(s_st, 16)
                            sp.dma_start(t[:, :, F:ROW0], logits[:, :, :]).then_inc(s_st, 16)
                        sp.wait_ge(s_st, 32)

                    @block.gpsimd
                    def _(pool):
                        pool.wait_ge(s_top, 1)
                        pool.partition_all_reduce(top_all[:, :], top[:, :], P, RMAX).then_inc(s_all, 1)

                    @block.vector
                    def _(dve):
                        step = Chain(dve, s_neg)
                        flat = lens[:, :]
                        step(dve.memset(top[:, :], -3e38))
                        step(dve.tensor_reduce(top[0:WN, 0:A0], logits[:, :, :].rearrange("p w h -> p h w"), AX, ALU.max))
                        dve.tensor_reduce(top[:, A0:A0 + 1], flat, AX, ALU.max).then_inc(s_top, 1)
                        dve.wait_ge(s_all, 1)
                        step(dve.tensor_scalar(top_all[:, 0:HEADS0], top_all[:, 0:HEADS0], top_all[:, A0:A0 + 1], None, ALU.add))
                        shift = top_all[:, 0:A0].unsqueeze(1).broadcast_to([P, CH * P, A0])
                        step(dve.memset(edge_term[:, :, HEADS0:A0], 0.0))
                        step(dve.tensor_copy(edge_term[:, :, 0:HEADS0], over(flat, HEADS0)))
                        step(dve.tensor_tensor(edge_term[:, :, :], edge_term[:, :, :], shift, ALU.subtract))

            NUM, EA, DEN, DEG, RAW = 0, A0 * F, A0 * F + F, A0 * F + F + A0, A0 * F + F + A0 + 1
            raw = first.sb("raw", [WN, NW, RAW])
            with Phase(nc, "edges0") as ph:
                zeros = ph.sb("zeros", [P, BANK], BF16)
                node_ids = ph.sb("node_ids", [P, N], F16)
                place = ph.sb("place", [P, QN])
                strip_start = ph.sb("strip_start", [P, NW * Q])
                src_f = ph.sb("src_f", [P, CH * P])
                idx = ph.sb("idx", [P, 2, Q], I32)
                rows = ph.sb("rows", [P, 2, Q, ROW0])
                into = ph.sb("into", [P, 2, Q, QN])
                into16 = ph.sb("into16", [P, 2, Q, QN], BF16)
                fro = ph.sb("fro", [P, 2, Q, N], BF16)
                logit = ph.sb("logit", [P, 2, Q, A0])
                prob = ph.sb("prob", [P, 2, Q, A0 + 1])
                weighted = ph.sb("weighted", [P, 2, Q, A0, F])
                ea = ph.sb("ea", [P, 2, Q, F])
                counts = ph.sb("counts", [WN, N], BF16)
                turned = ph.sb("turned", [WN, NW, WN], BF16)
                acc = ph.ps("acc", [P, 8 * BANK])
                TAIL = N
                NUM_PS = 7 * BANK
                turned_ps = acc[:, 0:4 * BANK].bitcast(BF16).rearrange("p (c n) -> p c n", n=P)
                s_idx, s_m, s_m_act, s_half = (ph.sem(n) for n in ("s_idx", "s_weighted", "s_weighted_act", "s_half_done"))
                s_rows = [ph.sem(f"s_rows{h}") for h in range(2)]
                s_ea = [ph.sem(f"s_ea{h}") for h in range(2)]
                s_into, s_into16, s_logit, s_prob, s_fro = (
                    ph.sem(n) for n in ("s_into", "s_into16", "s_logit", "s_prob", "s_fro"))
                s_free, s_counts, s_trps, s_turned, s_ctd, s_ctfree, s_init, s_iota, s_seen = (
                    ph.sem(n) for n in ("s_acc_free", "s_counts", "s_turned_ps", "s_turned", "s_counts_stored",
                                        "s_turned_free", "s_init", "s_iota", "s_seen"))
                s_ea_go = ph.sem("s_ea_go")
                BY_ACT = 4

                with nc.Block() as block:

                    @block.sync
                    def _(sp):
                        def body(w, tile, v):
                            for h in range(2):
                                first_edges = []
                                for q in range(Q):
                                    t = tile(q, h)
                                    early = ((t + ((1 << TILE_BIT) - TILES + 1)) >> TILE_BIT) * TAIL0
                                    first_edges.append(in_range(sp.snap(t * P - early), 0, E - P, "full tiles within the edges"))
                                sp.wait_ge(s_half, 2 * v + h + 1)
                                sp.sem_inc(s_ea_go, 1)
                                for q, e0 in enumerate(first_edges):
                                    sp.dma_start(ea[:, h, q, :], a["edge_attr_64"][bass.ds(e0, P), :]).then_inc(s_ea[h], 16)

                        def after(w, end):
                            sp.wait_ge(s_turned, w * 4 + 4)
                            sp.dma_start(counts_t[bass.ds(w, 1)].squeeze(0),
                                         turned[:, :, :].rearrange("p c n -> p (c n)")).then_inc(s_ctd, 16)
                            sp.wait_ge(s_ctd, w * 16 + 16)
                            sp.sem_inc(s_ctfree, 1)

                        loop_strips(sp, body, after=after)

                    @block.gpsimd
                    def _(pool):
                        pool.iota(node_ids[:, :], [[1, N]], base=-(N // 2), channel_multiplier=0,
                                  allow_small_or_imprecise_dtypes=True).then_inc(s_iota, 1)
                        pool.iota(place[:, :], [[1, QN]], base=0, channel_multiplier=0,
                                  allow_small_or_imprecise_dtypes=True).then_inc(s_iota, 1)
                        pool.iota(strip_start[:, :], [[WN, NW], [QN, Q]], base=0, channel_multiplier=0,
                                  allow_small_or_imprecise_dtypes=True).then_inc(s_iota, 1)

                        def body(w, tile, v):
                            for h in range(2):
                                t = [tile(q, h) for q in range(Q)]
                                pool.wait_ge(s_m, 2 * v + h + 1)
                                pool.wait_ge(s_m_act, 2 * v + h + 1)
                                for q in range(Q):
                                    last = pool.tensor_copy(idx[:, h, q:q + 1], src_t[:, bass.ds(t[q], 1)])
                                last.then_inc(s_idx, 1)
                                pool.wait_ge(s_idx, 2 * v + h + 1)
                                pool.sem_inc(s_seen, 1)
                                for q in range(Q):
                                    pool.indirect_dma_start(rows[:, h, q, :], None, table0,
                                                            bass.IndirectOffsetOnAxis(ap=idx[:, h, q:q + 1], axis=0)).then_inc(s_rows[h], 16)

                        loop_strips(pool, body)

                    @block.vector
                    def _(dve):
                        dve.memset(zeros[:, :], 0.0).then_inc(s_init, 1)
                        dve.memset(prob[:, :, :, A0:A0 + 1], 1.0).then_inc(s_init, 1)
                        dve.tensor_scalar(src_f[:, :], src_t[:, :], -float(N // 2), None, ALU.add).then_inc(s_init, 1)
                        dve.sem_inc(s_m, 2)
                        dve.wait_ge(s_init, 3)
                        dve.wait_ge(s_iota, 3)

                        def body(w, tile, v):
                            for h in range(2):
                                k = 2 * v + h + 1
                                t = [tile(q, h) for q in range(Q)]
                                dve.wait_ge(s_half, k)
                                for q in range(Q):
                                    last = dve.tensor_scalar(into[:, h, q, :], place[:, :], strip_start[:, bass.ds(w * Q + q, 1)],
                                                             dst_t[:, bass.ds(t[q], 1)], ALU.add, ALU.is_equal)
                                last.then_inc(s_into, 1)

                                def starts_at(q):
                                    return dve.tensor_scalar(fro[:, h, q, :], node_ids[:, :], src_f[:, bass.ds(t[q], 1)],
                                                             None, ALU.is_equal)

                                starts_at(0)
                                starts_at(1)
                                dve.wait_ge(s_rows[h], 16 * Q * (v + 1))
                                for q in range(Q):
                                    last = dve.tensor_tensor(logit[:, h, q, :], rows[:, h, q, F:ROW0],
                                                             edge_term[:, bass.ds(t[q], 1), :].squeeze(1), ALU.add)
                                last.then_inc(s_logit, 1)
                                starts_at(2)
                                starts_at(3).then_inc(s_fro, 1)
                                dve.wait_ge(s_prob, k)
                                n = A0 - BY_ACT
                                dve.tensor_tensor(weighted[:, h, :, 0:n, :], rows[:, h, :, 0:F].unsqueeze(2).broadcast_to([P, Q, n, F]),
                                                  prob[:, h, :, 0:n].unsqueeze(3).broadcast_to([P, Q, n, F]),
                                                  ALU.mult).then_inc(s_m, 1)

                        loop_strips(dve, body)

                    @block.scalar
                    def _(act):
                        act.sem_inc(s_free, 1)
                        act.sem_inc(s_ctfree, 1)
                        act.sem_inc(s_m_act, 2)
                        act.preload_act_table(ACT.Exp)
                        act.wait_ge(s_init, 3)

                        def body(w, tile, v):
                            for h in range(2):
                                k = 2 * v + h + 1
                                act.wait_ge(s_into, k)
                                act.copy(into16[:, h], into[:, h]).then_inc(s_into16, 1)
                                act.wait_ge(s_logit, k)
                                act.activation(prob[:, h, :, 0:A0], logit[:, h], ACT.Exp).then_inc(s_prob, 1)
                                act.wait_ge(s_prob, k)
                                for q in range(Q):
                                    for n in range(A0 - BY_ACT, A0):
                                        last = act.activation(weighted[:, h, q, n, :], rows[:, h, q, 0:F], ACT.Copy,
                                                              scale=prob[:, h, q, n:n + 1])
                                last.then_inc(s_m_act, 1)

                        def after(w, end):
                            act.wait_ge(s_half, 2 * end + 2)
                            act.copy(raw[:, bass.ds(w, 1), EA:RAW].squeeze(1), acc[0:WN, TAIL:TAIL + RAW - EA])
                            act.copy(raw[:, bass.ds(w, 1), NUM:EA].squeeze(1), acc[0:WN, NUM_PS:NUM_PS + EA])
                            act.copy(counts[:, :], acc[0:WN, 0:N]).then_inc(s_counts, 1)
                            act.wait_ge(s_ctfree, w + 1)
                            for b in range(4):
                                c0, c1 = 8 * b, min(8 * b + 8, NW)
                                act.wait_ge(s_trps, w * 4 + b + 1)
                                act.copy(turned[:, c0:c1, :], turned_ps[0:WN, c0:c1, 0:WN]).then_inc(s_turned, 1)
                            act.wait_ge(s_turned, w * 4 + 4)
                            act.sem_inc(s_free, 1)

                        loop_strips(act, body, after=after)

                    @block.tensor
                    def _(pe):
                        pe.sem_inc(s_half, 2)
                        pe.wait_ge(s_init, 3)

                        def strip_of(q, c0, c1):
                            return acc[q * QN:(q + 1) * QN, c0:c1]

                        def before(w):
                            pe.wait_ge(s_free, w + 1)
                            for b in range(8):
                                for q in range(Q):
                                    nc.tensor.matmul(strip_of(q, b * BANK, (b + 1) * BANK), zeros[:, 0:QN], zeros[:, :],
                                                     start=True, stop=True, tile_position=(0, q * QN))

                        def add(q, c0, c1, lhsT, rhs):
                            return nc.tensor.matmul(strip_of(q, c0, c1), lhsT, rhs, start=False, stop=True,
                                                    skip_group_check=True, tile_position=(0, q * QN))

                        def body(w, tile, v):
                            for h in range(2):
                                k = 2 * v + h + 1
                                pe.wait_ge(s_into16, k)
                                pe.wait_ge(s_fro, k)
                                for c in range(0, N, BANK):
                                    for q in range(Q):
                                        add(q, c, min(c + BANK, N), into16[:, h, q, :], fro[:, h, q, c:min(c + BANK, N)])
                                pe.wait_ge(s_ea[h], 16 * Q * (v + 1))
                                pe.wait_ge(s_m, 2 + k)
                                pe.wait_ge(s_m_act, 2 + k)
                                for q in range(Q):
                                    add(q, NUM_PS, NUM_PS + EA, into[:, h, q, :], weighted[:, h, q].rearrange("p n f -> p (n f)"))
                                for q in range(Q):
                                    add(q, TAIL, TAIL + F, into[:, h, q, :], ea[:, h, q, :])
                                for q in range(Q):
                                    last = add(q, TAIL + F, TAIL + RAW - EA, into[:, h, q, :], prob[:, h, q, :])
                                last.then_inc(s_half, 1)

                        def after(w, end):
                            pe.wait_ge(s_counts, w + 1)
                            for c in range(NW):
                                last = nc.tensor.transpose(turned_ps[0:WN, c, 0:WN], counts[:, c * WN:(c + 1) * WN],
                                                           ident16[0:WN, 0:WN])
                                if c % 8 == 7 or c == NW - 1:
                                    last.then_inc(s_trps, 1)

                        loop_strips(pe, body, before, after)

            with Phase(nc, "nodes0") as ph:
                rden = ph.sb("rden", [WN, NW, A0])
                twice = ph.sb("twice", [WN, NW, F])
                w_heads = ph.sb("w_heads", [P, 2, F])
                w_out = ph.sb("w_out", [F, F])
                mean = ph.sb("mean", [WN, NW, F])
                y = ph.sb("y", [WN, NW, F])
                s_ld, s_ch, s_ch2, s_ch3 = ph.sem("s_ld"), ph.sem("s_ch"), ph.sem("s_ch2"), ph.sem("s_ch3")
                msg = raw[:, :, 0:HEADS0 * F]
                with nc.Block() as block:

                    @block.sync
                    def _(sp):
                        wh = a["L0_gnn_w_proj"].rearrange("h f g -> (h f) g").rearrange("(k p) g -> p k g", p=P)
                        sp.dma_start(w_heads[:, :, :], wh).then_inc(s_ld, 16)
                        sp.dma_start(w_out[:, :], a["L0_gnn_w_out"]).then_inc(s_ld, 16)
                        with nc.allow_non_contiguous_dma("rows"):
                            sp.dma_start(edge_sum, raw[:, :, EA:DEN]).then_inc(s_ld, 16)
                        sp.wait_ge(s_ld, 48)

                    @block.vector
                    def _(dve):
                        step = Chain(dve, s_ch)
                        step(dve.tensor_copy(deg[:, :], raw[:, :, DEG:RAW].squeeze(2)))
                        step(dve.tensor_scalar(rden[:, :, :], raw[:, :, DEN:DEG], TINY, None, ALU.max))
                        step(dve.reciprocal(rden[:, :, :], rden[:, :, :]))
                        for k in range(A0):
                            part = raw[:, :, k * F:(k + 1) * F]
                            step(dve.tensor_tensor(part, part, over(rden[:, :, k], F), ALU.mult))
                        step(dve.tensor_tensor(msg, msg, raw[:, :, HEADS0 * F:A0 * F], ALU.add))
                        step(dve.tensor_scalar(stat[:, 0, :], deg[:, :], 1.0, 2.0, ALU.min, ALU.mult))
                        step(dve.tensor_tensor(twice[:, :, :], x[:, :, :], over(stat[:, 0, :], F), ALU.mult))
                        for k in range(HEADS0):
                            part = raw[:, :, k * F:(k + 1) * F]
                            step(dve.tensor_tensor(part, part, twice[:, :, :], ALU.subtract))

                node_linear(nc, "heads", raw, [(0, P), (P, P)], lambda k: w_heads[:, k, :], F, None, mean, 1.0 / HEADS0)
                with nc.Block() as block:

                    @block.vector
                    def _(dve):
                        step = Chain(dve, s_ch2)
                        step(dve.tensor_tensor(twice[:, :, :], mean[:, :, :], mean[:, :, :], ALU.is_equal))
                        step(dve.memset(y[:, :, :], 0.0))
                        step(dve.copy_predicated(y[:, :, :], twice[:, :, :].bitcast(I32), mean[:, :, :]))
                        step(dve.tensor_scalar(mean[:, :, :], y[:, :, :], 3.4028234e38, -3.4028234e38, ALU.min, ALU.max))

                node_linear(nc, "out0", mean, [(0, F)], lambda k: w_out[:, :], F, None, y)
                norm = Norm(ph, "norm", stat, minus_half)
                with nc.Block() as block:

                    @block.gpsimd
                    def _(pool):
                        norm.on_gpsimd(pool)

                    @block.vector
                    def _(dve):
                        step = Chain(dve, s_ch3)
                        step(dve.tensor_tensor(y[:, :, :], y[:, :, :], x[:, :, :], ALU.add))
                        step(dve.tensor_tensor(y[:, :, :], y[:, :, :], x[:, :, :], ALU.add))
                        norm.on_vector(step, dve, y[:, :, :], x[:, :, :], twice[:, :, :])

        def dense_sum(tag, counts_sb, parts, dst):
            with Phase(nc, tag) as ph:
                sum_ps = ph.ps("sum_ps", [WN, U, BANK])
                s_sum, s_out = ph.sem("s_sum"), ph.sem("s_out")
                with nc.Block() as block:

                    @block.tensor
                    def _(pe):
                        with pe.Fori(0, NW // U) as i:
                            for u in range(U):
                                w = i * U + u
                                pe.wait_ge(s_out, w + 1)
                                for c in range(NW):
                                    last = nc.tensor.matmul(sum_ps[:, u, 0:3 * F],
                                                            counts_sb[:, bass.ds(w, 1), c * WN:(c + 1) * WN].squeeze(1),
                                                            parts[:, c, :, :].rearrange("p k f -> p (k f)"),
                                                            start=(c == 0), stop=(c == NW - 1))
                                last.then_inc(s_sum, 1)

                    @block.vector
                    def _(dve):
                        dve.sem_inc(s_out, U)
                        with dve.Fori(0, NW // U) as i:
                            for u in range(U):
                                w = i * U + u
                                dve.wait_ge(s_sum, w + 1)
                                dve.tensor_reduce(dst[:, bass.ds(w, 1), 0:F].squeeze(1),
                                                  sum_ps[:, u, 0:3 * F].rearrange("p (k f) -> p f k", k=3),
                                                  AX, ALU.add).then_inc(s_out, 1)

        def split3(step, dve, parts, rest, src):
            step(dve.tensor_copy(parts[:, :, 0, :], src))
            step(dve.tensor_tensor(rest, src, parts[:, :, 0, :], ALU.subtract))
            step(dve.tensor_copy(parts[:, :, 1, :], rest))
            step(dve.tensor_tensor(rest, rest, parts[:, :, 1, :], ALU.subtract))
            step(dve.tensor_copy(parts[:, :, 2, :], rest))

        with Phase(nc, "rounds") as ph:
            counts_sb = ph.sb("counts_sb", [WN, NW, N], BF16)
            parts = ph.sb("parts", [WN, NW, 3, F], BF16)
            cat = ph.sb("cat", [WN, NW, 2 * F])
            w_lr = ph.sb("w_lr", [P, 3, F])
            w_one = ph.sb("w_one", [F, 2, F])
            vecs = ph.sb("vecs", [WN, 11, F])
            inv_deg = ph.sb("inv_deg", [WN, NW])
            y = ph.sb("y", [WN, NW, F])
            h_in = cat[:, :, F:2 * F]
            s_ld, s_ct = ph.sem("s_ld"), ph.sem("s_ct")
            with nc.Block() as block:

                @block.sync
                def _(sp):
                    for w in range(NW):
                        sp.dma_start(counts_sb[:, w, :], counts_t[w]).then_inc(s_ct, 16)
                    sp.wait_ge(s_ct, 16 * NW)

                @block.scalar
                def _(act):
                    with nc.allow_non_contiguous_dma("weights"):
                        act.dma_start(w_lr[0:F, :, :], a["L1_gnn_w_l"].rearrange("l f g -> f l g")).then_inc(s_ld, 16)
                        act.dma_start(w_lr[F:P, :, :], a["L1_gnn_w_r"].rearrange("l f g -> f l g")).then_inc(s_ld, 16)
                    act.dma_start(w_one[:, 0, :], a["L1_gnn_w_res"]).then_inc(s_ld, 16)
                    act.dma_start(w_one[:, 1, :], a["L1_gnn_w_fc"]).then_inc(s_ld, 16)
                    for n, name in enumerate(("L1_gnn_b_l", "L1_gnn_gamma", "L1_gnn_beta")):
                        act.dma_start(vecs[:, 3 * n:3 * n + 3, :], a[name].partition_broadcast(WN)).then_inc(s_ld, 16)
                    act.dma_start(vecs[:, 9, :], a["L1_gnn_b_res"].partition_broadcast(WN)).then_inc(s_ld, 16)
                    act.dma_start(vecs[:, 10, :], a["L1_gnn_b_fc"].partition_broadcast(WN)).then_inc(s_ld, 16)
                    act.wait_ge(s_ld, 16 * 9)

                s_ch = ph.sem("s_prep")

                @block.vector
                def _(dve):
                    step = Chain(dve, s_ch)
                    step(dve.tensor_scalar(inv_deg[:, :], deg[:, :], 1.0, None, ALU.max))
                    step(dve.reciprocal(inv_deg[:, :], inv_deg[:, :]))
                    step(dve.tensor_scalar(stat[:, 0, :], deg[:, :], 1.0, None, ALU.min))
                    step(dve.tensor_tensor(inv_deg[:, :], inv_deg[:, :], stat[:, 0, :], ALU.mult))
                    step(dve.tensor_copy(h_in, x[:, :, :]))
                    split3(step, dve, parts, y[:, :, :], x[:, :, :])

            for r in range(3):
                dense_sum(f"r{r}", counts_sb, parts, cat)
                s_ch = ph.sem(f"s_mean{r}")
                with nc.Block() as block:

                    @block.vector
                    def _(dve):
                        step = Chain(dve, s_ch)
                        step(dve.tensor_tensor(cat[:, :, 0:F], cat[:, :, 0:F], over(inv_deg[:, :], F), ALU.mult))

                node_linear(nc, f"lr{r}", cat, [(0, P)], lambda k: w_lr[:, r, :], F, vecs[:, r, :], y)
                s_ch = ph.sem(f"s_round{r}")
                norm = Norm(ph, f"norm{r}", stat, minus_half)
                with nc.Block() as block:

                    @block.gpsimd
                    def _(pool):
                        norm.on_gpsimd(pool)

                    @block.vector
                    def _(dve):
                        def each(n):
                            return vecs[:, n, :].unsqueeze(1).broadcast_to([WN, NW, F])
                        step = Chain(dve, s_ch)
                        norm.on_vector(step, dve, y[:, :, :], y[:, :, :], cat[:, :, 0:F])
                        step(dve.tensor_tensor(y[:, :, :], y[:, :, :], each(3 + r), ALU.mult))
                        step(dve.tensor_tensor(y[:, :, :], y[:, :, :], each(6 + r), ALU.add))
                        step(dve.tensor_scalar(y[:, :, :], y[:, :, :], 0.0, None, ALU.max))

                residual = h_in
                if r == 0:
                    residual = cat[:, :, 0:F]
                    node_linear(nc, "res", x, [(0, F)], lambda k: w_one[:, 0, :], F, vecs[:, 9, :], cat)
                s_ch = ph.sem(f"s_sum{r}")
                with nc.Block() as block:

                    @block.vector
                    def _(dve):
                        step = Chain(dve, s_ch)
                        step(dve.tensor_tensor(h_in, y[:, :, :], residual, ALU.add))
                        if r < 2:
                            split3(step, dve, parts, y[:, :, :], h_in)

            node_linear(nc, "fc", h_in, [(0, F)], lambda k: w_one[:, 1, :], F, vecs[:, 10, :], y)
            s_ch = ph.sem("s_norm1")
            norm = Norm(ph, "norm", stat, minus_half)
            with nc.Block() as block:

                @block.gpsimd
                def _(pool):
                    norm.on_gpsimd(pool)

                @block.vector
                def _(dve):
                    step = Chain(dve, s_ch)
                    step(dve.tensor_tensor(y[:, :, :], y[:, :, :], x[:, :, :], ALU.add))
                    norm.on_vector(step, dve, y[:, :, :], x[:, :, :], cat[:, :, 0:F])

        with Phase(nc, "attention") as layer:
            bias = layer.sb("bias", [P, NG, T * HEADS2])
            q = layer.sb("q", [WN, NW + 1, F])
            attn = layer.sb("attn", [WN, NW, F + HEADS2])
            w_sq = layer.sb("w_sq", [F, 4, F])
            b_sq = layer.sb("b_sq", [WN, 4, F])
            QUADS = 2
            with Phase(nc, "bias") as ph:
                attr = ph.sb("attr", [P, 2, 2, T, ED])
                attr_t = ph.sb("attr_t", [P, 2, 2 * QUADS, P])
                hidden = ph.sb("hidden", [P, 2, 2 * QUADS, P])
                w1 = ph.sb("w1", [P, P])
                w2 = ph.sb("w2", [P, H * HEADS2])
                b1 = ph.sb("b1", [P, 1])
                b2 = ph.sb("b2", [P, T, HEADS2])
                t_ps = ph.ps("t_ps", [P, 2, 2 * QUADS, P])
                h_ps = ph.ps("h_ps", [P, 2, 2 * QUADS, P])
                b_ps = ph.ps("b_ps", [P, 2, BANK])
                s_ld, s_zero, s_w = ph.sem("s_ld"), ph.sem("s_zero"), ph.sem("s_w")
                with nc.Block() as block:

                    @block.gpsimd
                    def _(pool):
                        pool.memset(w1[:, :], 0.0).then_inc(s_zero, 1)
                        pool.memset(w2[:, :], 0.0).then_inc(s_zero, 1)

                    @block.sync
                    def _(sp):
                        sp.wait_ge(s_zero, 2)
                        n = 0
                        with nc.allow_non_contiguous_dma("weights"):
                            for k in range(H):
                                r = slice(k * ED, (k + 1) * ED)
                                sp.dma_start(w1[r, r], a["L2_gnn_We1"]).then_inc(s_w, 16)
                                sp.dma_start(w2[r, k * HEADS2:(k + 1) * HEADS2], a["L2_gnn_We2"]).then_inc(s_w, 16)
                                sp.dma_start(b1[r, :], a["L2_gnn_be1"].rearrange("(f a) -> f a", a=1)).then_inc(s_w, 16)
                            for j in range(T):
                                sp.dma_start(b2[:, j, :], a["L2_gnn_be2"].partition_broadcast(P)).then_inc(s_w, 16)
                            for n, name in enumerate("QKVO"):
                                sp.dma_start(w_sq[:, n, :], a["L2_gnn_W" + name]).then_inc(s_w, 16)
                                sp.dma_start(b_sq[:, n, :], a["L2_gnn_b" + name].partition_broadcast(WN)).then_inc(s_w, 16)
                        sp.wait_ge(s_w, 16 * (3 * H + T + 8))

                s_attr = [ph.sem(f"s_attr{n}") for n in range(2)]
                s_t, s_tc, s_h, s_hc, s_b, s_bc = (ph.sem(n) for n in ("s_t", "s_tc", "s_h", "s_hc", "s_b", "s_bc"))
                TURNS = NG // 4
                assert NG == 4 * TURNS + 1

                def turns(eng, body):
                    with eng.Fori(0, TURNS) as i:
                        body(i, 2, 2)
                    body(TURNS, 1, 1)

                with nc.Block() as block:

                    @block.sync
                    def _(sp):
                        def body(i, slots, groups):
                            for s in range(slots):
                                sp.wait_ge(s_t, 2 * i + s + 1)
                                edges = a["edge_attr_32"]
                                for g in range(groups):
                                    e0 = LAST if groups == 1 else i * (4 * GE) + (2 * s + g) * GE
                                    rows = edges[bass.ds(e0, GE), :].rearrange("(p j) f -> p j f", j=T)
                                    sp.dma_start(attr[:, s, g], rows).then_inc(s_attr[s], 16)

                        turns(sp, body)

                    @block.tensor
                    def _(pe):
                        for s in (s_t, s_h, s_b):
                            pe.sem_inc(s, 2)

                        def body(i, slots, groups):
                            n = groups * QUADS
                            for s in range(slots):
                                pe.wait_ge(s_attr[s], 32 * i + 16 * groups)
                                pe.wait_ge(s_tc, 2 * i + s + 1)
                                for k in range(n):
                                    part = attr[:, s, k // QUADS, (k % QUADS) * H:(k % QUADS + 1) * H, :]
                                    last = nc.tensor.transpose(t_ps[:, s, k, :], part.rearrange("p j f -> p (j f)"), ident[:, :])
                                last.then_inc(s_t, 1)
                            for s in range(slots):
                                pe.wait_ge(s_tc, 2 * i + s + 3)
                                pe.wait_ge(s_hc, 2 * i + s + 1)
                                nc.tensor.matmul(h_ps[:, s, 0:n, :].rearrange("p k e -> p (k e)"), w1[:, :],
                                                 attr_t[:, s, 0:n, :].rearrange("p k e -> p (k e)"),
                                                 start=True, stop=True).then_inc(s_h, 1)
                            for s in range(slots):
                                pe.wait_ge(s_hc, 2 * i + s + 3)
                                pe.wait_ge(s_bc, 2 * i + s + 1)
                                for k in range(n):
                                    last = nc.tensor.matmul(b_ps[:, s, k * H * HEADS2:(k + 1) * H * HEADS2],
                                                            hidden[:, s, k, :], w2[:, :], start=True, stop=True)
                                last.then_inc(s_b, 1)

                        turns(pe, body)

                    @block.scalar
                    def _(act):
                        act.sem_inc(s_hc, 2)

                        def body(i, slots, groups):
                            n = groups * QUADS
                            for s in range(slots):
                                act.wait_ge(s_h, 2 * i + s + 3)
                                act.wait_ge(s_b, 2 * i + s + 1)
                                act.activation(hidden[:, s, 0:n, :], h_ps[:, s, 0:n, :], ACT.Silu, bias=b1[:, 0:1]).then_inc(s_hc, 1)

                        turns(act, body)

                    @block.vector
                    def _(dve):
                        dve.sem_inc(s_tc, 2)
                        dve.sem_inc(s_bc, 2)

                        def body(i, slots, groups):
                            n = groups * QUADS
                            for s in range(slots):
                                dve.wait_ge(s_t, 2 * i + s + 3)
                                dve.wait_ge(s_h, 2 * i + s + 1)
                                dve.tensor_copy(attr_t[:, s, 0:n, :], t_ps[:, s, 0:n, :]).then_inc(s_tc, 1)
                            for s in range(slots):
                                dve.wait_ge(s_b, 2 * i + s + 3)
                                g0 = NG - 1 if groups == 1 else i * 4 + 2 * s
                                dve.tensor_tensor(bias[:, bass.ds(g0, groups), :],
                                                  b_ps[:, s, 0:n * H * HEADS2].rearrange("p (g c) -> p g c", g=groups),
                                                  b2[:, :, :].rearrange("p j h -> p (j h)").unsqueeze(1)
                                                  .broadcast_to([P, groups, T * HEADS2]), ALU.add).then_inc(s_bc, 1)

                        turns(dve, body)

            with Phase(nc, "kvq") as ph:
                kv = ph.sb("kv", [WN, NW, 2 * F])
                sq = ph.sb("sq", [WN, NW, F])
                norms = ph.sb("norms", [WN, NW, HEADS2])
                top = ph.sb("top", [P, 3 * HEADS2])
                top_all = ph.sb("top_all", [P, 3 * HEADS2])
                bound = ph.sb("bound", [P, HEADS2])
                node_linear(nc, "q", x, [(0, F)], lambda k: w_sq[:, 0, :], F, b_sq[:, 0, :], q)
                node_linear(nc, "kv", x, [(0, F)], lambda k: w_sq[:, 1:3, :].rearrange("p a f -> p (a f)"), 2 * F,
                            b_sq[:, 1:3, :].rearrange("p a f -> p (a f)"), kv)
                s_st, s_ch, s_top, s_all = ph.sem("s_st"), ph.sem("s_ch"), ph.sem("s_top"), ph.sem("s_all")
                s_bound, s_root = ph.sem("s_bound"), ph.sem("s_root")
                with nc.Block() as block:

                    @block.sync
                    def _(sp):
                        with nc.allow_non_contiguous_dma("table rows"):
                            sp.dma_start(table_kv.rearrange("(w p) c -> p w c", p=WN), kv[:, :, :]).then_inc(s_st, 16)
                        sp.wait_ge(s_st, 16)

                    @block.gpsimd
                    def _(pool):
                        pool.wait_ge(s_top, 1)
                        pool.partition_all_reduce(top_all[:, :], top[:, :], P, RMAX).then_inc(s_all, 1)
                        pool.wait_ge(s_bound, 1)
                        pool.tensor_tensor(bound[:, :], bound[:, :], half[:, :], ALU.pow).then_inc(s_root, 1)

                    @block.vector
                    def _(dve):
                        step = Chain(dve, s_ch)
                        step(dve.memset(q[:, NW, :], 0.0))
                        step(dve.tensor_scalar(q[:, 0:NW, :], q[:, 0:NW, :], float(DK) ** -0.5, None, ALU.mult))
                        step(dve.memset(top[:, :], -3e38))
                        for n, of in enumerate((q[:, 0:NW, :], kv[:, :, 0:F])):
                            step(dve.tensor_tensor(sq[:, :, :], of, of, ALU.mult))
                            step(dve.tensor_reduce(norms[:, :, :], sq[:, :, :].rearrange("p w (h d) -> p w h d", d=DK), AX, ALU.add))
                            step(dve.tensor_reduce(top[0:WN, n * HEADS2:(n + 1) * HEADS2],
                                                   norms[:, :, :].rearrange("p w h -> p h w"), AX, ALU.max))
                        by_head = bias[:, :, :].rearrange("p g (j h) -> p (g j) h", h=HEADS2)
                        dve.tensor_reduce(top[:, 2 * HEADS2:3 * HEADS2], by_head.rearrange("p e h -> p h e"), AX,
                                          ALU.max).then_inc(s_top, 1)
                        dve.wait_ge(s_all, 1)
                        dve.tensor_tensor(bound[:, :], top_all[:, 0:HEADS2], top_all[:, HEADS2:2 * HEADS2],
                                          ALU.mult).then_inc(s_bound, 1)
                        dve.wait_ge(s_root, 1)
                        step(dve.tensor_tensor(bound[:, :], bound[:, :], top_all[:, 2 * HEADS2:3 * HEADS2], ALU.add))
                        step(dve.tensor_tensor(by_head, by_head, bound[:, :].unsqueeze(1).broadcast_to([P, NG * T, HEADS2]),
                                               ALU.subtract))

            with Phase(nc, "edges2") as ph:
                zeros = ph.sb("zeros", [P, P])
                idx = ph.sb("idx", [P, 2, H], I32)
                rows = ph.sb("rows", [P, 2, H, 2 * F])
                dst_rel = ph.sb("dst_rel", [P, 2, H])
                dst_ahead = ph.sb("dst_ahead", [P, 2, H])
                into = ph.sb("into", [P, 2, H, WN])
                ahead = ph.sb("ahead", [P, 2, H, WN])
                into_t = ph.sb("into_t", [WN, 2, H, P])
                prod = ph.sb("prod", [P, 2, H, F])
                score = ph.sb("score", [P, 2, H, HEADS2])
                weighted = ph.sb("weighted", [P, 2, H, F + HEADS2])
                t_ps = ph.ps("t_ps", [P, 2, H, P])
                q_ps = ph.ps("q_ps", [P, 2, H, P])
                acc = ph.ps("acc", [P, BANK])
                s_idx, s_rel, s_into, s_t, s_tc, s_q, s_prod, s_score, s_sb, s_exp, s_m, s_half, s_free, s_seen, s_init = (
                    ph.sem(n) for n in ("s_idx", "s_rel", "s_into", "s_turned_ps", "s_turned", "s_query", "s_prod",
                                        "s_dot", "s_score", "s_exp", "s_weighted", "s_half_done", "s_acc_free", "s_seen", "s_init"))
                s_rel2, s_ahead = ph.sem("s_rel_ahead"), ph.sem("s_ahead")
                s_rows = [ph.sem(f"s_rows{h}") for h in range(2)]

                def next_window(eng, w, v, end):
                    bit = END_BIT - CUM_BIT
                    last = in_range(eng.snap(1 - (((end - v - 2 + (1 << bit)) >> bit) & 1)), 0, 1, "one bit")
                    return last, in_range(eng.snap(w + last), 0, NW, "one past the last window at most")

                with nc.Block() as block:

                    @block.gpsimd
                    def _(pool):
                        def body(w, g, v, end):
                            for h in range(2):
                                pool.wait_ge(s_m, 2 * v + h + 1)
                                pool.tensor_copy(idx[:, h, :], src_i[:, bass.ds(g, 1), h * H:(h + 1) * H].squeeze(1)).then_inc(s_idx, 1)
                                pool.wait_ge(s_idx, 2 * v + h + 1)
                                pool.sem_inc(s_seen, 1)
                                for j in range(H):
                                    pool.indirect_dma_start(rows[:, h, j, :], None, table_kv,
                                                            bass.IndirectOffsetOnAxis(ap=idx[:, h, j:j + 1], axis=0)).then_inc(s_rows[h], 16)

                        loop_windows(pool, body)

                    @block.vector
                    def _(dve):
                        dve.memset(zeros[:, :], 0.0).then_inc(s_init, 1)
                        dve.sem_inc(s_m, 2)
                        dve.sem_inc(s_prod, 2)

                        def match(to, rel, s_rel, s_to, w, g, h, k):
                            dve.tensor_scalar(rel[:, h], dst_f[:, bass.ds(g, 1), h * H:(h + 1) * H].squeeze(1),
                                              window_start[:, bass.ds(w, 1)], None, ALU.subtract).then_inc(s_rel, 1)
                            dve.wait_ge(s_rel, k)
                            dve.tensor_tensor(to[:, h], iota_n[:, :].unsqueeze(1).broadcast_to([P, H, WN]),
                                              over(rel[:, h], WN), ALU.is_equal).then_inc(s_to, 1)

                        def match_ahead(w, g, h, k):
                            dve.wait_ge(s_t, k)
                            match(ahead, dst_ahead, s_rel2, s_ahead, w, g, h, k)

                        def match_into(w, g, h, k):
                            dve.wait_ge(s_half, k)
                            match(into, dst_rel, s_rel, s_into, w, g, h, k)

                        def scores(g, v, h, k):
                            dve.wait_ge(s_rows[h], 16 * H * (v + 1))
                            dve.wait_ge(s_q, 2 + k)
                            dve.tensor_tensor(prod[:, h], rows[:, h, :, 0:F], q_ps[:, h, :, 0:F], ALU.mult).then_inc(s_prod, 1)
                            dve.wait_ge(s_prod, 2 + k)
                            dve.tensor_reduce(score[:, h], prod[:, h].rearrange("p j (h d) -> p j h d", d=DK), AX,
                                              ALU.add).then_inc(s_score, 1)
                            dve.wait_ge(s_score, k)
                            dve.tensor_tensor(score[:, h], score[:, h],
                                              bias[:, bass.ds(g, 1), h * H * HEADS2:(h + 1) * H * HEADS2].squeeze(1)
                                              .rearrange("p (j h) -> p j h", h=HEADS2), ALU.add).then_inc(s_sb, 1)

                        def weigh(h, k):
                            dve.wait_ge(s_exp, k)
                            dve.tensor_tensor(weighted[:, h, :, 0:F].rearrange("p j (h d) -> p j h d", d=DK),
                                              rows[:, h, :, F:2 * F].rearrange("p j (h d) -> p j h d", d=DK),
                                              weighted[:, h, :, F:F + HEADS2].unsqueeze(3).broadcast_to([P, H, HEADS2, DK]),
                                              ALU.mult).then_inc(s_m, 1)

                        def body(w, g, v, end):
                            k = 2 * v + 1
                            last, w_next = next_window(dve, w, v, end)
                            g_next = dve.snap(g + 1 + last * (lo_next[0] - g - 1))
                            g_next = in_range(g_next, 0, NG - 1, "visits go to groups that exist")
                            scores(g, v, 0, k)
                            match_into(w, g, 1, k + 1)
                            weigh(0, k)
                            match_ahead(w_next, g_next, 0, k + 2)
                            scores(g, v, 1, k + 1)
                            match_into(w_next, g_next, 0, k + 2)
                            weigh(1, k + 1)
                            match_ahead(w_next, g_next, 1, k + 3)

                        def before(w):
                            lo_next[0] = dve.value_load(visits[0:1, 1, bass.ds(w + 1, 1)], min_val=0, max_val=NG - 1)

                        lo_next = [None]
                        g0 = dve.value_load(visits[0:1, 1, 0:1], min_val=0, max_val=NG - 1)
                        match_ahead(0, g0, 0, 1)
                        match_ahead(0, g0, 1, 2)
                        match_into(0, g0, 0, 1)
                        loop_windows(dve, body, before)

                    @block.scalar
                    def _(act):
                        act.sem_inc(s_free, 1)
                        act.sem_inc(s_tc, 2)
                        act.preload_act_table(ACT.Exp)

                        def copy_turned(h, k):
                            act.wait_ge(s_t, k + 2)
                            act.wait_ge(s_q, k)
                            act.copy(into_t[:, h], t_ps[0:WN, h]).then_inc(s_tc, 1)

                        def exps(h, k):
                            act.wait_ge(s_sb, k)
                            act.activation(weighted[:, h, :, F:F + HEADS2], score[:, h], ACT.Exp).then_inc(s_exp, 1)

                        def body(w, g, v, end):
                            k = 2 * v + 1
                            exps(0, k)
                            copy_turned(0, k + 2)
                            exps(1, k + 1)
                            copy_turned(1, k + 3)

                        def after(w, end):
                            act.wait_ge(s_half, 2 * end + 2)
                            act.copy(attn[:, bass.ds(w, 1), :].squeeze(1), acc[0:WN, 0:F + HEADS2]).then_inc(s_free, 1)

                        copy_turned(0, 1)
                        copy_turned(1, 2)
                        loop_windows(act, body, after=after)

                    @block.tensor
                    def _(pe):
                        for s in (s_half, s_t, s_q):
                            pe.sem_inc(s, 2)
                        pe.wait_ge(s_init, 1)

                        def before(w):
                            pe.wait_ge(s_free, w + 1)
                            nc.tensor.matmul(acc[0:WN, 0:P], zeros[:, 0:WN], zeros[:, :], start=True, stop=True)

                        def spread(w, h, k):
                            pe.wait_ge(s_ahead, k)
                            pe.wait_ge(s_tc, k)
                            for j in range(H):
                                last = nc.tensor.transpose(t_ps[0:WN, h, j, :], ahead[:, h, j, :], ident[:, :])
                            last.then_inc(s_t, 1)
                            pe.wait_ge(s_tc, 2 + k)
                            pe.wait_ge(s_prod, k)
                            for j in range(H):
                                last = nc.tensor.matmul(q_ps[:, h, j, 0:F], into_t[:, h, j, :],
                                                        q[:, bass.ds(w, 1), :].squeeze(1), start=True, stop=True)
                            last.then_inc(s_q, 1)

                        def add(h, k):
                            pe.wait_ge(s_m, 2 + k)
                            for j in range(H):
                                last = nc.tensor.matmul(acc[0:WN, 0:F + HEADS2], into[:, h, j, :], weighted[:, h, j, :],
                                                        start=False, stop=True, skip_group_check=True)
                            last.then_inc(s_half, 1)

                        def body(w, g, v, end):
                            k = 2 * v + 1
                            _, w_next = next_window(pe, w, v, end)
                            for h in range(2):
                                add(h, k + h)
                                spread(w_next, h, k + h + 2)

                        spread(0, 0, 1)
                        spread(0, 1, 2)
                        loop_windows(pe, body, before)

            with Phase(nc, "nodes2") as ph:
                rden = ph.sb("rden", [WN, NW, HEADS2])
                y = ph.sb("y", [WN, NW, F])
                tmp = ph.sb("tmp", [WN, NW, F])
                s_ch, s_ch2 = ph.sem("s_ch"), ph.sem("s_ch2")
                with nc.Block() as block:

                    @block.vector
                    def _(dve):
                        step = Chain(dve, s_ch)
                        step(dve.tensor_scalar(rden[:, :, :], attn[:, :, F:F + HEADS2], TINY, None, ALU.max))
                        step(dve.reciprocal(rden[:, :, :], rden[:, :, :]))
                        for h in range(HEADS2):
                            part = attn[:, :, h * DK:(h + 1) * DK]
                            step(dve.tensor_tensor(part, part, over(rden[:, :, h], DK), ALU.mult))

                node_linear(nc, "wo", attn, [(0, F)], lambda k: w_sq[:, 3, :], F, b_sq[:, 3, :], y)
                norm = Norm(ph, "norm", stat, minus_half)
                with nc.Block() as block:

                    @block.gpsimd
                    def _(pool):
                        norm.on_gpsimd(pool)

                    @block.vector
                    def _(dve):
                        step = Chain(dve, s_ch2)
                        step(dve.tensor_tensor(y[:, :, :], y[:, :, :], x[:, :, :], ALU.add))
                        norm.on_vector(step, dve, y[:, :, :], x[:, :, :], tmp[:, :, :])

        with Phase(nc, "last") as ph:
            counts_sb = ph.sb("counts_sb", [WN, NW, N], BF16)
            parts = ph.sb("parts", [WN, NW, 3, F], BF16)
            y = ph.sb("y", [WN, NW, F])
            tmp = ph.sb("tmp", [WN, NW, F])
            sums = ph.sb("sums", [WN, NW, F])
            s_ct, s_ch, s_ch2, s_out = ph.sem("s_ct"), ph.sem("s_ch"), ph.sem("s_ch2"), ph.sem("s_out")
            with nc.Block() as block:

                @block.sync
                def _(sp):
                    for w in range(NW):
                        sp.dma_start(counts_sb[:, w, :], counts_t[w]).then_inc(s_ct, 16)
                    sp.dma_start(sums[:, :, :], edge_sum).then_inc(s_ct, 16)
                    sp.wait_ge(s_ct, 16 * NW + 16)

                @block.vector
                def _(dve):
                    step = Chain(dve, s_ch)
                    split3(step, dve, parts, y[:, :, :], x[:, :, :])

            dense_sum("neighbours", counts_sb, parts, y)
            s_res = ph.sem("s_res")
            norm = Norm(ph, "norm", stat, minus_half)
            with nc.Block() as block:

                @block.gpsimd
                def _(pool):
                    norm.on_gpsimd(pool)

                @block.vector
                def _(dve):
                    step = Chain(dve, s_ch2)
                    step(dve.tensor_tensor(y[:, :, :], y[:, :, :], sums[:, :, :], ALU.add))
                    step(dve.tensor_tensor(tmp[:, :, :], x[:, :, :], over(deg[:, :], F), ALU.mult))
                    step(dve.tensor_tensor(y[:, :, :], y[:, :, :], tmp[:, :, :], ALU.add))
                    step(dve.tensor_tensor(y[:, :, :], y[:, :, :], x[:, :, :], ALU.add))
                    norm.on_vector(step, dve, y[:, :, :], x[:, :, :], tmp[:, :, :])
                    dve.sem_inc(s_res, 1)

                @block.sync
                def _(sp):
                    sp.wait_ge(s_res, 1)
                    with nc.allow_non_contiguous_dma("rows"):
                        sp.dma_start(out.rearrange("(w p) f -> p w f", p=WN), x[:, :, :]).then_inc(s_out, 16)
                    sp.wait_ge(s_out, 16)


def kernel(**inputs):
    import numpy as np
    import concourse.bacc as bacc
    from concourse.bass_utils import run_bass_kernel_spmd

    nc = bacc.Bacc("TRN2", target_bir_lowering=False, num_devices=1)
    arrays, args = {}, {}
    for name in inputs:
        if name == "edge_attr_3":
            continue
        arr = np.ascontiguousarray(inputs[name])
        if arr.ndim == 0:
            arr = arr.reshape(1)
        arrays["in_" + name] = arr
        args[name] = nc.dram_tensor("in_" + name, arr.shape, mybir.dt.from_np(arr.dtype), kind="ExternalInput").ap()
    out = nc.dram_tensor("out", (N, F), F32, kind="ExternalOutput").ap()
    build(nc, args, out)
    got = run_bass_kernel_spmd(nc, [arrays], core_ids=[0])
    return got.results[0]["out"]
```

```python
import concourse.bass as bass
from concourse import mybir
from contextlib import ExitStack, contextmanager

F32 = mybir.dt.float32
BF16 = mybir.dt.bfloat16
F16 = mybir.dt.float16
I32 = mybir.dt.int32
ALU = mybir.AluOpType
ACT = mybir.ActivationFunctionType
AX = mybir.AxisListType.X
RMAX = bass.bass_isa.ReduceOp.max

P = 128
N, E, F = 3125, 103125, 64
WN = 125
NW = N // WN
T = 8
H = 4
GE = P * T
NG = -(-E // GE)
LAST = E - GE
DUP = NG * GE - E
HEADS0, HEADS2, DK = 4, 8, 8
A0 = 2 * HEADS0
ROW0 = HEADS0 * F + HEADS0
ED = 32
U = 5
Q, QN = 4, 32
TILES = -(-E // P)
TAIL0 = TILES * P - E
CH = -(-TILES // P)
STEP = 2
MIN_TURNS = 5
TURN_BIT, TILE_BIT = 14, 10
assert TILES % STEP == 0 and NW * TILES // STEP < 1 << TURN_BIT and TILES < 1 << TILE_BIT
CUM_BIT, END_BIT = 7, 19
assert NG < 1 << CUM_BIT and NW * NG < 1 << (END_BIT - CUM_BIT)
TINY = 1e-30
WIDEST = 60.0
SMALLEST = 1e-20
MOST_EXACT = 256.0
EPS = 1e-5
BANK = 512


class Phase:

    def __init__(self, nc, name):
        self.nc, self.name, self.ctx, self.sems = nc, name, ExitStack(), []

    def __enter__(self):
        self.ctx.__enter__()
        return self

    def __exit__(self, *a):
        done = self.ctx.__exit__(*a)
        if self.sems and a[0] is None:
            self.nc.clear_and_free_semaphores(self.sems)
            self.nc.all_engine_barrier()
        return done

    def sb(self, name, shape, dt=F32):
        return self.ctx.enter_context(self.nc.sbuf_tensor(f"{self.name}_{name}", shape, dt))

    def ps(self, name, shape, dt=F32):
        return self.ctx.enter_context(self.nc.psum_tensor(f"{self.name}_{name}", shape, dt))

    def sem(self, name):
        self.sems.append(self.nc.alloc_semaphore(f"{self.name}_{name}"))
        return self.sems[-1]



class Chain:

    def __init__(self, eng, sem, base=0):
        self.eng, self.sem, self.n, self.base = eng, sem, 0, base

    def __call__(self, ins):
        ins.then_inc(self.sem, 1)
        self.n += 1
        self.eng.wait_ge(self.sem, self.base + self.n)
        return ins


def grouped(a):
    return a[0:(NG - 1) * GE].rearrange("(g p j) -> p g j", p=P, j=T)


def node_linear(nc, tag, src, chunks, weights, fout, bias, dst, scale=None):
    with Phase(nc, tag) as ph:
        nk = len(chunks)
        width = max(c for _, c in chunks)
        fin = sum(c for _, c in chunks)
        turns = NW // U
        staged = ph.sb("staged", [WN, U, fin])
        turned = ph.sb("turned", [P, U, nk, P])
        turned_ps = ph.ps("turned_ps", [P, 8, nk, P])
        out_ps = ph.ps("out_ps", [WN, 6, 256])
        s_go = ph.sem("s_go")
        s_staged, s_turned_ps, s_turned, s_out_ps, s_out = (
            ph.sem(n) for n in ("s_staged", "s_turned_ps", "s_turned", "s_out_ps", "s_out"))
        block = ph.ctx.enter_context(nc.Block())

        @block.gpsimd
        def _(pool):
            with pool.Fori(0, turns) as i:
                pool.wait_ge(s_turned_ps, i + 1)
                pool.tensor_copy(staged[:, :, :], src[:, bass.ds(i * U, U), 0:fin]).then_inc(s_staged, 1)

        @block.tensor
        def _(pe):
            pe.sem_inc(s_turned_ps, 1)
            with pe.Fori(0, turns) as i:
                pe.wait_ge(s_staged, i + 1)
                pe.wait_ge(s_turned, i + 1)
                pe.sem_inc(s_go, 1)
                for u in range(U):
                    for k, (c0, cw) in enumerate(chunks):
                        last = nc.tensor.transpose(turned_ps[0:cw, u, k, 0:WN], staged[:, u, c0:c0 + cw],
                                                   nc_ident(nc)[0:WN, 0:WN])
                last.then_inc(s_turned_ps, 1)
                pe.wait_ge(s_turned, i + 2)
                pe.wait_ge(s_out, i + 1)
                for u in range(U):
                    for k, (c0, cw) in enumerate(chunks):
                        last = nc.tensor.matmul(out_ps[:, u, 0:fout], turned[0:cw, u, k, 0:WN], weights(k),
                                                start=(k == 0), stop=(k == nk - 1))
                last.then_inc(s_out_ps, 1)

        @block.scalar
        def _(act):
            act.sem_inc(s_turned, 1)
            act.sem_inc(s_out_ps, 1)
            with act.Fori(0, turns) as i:
                act.wait_ge(s_turned_ps, i + 2)
                act.wait_ge(s_out_ps, i + 1)
                act.copy(turned[0:width, :, :, 0:WN], turned_ps[0:width, 0:U, :, 0:WN]).then_inc(s_turned, 1)

        @block.vector
        def _(dve):
            dve.sem_inc(s_out, 1)
            with dve.Fori(0, turns) as i:
                dve.wait_ge(s_out_ps, i + 2)
                to, by = dst[:, bass.ds(i * U, U), 0:fout], 1.0 if scale is None else scale
                if bias is None:
                    dve.tensor_scalar(to, out_ps[:, 0:U, 0:fout], by, None, ALU.mult).then_inc(s_out, 1)
                else:
                    dve.scalar_tensor_tensor(to, out_ps[:, 0:U, 0:fout], by,
                                             bias.unsqueeze(1).broadcast_to([WN, U, fout]),
                                             ALU.mult, ALU.add).then_inc(s_out, 1)


_IDENT = {}


def nc_ident(nc):
    return _IDENT["ident"]


def over(ap, n):
    return ap.unsqueeze(2).broadcast_to([ap.shape[0], ap.shape[1], n])


class Norm:

    def __init__(self, ph, name, stat, minus_half):
        self.stat, self.minus_half = stat, minus_half
        self.s_var, self.s_rstd = ph.sem(f"{name}_s_var"), ph.sem(f"{name}_s_rstd")

    def on_gpsimd(self, pool):
        pool.wait_ge(self.s_var, 1)
        pool.tensor_tensor(self.stat[:, 0, :], self.stat[:, 1, :], self.minus_half[0:WN, 0:NW], ALU.pow).then_inc(self.s_rstd, 1)

    def on_vector(self, step, dve, y, out, tmp):
        stat = self.stat
        step(dve.tensor_reduce(stat[:, 0, :], y, AX, ALU.add))
        step(dve.tensor_scalar(stat[:, 1, :], stat[:, 0, :], 1.0 / F, None, ALU.mult))
        step(dve.tensor_tensor(y, y, over(stat[:, 1, :], F), ALU.subtract))
        step(dve.tensor_tensor(tmp, y, y, ALU.mult))
        step(dve.tensor_reduce(stat[:, 0, :], tmp, AX, ALU.add))
        dve.tensor_scalar(stat[:, 1, :], stat[:, 0, :], 1.0 / F, EPS, ALU.mult, ALU.add).then_inc(self.s_var, 1)
        dve.wait_ge(self.s_rstd, 1)
        step(dve.tensor_tensor(out, y, over(stat[:, 0, :], F), ALU.mult))


def build(nc, a, out):
    with Phase(nc, "all") as whole:
        sb, sem = whole.sb, whole.sem
        table0 = nc.dram_tensor("table0", [N, ROW0], F32).ap()
        table_kv = nc.dram_tensor("table_kv", [N, 2 * F], F32).ap()
        edge_sum = nc.dram_tensor("edge_sum", [WN, NW, F], F32).ap()
        counts_t = nc.dram_tensor("counts_t", [NW + 1, WN, NW * WN], BF16).ap()
        logits_kept = nc.dram_tensor("logits_kept", [N, A0], F32).ap()
        table_h = nc.dram_tensor("table_h", [N, F], F32).ap()
        table_q = nc.dram_tensor("table_q", [N, F], F32).ap()
        bias_kept = nc.dram_tensor("bias_kept", [P, NG * T * HEADS2], F32).ap()

        ident = sb("ident", [P, P])
        _IDENT["ident"] = ident
        ident16 = sb("ident16", [P, P], BF16)
        iota_n = sb("iota_n", [P, WN])
        window_start = sb("window_start", [P, NW + 1])
        x = sb("x", [WN, NW, F])
        src_i = sb("src_i", [P, NG, T], I32)
        dst_f = sb("dst_f", [P, NG, T])
        visits = sb("visits", [P, 4, NW + 1], I32)
        turns_of = sb("turns_of", [P, 3, NW], I32)
        deg = sb("deg", [WN, NW])
        flags = sb("flags", [P, 3], I32)
        wide0 = sb("wide0", [P, 1])
        stat = sb("stat", [WN, 2, NW])
        minus_half = sb("minus_half", [P, NW])
        half = sb("half", [P, HEADS2])

        def in_range(v, lo, hi, why):
            return nc.s_assert_within(v, lo, hi, skip_runtime_bounds_check_because=why)

        def loop_windows(eng, body, before=None, after=None, again=None):
            with eng.Fori(0, NW) as w:
                code = eng.value_load(visits[0:1, 0, bass.ds(w, 1)], min_val=0, max_val=(1 << 31) - 1)
                why = "packed so by the first stage"
                lo = in_range(eng.snap(code & ((1 << CUM_BIT) - 1)), 0, NG - 1, why)
                cum = in_range(eng.snap((code >> CUM_BIT) & ((1 << (END_BIT - CUM_BIT)) - 1)), 0, NW * NG, why)
                end = in_range(eng.snap(code >> END_BIT), 1, NW * NG, why)
                if before:
                    before(w)
                with eng.Fori(cum, end) as v:
                    body(w, in_range(eng.snap(v - cum + lo), 0, NG - 1, "visits go to groups that exist"), v, end)
                if again:
                    with eng.Fori(cum, end) as v:
                        again(w, in_range(eng.snap(v - cum + lo), 0, NG - 1, "visits go to groups that exist"), v, end)
                if after:
                    after(w, end)

        def loop_strips(eng, body, before=None, after=None, turn0=None):
            with eng.Fori(0, NW) as w:
                code = [eng.value_load(turns_of[0:1, n, bass.ds(w, 1)], min_val=0, max_val=(1 << 31) - 1) for n in range(3)]
                why, ones = "packed so by the first stage", (1 << TILE_BIT) - 1
                cum = in_range(eng.snap(code[0] & ((1 << TURN_BIT) - 1)), 0, NW * TILES // STEP, why)
                end = in_range(eng.snap(code[0] >> TURN_BIT), 1, NW * TILES // STEP, why)
                lo = [eng.snap(code[1] & ones), eng.snap((code[1] >> TILE_BIT) & ones),
                      eng.snap(code[1] >> 2 * TILE_BIT), code[2]]
                if turn0 is not None:
                    turn0[0] = cum
                if before:
                    before(w)
                with eng.Fori(cum, end) as v:
                    done = eng.snap(STEP * (v - cum))

                    def tile(q, h):
                        return in_range(eng.snap(lo[q] + done + h), 0, TILES - 1, "strips stay within the tiles")

                    body(w, tile, v)
                if after:
                    after(w, end)

        def edge_sums(tag, table, weights, out):
            with Phase(nc, tag) as ph:
                width = F if weights is None else A0 * F + A0
                idx = ph.sb("idx", [P, 1], I32)
                rows = ph.sb("rows", [P, F])
                rel = ph.sb("rel", [P, 1])
                into = ph.sb("into", [P, WN])
                values = ph.sb("values", [P, A0 * F + A0])
                zeros = ph.sb("zeros", [P, BANK])
                acc = ph.ps("acc", [P, 2 * BANK])
                s_zero, s_used, s_idx, s_seen, s_rows, s_steps, s_ready, s_free = (
                    ph.sem(n) for n in ("s_zero", "s_used", "s_idx", "s_seen", "s_rows", "s_steps", "s_ready", "s_free"))
                with nc.Block() as block:

                    @block.gpsimd
                    def _(pool):
                        def body(w, g, v, end):
                            for j in range(T):
                                pool.wait_ge(s_used, v * T + j + 1)
                                pool.sem_inc(s_seen, 1)
                                pool.tensor_copy(idx[:, :], src_i[:, bass.ds(g, 1), j:j + 1].squeeze(1)).then_inc(s_idx, 1)
                                pool.wait_ge(s_idx, v * T + j + 1)
                                pool.sem_inc(s_seen, 1)
                                pool.indirect_dma_start(rows[:, :], None, table,
                                                        bass.IndirectOffsetOnAxis(ap=idx[:, 0:1], axis=0)).then_inc(s_rows, 16)

                        loop_windows(pool, body)

                    @block.vector
                    def _(dve):
                        dve.memset(zeros[:, :], 0.0).then_inc(s_zero, 1)

                        def body(w, g, v, end):
                            for j in range(T):
                                steps = 3 if weights is None else 4
                                n = steps * (v * T + j)
                                dve.wait_ge(s_rows, 16 * (v * T + j + 1))
                                dve.tensor_scalar(rel[:, :], dst_f[:, bass.ds(g, 1), j:j + 1].squeeze(1),
                                                  window_start[:, bass.ds(w, 1)], None, ALU.subtract).then_inc(s_steps, 1)
                                dve.wait_ge(s_steps, n + 1)
                                dve.tensor_scalar(into[:, :], iota_n[:, :], rel[:, 0:1], None, ALU.is_equal).then_inc(s_steps, 1)
                                if weights is None:
                                    dve.tensor_copy(values[:, 0:F], rows[:, :]).then_inc(s_steps, 1)
                                else:
                                    of = weights[:, bass.ds(g, 1), j, :].squeeze(1)
                                    dve.tensor_copy(values[:, A0 * F:width], of).then_inc(s_steps, 1)
                                    dve.tensor_tensor(values[:, 0:A0 * F].rearrange("p (h f) -> p h f", f=F),
                                                      rows[:, :].unsqueeze(1).broadcast_to([P, A0, F]), over(of, F),
                                                      ALU.mult).then_inc(s_steps, 1)
                                dve.wait_ge(s_steps, n + steps)
                                dve.sem_inc(s_ready, 1)

                        def after(w, end):
                            dve.wait_ge(s_used, T * end + 1)
                            dve.tensor_copy(out[:, bass.ds(w, 1), 0:width].squeeze(1), acc[0:WN, 0:width]).then_inc(s_free, 1)

                        loop_windows(dve, body, after=after)

                    @block.tensor
                    def _(pe):
                        pe.sem_inc(s_used, 1)
                        pe.sem_inc(s_free, 1)
                        pe.wait_ge(s_zero, 1)

                        def before(w):
                            pe.wait_ge(s_free, w + 1)
                            for b in range(2):
                                nc.tensor.matmul(acc[:, b * BANK:(b + 1) * BANK], zeros[:, 0:P], zeros[:, :], start=True, stop=True)

                        def body(w, g, v, end):
                            for j in range(T):
                                pe.wait_ge(s_ready, v * T + j + 1)
                                for c in range(0, width, BANK):
                                    last = nc.tensor.matmul(acc[0:WN, c:min(c + BANK, width)], into[:, :],
                                                            values[:, c:min(c + BANK, width)], start=False, stop=True,
                                                            skip_group_check=True)
                                last.then_inc(s_used, 1)

                        loop_windows(pe, body, before)

        def subtract_largest(tag, scores, target):
            with Phase(nc, tag) as ph:
                rel = ph.sb("rel", [P, 1])
                into = ph.sb("into", [P, WN])
                spread_out = ph.sb("spread_out", [P, A0, WN])
                tops = ph.sb("tops", [P, A0, WN])
                largest = ph.sb("largest", [P, A0, WN])
                shift = ph.sb("shift", [P, A0])
                score = ph.sb("score", [P, A0])
                s_steps, s_low, s_top, s_steps2, s_seen, s_matched = (
                    ph.sem(n) for n in ("s_steps", "s_low", "s_top", "s_steps2", "s_seen", "s_matched"))

                def match(dve, w, g, j, sem, n):
                    dve.tensor_scalar(rel[:, :], dst_f[:, bass.ds(g, 1), j:j + 1].squeeze(1),
                                      window_start[:, bass.ds(w, 1)], None, ALU.subtract).then_inc(sem, 1)
                    dve.wait_ge(sem, n)
                    dve.tensor_scalar(into[:, :], iota_n[:, :], rel[:, 0:1], None, ALU.is_equal).then_inc(sem, 1)
                    dve.wait_ge(sem, n + 1)

                with nc.Block() as block:

                    @block.gpsimd
                    def _(pool):
                        def body(w, g, v, end):
                            for j in range(T):
                                pool.wait_ge(s_low, v * T + j + 1)
                                pool.sem_inc(s_seen, 1)
                                pool.partition_all_reduce(tops[:, :, :].rearrange("p h n -> p (h n)"),
                                                          spread_out[:, :, :].rearrange("p h n -> p (h n)"), P, RMAX).then_inc(s_top, 1)

                        loop_windows(pool, body)

                    @block.vector
                    def _(dve):
                        def before(w):
                            dve.memset(largest[:, :, :], -3e38)

                        def body(w, g, v, end):
                            for j in range(T):
                                n = 4 * (v * T + j)
                                dve.memset(spread_out[:, :, :], -3e38)
                                dve.tensor_copy(score[:, :], scores[:, bass.ds(g, 1), j, :].squeeze(1))
                                match(dve, w, g, j, s_steps, n + 1)
                                dve.sem_inc(s_matched, 1)
                                dve.copy_predicated(spread_out[:, :, :], into[:, :].bitcast(I32).unsqueeze(1).broadcast_to([P, A0, WN]),
                                                    over(score[:, :], WN)).then_inc(s_steps, 1)
                                dve.wait_ge(s_steps, n + 3)
                                dve.sem_inc(s_low, 1)
                                dve.wait_ge(s_top, v * T + j + 1)
                                dve.tensor_tensor(largest[:, :, :], largest[:, :, :], tops[:, :, :], ALU.max).then_inc(s_steps, 1)
                                dve.wait_ge(s_steps, n + 4)

                        def again(w, g, v, end):
                            for j in range(T):
                                n = 5 * (v * T + j)
                                match(dve, w, g, j, s_steps2, n + 1)
                                dve.tensor_tensor(spread_out[:, :, :], largest[:, :, :], into[:, :].unsqueeze(1).broadcast_to([P, A0, WN]),
                                                  ALU.mult).then_inc(s_steps2, 1)
                                dve.wait_ge(s_steps2, n + 3)
                                dve.tensor_reduce(shift[:, :], spread_out[:, :, :], AX, ALU.add).then_inc(s_steps2, 1)
                                dve.wait_ge(s_steps2, n + 4)
                                of = target[:, bass.ds(g, 1), j, :].squeeze(1)
                                dve.tensor_tensor(of, of, shift[:, :], ALU.subtract).then_inc(s_steps2, 1)
                                dve.wait_ge(s_steps2, n + 5)

                        loop_windows(dve, body, before, again=again)

        with Phase(nc, "plan") as ph:
            dst_i = ph.sb("dst_i", [P, NG, T], I32)
            ramp = ph.sb("ramp", [P, NG * 2], I32)
            ramp_f = ph.sb("ramp_f", [P, NG * 2])
            dup = ph.sb("dup", [P, 3, T])
            ends = ph.sb("ends", [P, 2, NG])
            ends_all = ph.sb("ends_all", [P, 2, NG])
            touch = ph.sb("touch", [P, 3, NW, NG])
            wf = ph.sb("wf", [P, 6, NW])
            ones = ph.sb("ones", [P, NW])
            s_ld, s_pool, s_ch = ph.sem("s_ld"), ph.sem("s_pool"), ph.sem("s_ch")
            s_ends = ph.sem("s_ends")
            s_all = ph.sem("s_all")
            block = ph.ctx.enter_context(nc.Block())

            @block.sync
            def _(sp):
                with nc.allow_non_contiguous_dma("runs of eight edges"):
                    for to, fro in ((src_i, a["src"]), (dst_i, a["dst"])):
                        sp.dma_start(to[:, 0:NG - 1, :], grouped(fro)).then_inc(s_ld, 16)
                        sp.dma_start(to[:, NG - 1, :], fro[LAST:E].rearrange("(p j) -> p j", j=T)).then_inc(s_ld, 16)
                    sp.dma_start(x[:, :, :], a["x"].rearrange("(w p) f -> p w f", p=WN)).then_inc(s_ld, 16)
                sp.wait_ge(s_ld, 80)

            @block.gpsimd
            def _(pool):
                step = Chain(pool, s_pool)
                step(pool.memset(ident[:, :], 0.0))
                step(pool.affine_select(out=ident[:, :], in_=ident[:, :], compare_op=ALU.not_equal, fill=1.0,
                                        base=0, pattern=[[-1, P]], channel_multiplier=1))
                step(pool.tensor_copy(ident16[:, :], ident[:, :]))
                step(pool.iota(ramp[:, :], [[1, 2 * NG]], base=0, channel_multiplier=0))
                step(pool.tensor_copy(ramp_f[:, :], ramp[:, :]))
                step(pool.tensor_copy(iota_n[:, :], ramp_f[:, 0:WN]))
                step(pool.tensor_scalar(window_start[:, :], ramp_f[:, 0:NW + 1], float(WN), None, ALU.mult))
                step(pool.iota(ramp[:, 0:T], [[1, T]], base=0, channel_multiplier=T))
                step(pool.tensor_copy(dup[:, 0, :], ramp[:, 0:T]))
                pool.memset(minus_half[:, :], -0.5)
                pool.memset(half[:, :], 0.5)
                pool.wait_ge(s_ends, 1)
                pool.partition_all_reduce(ends_all[:, :, :].rearrange("p a g -> p (a g)"),
                                          ends[:, :, :].rearrange("p a g -> p (a g)"), P, RMAX).then_inc(s_all, 1)

            @block.vector
            def _(dve):
                step = Chain(dve, s_ch)
                dve.wait_ge(s_ld, 80)
                dve.wait_ge(s_pool, 9)
                step(dve.memset(ones[:, :], 1.0))
                step(dve.tensor_copy(dst_f[:, :, :], dst_i[:, :, :]))
                last = dst_f[:, NG - 1, :]
                step(dve.tensor_scalar(dup[:, 1, :], dup[:, 0, :], float(DUP), None, ALU.is_ge))
                step(dve.tensor_scalar(last, last, 1.0, None, ALU.add))
                step(dve.tensor_tensor(last, last, dup[:, 1, :], ALU.mult))
                step(dve.tensor_scalar(last, last, -1.0, None, ALU.add))
                step(dve.tensor_reduce(ends[:, 0, :], dst_f[:, :, :], AX, ALU.max))
                step(dve.tensor_reduce(ends[:, 1, :], dst_f[:, :, :], AX, ALU.min))
                step(dve.tensor_scalar(dup[:, 2, :], dup[:, 1, :], -2.0 * N, 2.0 * N, ALU.mult, ALU.add))
                step(dve.tensor_tensor(dup[:, 2, :], dup[:, 2, :], last, ALU.add))
                step(dve.tensor_reduce(ends[:, 1, NG - 1:NG], dup[:, 2, :], AX, ALU.min))
                dve.tensor_scalar(ends[:, 1, :], ends[:, 1, :], -1.0, None, ALU.mult).then_inc(s_ends, 1)
                dve.wait_ge(s_all, 1)
                step(dve.tensor_scalar(ends[:, 1, :], ends_all[:, 1, :], -1.0, None, ALU.mult))
                step(dve.tensor_scalar(wf[:, 5, :], window_start[:, 0:NW], float(WN - 1), None, ALU.add))

                def by_window(ap):
                    return ap.unsqueeze(1).broadcast_to([P, NW, NG])

                step(dve.tensor_tensor(touch[:, 0], by_window(ends_all[:, 0, :]), over(window_start[:, 0:NW], NG), ALU.is_ge))
                step(dve.tensor_tensor(touch[:, 1], by_window(ends[:, 1, :]), over(wf[:, 5, :], NG), ALU.is_le))
                step(dve.tensor_tensor(touch[:, 0], touch[:, 0], touch[:, 1], ALU.mult))
                step(dve.tensor_tensor(touch[:, 1], touch[:, 0], by_window(ramp_f[:, 1:NG + 1]), ALU.mult))
                step(dve.tensor_reduce(wf[:, 0, :], touch[:, 1], AX, ALU.max))
                step(dve.tensor_scalar(wf[:, 0, :], wf[:, 0, :], 1.0, None, ALU.max))
                step(dve.tensor_scalar(ends[:, 0, :], ramp_f[:, 0:NG], -1.0, float(NG), ALU.mult, ALU.add))
                step(dve.tensor_tensor(touch[:, 1], touch[:, 0], by_window(ends[:, 0, :]), ALU.mult))
                step(dve.tensor_reduce(wf[:, 1, :], touch[:, 1], AX, ALU.max))
                step(dve.tensor_scalar(wf[:, 1, :], wf[:, 1, :], -1.0, float(NG), ALU.mult, ALU.add))
                step(dve.tensor_scalar(wf[:, 2, :], wf[:, 0, :], -1.0, None, ALU.add))
                step(dve.tensor_tensor(wf[:, 1, :], wf[:, 1, :], wf[:, 2, :], ALU.min))
                step(dve.tensor_tensor(wf[:, 2, :], wf[:, 0, :], wf[:, 1, :], ALU.subtract))
                step(dve.tensor_tensor_scan(wf[:, 3, :], ones[:, :], wf[:, 2, :], 0.0, ALU.mult, ALU.add))
                step(dve.tensor_tensor(wf[:, 3, :], wf[:, 3, :], wf[:, 2, :], ALU.subtract))
                step(dve.tensor_tensor(wf[:, 2, :], wf[:, 3, :], wf[:, 2, :], ALU.add))
                step(dve.memset(visits[:, :, :], 0))
                step(dve.tensor_copy(visits[:, 1:4, 0:NW], wf[:, 1:4, :]))
                step(dve.tensor_scalar(visits[:, 2, :], visits[:, 2, :], END_BIT, None, ALU.logical_shift_left))
                step(dve.tensor_scalar(visits[:, 3, :], visits[:, 3, :], CUM_BIT, None, ALU.logical_shift_left))
                step(dve.tensor_tensor(visits[:, 2, :], visits[:, 2, :], visits[:, 3, :], ALU.bitwise_or))
                step(dve.tensor_tensor(visits[:, 0, :], visits[:, 1, :], visits[:, 2, :], ALU.bitwise_or))

        with Phase(nc, "first") as first:
            edge = first.sb("edge", [P, TILES, 4])
            factor_r = first.sb("factor_r", [WN, NW, HEADS0])
            factor_t = first.sb("factor_t", [WN, NW, HEADS0])
            bias = first.sb("bias", [P, NG + 1, T * HEADS2])
            with Phase(nc, "tiles") as ph:
                lens = ph.sb("lens", [P, TILES])
                with Phase(nc, "strips") as pt:
                    FULL = TILES // P * P
                    REST = TILES - FULL - 1
                    row_i = pt.sb("row_i", [P, 2, CH, P], I32)
                    row = pt.sb("row", [P, 3, CH, P])
                    late = pt.sb("late", [P, CH, P])
                    strip = pt.sb("strip", [P, 4, NW * Q])
                    ramp_i = pt.sb("ramp_i", [P, NW * Q], I32)
                    tile_i = pt.sb("tile_i", [P, CH], I32)
                    tile_f = pt.sb("tile_f", [P, 2, CH])
                    ends = pt.sb("ends", [P, 2, CH])
                    touch = pt.sb("touch", [P, 3, CH, NW * Q])
                    reach = pt.sb("reach", [P, 2, NW * Q])
                    reach_all = pt.sb("reach_all", [P, 2, NW * Q])
                    wf = pt.sb("wf", [P, 6, NW])
                    wi = pt.sb("wi", [P, 2, NW], I32)
                    lo_i = pt.sb("lo_i", [P, NW * Q], I32)
                    turn_ps = pt.ps("turn_ps", [P, 3, 2 * BANK])
                    s_zero, s_ld, s_pool, s_ch, s_f, s_turned, s_reach, s_all, s_copied = (
                        pt.sem(n) for n in ("s_zero", "s_ld", "s_pool", "s_ch", "s_floats", "s_turned", "s_reach", "s_all", "s_copied"))
                    with nc.Block() as block:

                        @block.sync
                        def _(sp):
                            sp.wait_ge(s_zero, 3)
                            for to, fro in ((row_i[:, 0], a["src"]), (row_i[:, 1], a["dst"]), (row[:, 2], a["edge_weight"])):
                                sp.dma_start(to[:, 0:CH - 1, :],
                                             fro[0:FULL * P].rearrange("(c r i) -> r c i", r=P, i=P)).then_inc(s_ld, 16)
                                sp.dma_start(to[0:REST, CH - 1, :],
                                             fro[FULL * P:(TILES - 1) * P].rearrange("(r i) -> r i", i=P)).then_inc(s_ld, 16)
                                sp.dma_start(to[REST:REST + 1, CH - 1, TAIL0:P],
                                             fro[(TILES - 1) * P:E].rearrange("(r i) -> r i", r=1)).then_inc(s_ld, 16)
                            sp.wait_ge(s_ld, 144)

                        @block.gpsimd
                        def _(pool):
                            step = Chain(pool, s_pool)
                            step(pool.iota(ramp_i[:, :], [[WN, NW], [QN, Q]], base=0, channel_multiplier=0))
                            step(pool.tensor_copy(strip[:, 0, :], ramp_i[:, :]))
                            step(pool.iota(tile_i[:, :], [[P, CH]], base=1, channel_multiplier=1))
                            step(pool.tensor_copy(tile_f[:, 0, :], tile_i[:, :]))
                            pool.wait_ge(s_reach, 1)
                            pool.partition_all_reduce(reach_all[:, :, :].rearrange("p a w -> p (a w)"),
                                                      reach[:, :, :].rearrange("p a w -> p (a w)"), P, RMAX).then_inc(s_all, 1)

                        @block.vector
                        def _(dve):
                            dve.memset(row_i[:, 0], 0).then_inc(s_zero, 1)
                            dve.memset(row_i[:, 1], -1).then_inc(s_zero, 1)
                            dve.memset(row[:, 2], 0.0).then_inc(s_zero, 1)
                            step = Chain(dve, s_ch)
                            dve.wait_ge(s_ld, 144)
                            dve.tensor_copy(row[:, 0:2], row_i[:, :, :, :]).then_inc(s_f, 1)
                            dve.wait_ge(s_f, 1)
                            step(dve.tensor_reduce(ends[:, 0, :], row[:, 1], AX, ALU.max))
                            step(dve.tensor_scalar(late[:, :, :], row[:, 1], 0.0, 4.0 * N, ALU.is_lt, ALU.mult))
                            step(dve.tensor_tensor(late[:, :, :], late[:, :, :], row[:, 1], ALU.add))
                            step(dve.tensor_reduce(ends[:, 1, :], late[:, :, :], AX, ALU.min))
                            dve.wait_ge(s_pool, 4)
                            step(dve.tensor_scalar(strip[:, 1, :], strip[:, 0, :], float(QN - 1), None, ALU.add))
                            step(dve.tensor_scalar(tile_f[:, 1, :], tile_f[:, 0, :], -1.0, float(TILES + 1), ALU.mult, ALU.add))

                            def by_tile(ap):
                                return ap.unsqueeze(1).broadcast_to([P, CH, NW * Q])

                            step(dve.tensor_tensor(touch[:, 0], over(ends[:, 0, :], NW * Q), by_tile(strip[:, 0, :]), ALU.is_ge))
                            step(dve.tensor_tensor(touch[:, 1], over(ends[:, 1, :], NW * Q), by_tile(strip[:, 1, :]), ALU.is_le))
                            step(dve.tensor_tensor(touch[:, 0], touch[:, 0], touch[:, 1], ALU.mult))
                            for n in range(2):
                                step(dve.tensor_tensor(touch[:, 1 + n], touch[:, 0], over(tile_f[:, n, :], NW * Q), ALU.mult))
                            step(dve.tensor_reduce(reach[:, 0, :], touch[:, 1].rearrange("p c w -> p w c"), AX, ALU.max))
                            dve.tensor_reduce(reach[:, 1, :], touch[:, 2].rearrange("p c w -> p w c"), AX, ALU.max).then_inc(s_reach, 1)
                            dve.wait_ge(s_all, 1)
                            lo = strip[:, 2, :]
                            step(dve.tensor_scalar(lo, reach_all[:, 1, :], -1.0, float(TILES), ALU.mult, ALU.add))
                            step(dve.tensor_tensor(strip[:, 3, :], reach_all[:, 0, :], lo, ALU.subtract))
                            step(dve.tensor_reduce(wf[:, 0, :], strip[:, 3, :].rearrange("p (w q) -> p w q", q=Q), AX, ALU.max))
                            step(dve.tensor_scalar(wf[:, 0, :], wf[:, 0, :], float(STEP * MIN_TURNS), 1.0, ALU.max, ALU.add))
                            step(dve.tensor_copy(wi[:, 0, :], wf[:, 0, :]))
                            step(dve.tensor_scalar(wi[:, 1, :], wi[:, 0, :], 1, None, ALU.logical_shift_right))
                            step(dve.tensor_copy(wf[:, 1, :], wi[:, 1, :]))
                            step(dve.tensor_scalar(wf[:, 2, :], wf[:, 1, :], -float(STEP), float(TILES), ALU.mult, ALU.add))
                            by_strip = lo.rearrange("p (w q) -> p w q", q=Q)
                            step(dve.tensor_tensor(by_strip, by_strip, over(wf[:, 2, :], Q), ALU.min))
                            step(dve.memset(wf[:, 3, :], 1.0))
                            step(dve.tensor_tensor_scan(wf[:, 4, :], wf[:, 3, :], wf[:, 1, :], 0.0, ALU.mult, ALU.add))
                            step(dve.tensor_tensor(wf[:, 5, :], wf[:, 4, :], wf[:, 1, :], ALU.subtract))
                            step(dve.tensor_copy(wi[:, :, :], wf[:, 4:6, :]))
                            step(dve.tensor_scalar(wi[:, 0, :], wi[:, 0, :], TURN_BIT, None, ALU.logical_shift_left))
                            step(dve.tensor_tensor(turns_of[:, 0, :], wi[:, 0, :], wi[:, 1, :], ALU.bitwise_or))
                            step(dve.tensor_copy(lo_i[:, :], lo))
                            los = lo_i[:, :].rearrange("p (w q) -> p q w", q=Q)
                            step(dve.tensor_copy(turns_of[:, 2, :], los[:, 3, :]))
                            for n in (1, 2):
                                step(dve.tensor_scalar(wi[:, 0, :], los[:, n, :], n * TILE_BIT, None, ALU.logical_shift_left))
                                step(dve.tensor_tensor(turns_of[:, 1, :], wi[:, 0, :],
                                                       los[:, 0, :] if n == 1 else turns_of[:, 1, :], ALU.bitwise_or))

                        @block.tensor
                        def _(pe):
                            pe.wait_ge(s_f, 1)
                            for n in range(3):
                                for c in range(CH):
                                    last = nc.tensor.transpose(turn_ps[:, n, c * P:(c + 1) * P], row[:, n, c, :], ident[:, :])
                            last.then_inc(s_turned, 1)

                        @block.scalar
                        def _(act):
                            act.wait_ge(s_turned, 1)
                            act.copy(edge[:, :, 2], turn_ps[:, 0, 0:TILES]).then_inc(s_copied, 1)
                            act.copy(edge[:, :, 0], turn_ps[:, 1, 0:TILES]).then_inc(s_copied, 1)
                            act.copy(lens[:, :], turn_ps[:, 2, 0:TILES]).then_inc(s_copied, 1)

                w_proj = ph.sb("w_proj", [F, HEADS0, F])
                score = ph.sb("score", [F, 2, HEADS0, F])
                prod = ph.sb("prod", [F, HEADS0, F])
                u = ph.sb("u", [F, A0])
                neg_c = ph.sb("neg_c", [P, 1])
                logits = ph.sb("logits", [WN, NW, A0])
                top = ph.sb("top", [P, 2, A0 + 1])
                top_all = ph.sb("top_all", [P, 2, A0 + 1])
                spread = ph.sb("spread", [P, A0 + 1])
                rows = ph.sb("rows", [WN, NW, ROW0])
                s_ld, s_ch, s_less, s_exp, s_rows = (ph.sem(n) for n in ("s_ld", "s_ch", "s_less", "s_exp", "s_rows"))
                s_top, s_all, s_st, s_neg = ph.sem("s_top"), ph.sem("s_all"), ph.sem("s_st"), ph.sem("s_neg")
                with nc.Block() as block:

                    @block.sync
                    def _(sp):
                        sp.dma_start(w_proj[:, :, :], a["L0_gnn_w_proj"].rearrange("h f g -> f h g")).then_inc(s_ld, 16)
                        for n, name in enumerate(("L0_gnn_radial_score", "L0_gnn_tangential_score")):
                            sp.dma_start(score[:, n], a[name].partition_broadcast(F)).then_inc(s_ld, 16)
                        sp.dma_start(neg_c[:, :], a["L0_gnn_radial_distance_scale"].partition_broadcast(P)).then_inc(s_ld, 16)
                        sp.wait_ge(s_ld, 64)

                    @block.vector
                    def _(dve):
                        step = Chain(dve, s_ch)
                        dve.wait_ge(s_ld, 64)
                        for n in range(2):
                            step(dve.tensor_tensor(prod[:, :, :], w_proj[:, :, :], score[:, n], ALU.mult))
                            step(dve.tensor_reduce(u[:, n * HEADS0:(n + 1) * HEADS0], prod[:, :, :], AX, ALU.add))
                        step(dve.tensor_scalar(neg_c[:, :], neg_c[:, :], -1.0, None, ALU.mult))
                        step(dve.tensor_scalar(lens[:, :], lens[:, :], neg_c[:, 0:1], None, ALU.mult))
                        step(dve.tensor_scalar(edge[:, :, 3], edge[:, :, 2], -float(N // 2), None, ALU.add))

                node_linear(nc, "l0", x, [(0, F)], lambda k: u[:, :], A0, None, logits)

                with nc.Block() as block:

                    @block.sync
                    def _(sp):
                        sp.wait_ge(s_less, 1)
                        with nc.allow_non_contiguous_dma("table rows"):
                            sp.dma_start(logits_kept.rearrange("(w p) c -> p w c", p=WN), logits[:, :, :]).then_inc(s_st, 16)
                        sp.wait_ge(s_rows, 1)
                        sp.dma_start(table0.rearrange("(w p) c -> p w c", p=WN), rows[:, :, :]).then_inc(s_st, 16)
                        sp.wait_ge(s_st, 32)

                    @block.gpsimd
                    def _(pool):
                        pool.wait_ge(s_top, 1)
                        pool.partition_all_reduce(top_all[:, :, :].rearrange("p a n -> p (a n)"),
                                                  top[:, :, :].rearrange("p a n -> p (a n)"), P, RMAX).then_inc(s_all, 1)

                    @block.vector
                    def _(dve):
                        step = Chain(dve, s_neg)
                        by_head = logits[:, :, :].rearrange("p w h -> p h w")
                        step(dve.memset(top[:, :, :], -3e38))
                        step(dve.tensor_reduce(top[0:WN, 0, 0:A0], by_head, AX, ALU.max))
                        step(dve.tensor_reduce(top[0:WN, 1, 0:A0], by_head, AX, ALU.min))
                        step(dve.tensor_reduce(top[:, 0, A0:A0 + 1], lens[:, :], AX, ALU.max))
                        step(dve.tensor_reduce(top[:, 1, A0:A0 + 1], lens[:, :], AX, ALU.min))
                        step(dve.tensor_scalar(top[0:WN, 1, 0:A0], top[0:WN, 1, 0:A0], -1.0, None, ALU.mult))
                        dve.tensor_scalar(top[:, 1, A0:A0 + 1], top[:, 1, A0:A0 + 1], -1.0, None, ALU.mult).then_inc(s_top, 1)
                        dve.wait_ge(s_all, 1)
                        dve.tensor_tensor(logits[:, :, :], logits[:, :, :],
                                          top_all[0:WN, 0, 0:A0].unsqueeze(1).broadcast_to([WN, NW, A0]), ALU.subtract).then_inc(s_less, 1)
                        dve.tensor_scalar(lens[:, :], lens[:, :], top_all[:, 0, A0:A0 + 1], None, ALU.subtract).then_inc(s_less, 1)
                        step(dve.tensor_tensor(spread[:, :], top_all[:, 0, :], top_all[:, 1, :], ALU.add))
                        step(dve.tensor_scalar(spread[:, 0:HEADS0], spread[:, 0:HEADS0], spread[:, A0:A0 + 1], None, ALU.add))
                        step(dve.tensor_reduce(wide0[:, :], spread[:, 0:A0], AX, ALU.max))
                        dve.wait_ge(s_exp, 3)
                        for k in range(HEADS0):
                            step(dve.tensor_tensor(rows[:, :, k * F:(k + 1) * F], x[:, :, :], over(factor_r[:, :, k], F), ALU.mult))
                        dve.tensor_copy(rows[:, :, HEADS0 * F:ROW0], factor_r[:, :, :]).then_inc(s_rows, 1)

                    @block.scalar
                    def _(act):
                        act.wait_ge(s_less, 2)
                        act.activation(factor_r[:, :, :], logits[:, :, 0:HEADS0], ACT.Exp).then_inc(s_exp, 1)
                        act.activation(factor_t[:, :, :], logits[:, :, HEADS0:A0], ACT.Exp).then_inc(s_exp, 1)
                        act.activation(edge[:, :, 1], lens[:, :], ACT.Exp).then_inc(s_exp, 1)

            def exact_first_layer():
                with Phase(nc, "exact0") as ph:
                    score = ph.sb("score", [P, NG, T, A0])
                    lens = ph.sb("lens", [P, NG, T])
                    neg_c = ph.sb("neg_c", [P, 1])
                    idx = ph.sb("idx", [P, 1], I32)
                    row = ph.sb("row", [P, A0])
                    sums = ph.sb("sums", [WN, NW, A0 * F + A0])
                    twice = ph.sb("twice", [WN, NW, F])
                    w_heads = ph.sb("w_heads", [P, 2, F])
                    s_ld, s_idx, s_seen, s_rows, s_used, s_ch, s_neg = (
                        ph.sem(n) for n in ("s_ld", "s_idx", "s_seen", "s_rows", "s_used", "s_ch", "s_neg"))
                    s_exp, s_ch2, s_ch3 = ph.sem("s_exp"), ph.sem("s_ch2"), ph.sem("s_ch3")
                    with nc.Block() as block:

                        @block.sync
                        def _(sp):
                            with nc.allow_non_contiguous_dma("runs of eight edges"):
                                sp.dma_start(lens[:, 0:NG - 1, :], grouped(a["edge_weight"])).then_inc(s_ld, 16)
                                sp.dma_start(lens[:, NG - 1, :], a["edge_weight"][LAST:E].rearrange("(p j) -> p j", j=T)).then_inc(s_ld, 16)
                            sp.dma_start(neg_c[:, :], a["L0_gnn_radial_distance_scale"].partition_broadcast(P)).then_inc(s_ld, 16)
                            wh = a["L0_gnn_w_proj"].rearrange("h f g -> (h f) g").rearrange("(k p) g -> p k g", p=P)
                            sp.dma_start(w_heads[:, :, :], wh).then_inc(s_ld, 16)
                            sp.wait_ge(s_ld, 64)

                        @block.gpsimd
                        def _(pool):
                            pool.sem_inc(s_used, 1)
                            with pool.Fori(0, NG) as g:
                                for j in range(T):
                                    pool.wait_ge(s_used, g * T + j + 1)
                                    pool.sem_inc(s_seen, 1)
                                    pool.tensor_copy(idx[:, :], src_i[:, bass.ds(g, 1), j:j + 1].squeeze(1)).then_inc(s_idx, 1)
                                    pool.wait_ge(s_idx, g * T + j + 1)
                                    pool.sem_inc(s_seen, 1)
                                    pool.indirect_dma_start(row[:, :], None, logits_kept,
                                                            bass.IndirectOffsetOnAxis(ap=idx[:, 0:1], axis=0)).then_inc(s_rows, 16)

                        @block.vector
                        def _(dve):
                            step = Chain(dve, s_ch)
                            dve.wait_ge(s_ld, 64)
                            step(dve.tensor_scalar(neg_c[:, :], neg_c[:, :], -1.0, None, ALU.mult))
                            step(dve.memset(score[:, :, :, HEADS0:A0], 0.0))
                            step(dve.tensor_scalar(lens[:, :, :], lens[:, :, :], neg_c[:, 0:1], None, ALU.mult))
                            for k in range(HEADS0):
                                step(dve.tensor_copy(score[:, :, :, k], lens[:, :, :]))
                            with dve.Fori(0, NG) as g:
                                for j in range(T):
                                    dve.wait_ge(s_rows, 16 * (g * T + j + 1))
                                    of = score[:, bass.ds(g, 1), j, :].squeeze(1)
                                    dve.tensor_tensor(of, of, row[:, :], ALU.add).then_inc(s_used, 1)

                    subtract_largest("largest0", score, score)
                    with nc.Block() as block:

                        @block.vector
                        def _(dve):
                            dve.tensor_scalar(score[:, :, :, :], score[:, :, :, :], 0.0, None, ALU.min).then_inc(s_neg, 1)

                        @block.scalar
                        def _(act):
                            act.wait_ge(s_neg, 1)
                            act.activation(score[:, :, :, :], score[:, :, :, :], ACT.Exp).then_inc(s_exp, 1)

                    edge_sums("sums0", a["x"], score, sums)
                    with nc.Block() as block:

                        @block.vector
                        def _(dve):
                            step = Chain(dve, s_ch2)
                            den = sums[:, :, A0 * F:A0 * F + A0]
                            step(dve.tensor_scalar(den, den, TINY, None, ALU.max))
                            step(dve.reciprocal(den, den))
                            for k in range(A0):
                                part = sums[:, :, k * F:(k + 1) * F]
                                step(dve.tensor_tensor(part, part, over(den[:, :, k], F), ALU.mult))
                            both = sums[:, :, 0:HEADS0 * F]
                            step(dve.tensor_tensor(both, both, sums[:, :, HEADS0 * F:A0 * F], ALU.add))
                            step(dve.tensor_scalar(stat[:, 0, :], deg[:, :], 1.0, 2.0, ALU.min, ALU.mult))
                            step(dve.tensor_tensor(twice[:, :, :], x[:, :, :], over(stat[:, 0, :], F), ALU.mult))
                            for k in range(HEADS0):
                                part = sums[:, :, k * F:(k + 1) * F]
                                step(dve.tensor_tensor(part, part, twice[:, :, :], ALU.subtract))

                    node_linear(nc, "exact_heads", sums, [(0, P), (P, P)], lambda k: w_heads[:, k, :], F, None,
                                mean[:, 2:NW + 2, :], 1.0 / HEADS0)

            RAD, DEN, EA, DEG, RAW = 0, HEADS0 * F, ROW0, ROW0 + F, ROW0 + F + 1
            raw = first.sb("raw", [WN, NW, RAW])
            with Phase(nc, "edges0") as ph:
                zeros = ph.sb("zeros", [P, BANK], BF16)
                node_ids = ph.sb("node_ids", [P, N], F16)
                place = ph.sb("place", [P, QN])
                strip_start = ph.sb("strip_start", [P, NW * Q])
                ctl = ph.sb("ctl", [P, 2, Q, 4])
                idx = ph.sb("idx", [P, 2, Q], I32)
                rows = ph.sb("rows", [P, 2, Q, ROW0])
                rel = ph.sb("rel", [P, 2, Q])
                into = ph.sb("into", [P, 2, Q, QN])
                into_w = ph.sb("into_w", [P, 2, Q, QN])
                into16 = ph.sb("into16", [P, 2, Q, QN], BF16)
                fro = ph.sb("fro", [P, 2, Q, N], BF16)
                ea = ph.sb("ea", [P, 2, Q, F + 1])
                counts = ph.sb("counts", [WN, N], BF16)
                turned = ph.sb("turned", [WN, NW, WN], BF16)
                attr = ph.sb("attr", [P, 2, H, ED])
                attr_t = ph.sb("attr_t", [P, 2, P])
                hidden = ph.sb("hidden", [P, 2, P])
                w1 = ph.sb("w1", [P, P])
                w2 = ph.sb("w2", [P, H * HEADS2])
                b1 = ph.sb("b1", [P, 1])
                acc = ph.ps("acc", [P, 7 * BANK])
                side = ph.ps("side", [P, BANK])
                TAIL = N
                assert N + RAW <= 7 * BANK
                SPLIT = 3 * BANK
                HID, BIA, TUR, THREE = P, 2 * P, 2 * P + H * HEADS2, 3
                turn0 = [None]
                side_t = side[0:WN, TUR:TUR + 192].bitcast(BF16)[:, 0:THREE * P].rearrange("p (c n) -> p c n", n=P)
                side_all = side[0:WN, :].bitcast(BF16).rearrange("p (c n) -> p c n", n=P)
                s_w, s_zero, s_iota, s_init, s_ctl, s_idx, s_seen, s_rel, s_into, s_into_w, s_into16, s_fro, s_half = (
                    ph.sem(n) for n in ("s_w", "s_zero", "s_iota", "s_init", "s_ctl", "s_idx", "s_seen", "s_rel", "s_into",
                                        "s_into_w", "s_into16", "s_fro", "s_half_done"))
                s_side, s_read, s_free, s_stored, s_ctfree, s_ea_go, s_tail, s_tail_read = (
                    ph.sem(n) for n in ("s_side", "s_side_read", "s_acc_free", "s_counts_stored", "s_turned_free", "s_ea_go",
                                        "s_tail", "s_tail_read"))
                s_seen_pe, s_seen_ctl = ph.sem("s_seen_pe"), ph.sem("s_seen_ctl")
                s_rows = [ph.sem(f"s_rows{h}") for h in range(2)]
                s_ea = [ph.sem(f"s_ea{h}") for h in range(2)]
                s_attr = [ph.sem(f"s_attr{h}") for h in range(2)]

                with nc.Block() as block:

                    @block.gpsimd
                    def _(pool):
                        pool.memset(w1[:, :], 0.0).then_inc(s_zero, 1)
                        pool.memset(w2[:, :], 0.0).then_inc(s_zero, 1)
                        for ap in (attr_t, hidden):
                            pool.memset(ap[:, :, :], 0.0).then_inc(s_zero, 1)
                        pool.memset(counts[:, :], 0.0).then_inc(s_zero, 1)
                        pool.memset(turned[:, :, :], 0.0).then_inc(s_zero, 1)
                        pool.memset(ea[:, :, :, F:F + 1], 1.0).then_inc(s_zero, 1)

                    @block.sync
                    def _(sp):
                        sp.wait_ge(s_zero, 2)
                        with nc.allow_non_contiguous_dma("weights"):
                            for k in range(H):
                                part = slice(k * ED, (k + 1) * ED)
                                sp.dma_start(w1[part, part], a["L2_gnn_We1"]).then_inc(s_w, 16)
                                sp.dma_start(w2[part, k * HEADS2:(k + 1) * HEADS2], a["L2_gnn_We2"]).then_inc(s_w, 16)
                                sp.dma_start(b1[part, :], a["L2_gnn_be1"].rearrange("(f a) -> f a", a=1)).then_inc(s_w, 16)
                        sp.wait_ge(s_w, 16 * 3 * H)

                def least(eng, v, top):
                    past = eng.snap(((v + ((1 << 16) - top)) >> 16) & 1)
                    return in_range(eng.snap(v * (1 - past) + past * top), 0, top, "the smaller of two")

                with nc.Block() as block:

                    @block.sync
                    def _(sp):
                        def body(w, tile, v):
                            g = least(sp, v, NG - 1)
                            for h in range(2):
                                first_edges = []
                                for q in range(Q):
                                    t = tile(q, h)
                                    early = ((t + ((1 << TILE_BIT) - TILES + 1)) >> TILE_BIT) * TAIL0
                                    first_edges.append(in_range(sp.snap(t * P - early), 0, E - P, "full tiles within the edges"))
                                early = ((g + ((1 << CUM_BIT) - NG + 1)) >> CUM_BIT) * (NG * GE - E)
                                g0 = in_range(sp.snap(g * GE - early), 0, LAST, "full groups within the edges")
                                sp.wait_ge(s_side, 2 * v + h + 1)
                                sp.sem_inc(s_ea_go, 1)
                                of = a["edge_attr_32"][bass.ds(g0, GE), :].rearrange("(p j) f -> p j f", j=T)
                                sp.dma_start(attr[:, h], of[:, h * H:(h + 1) * H, :]).then_inc(s_attr[h], 16)
                                sp.wait_ge(s_half, 2 * v + h + 1)
                                sp.sem_inc(s_ea_go, 1)
                                for q, e0 in enumerate(first_edges):
                                    sp.dma_start(ea[:, h, q, 0:F], a["edge_attr_64"][bass.ds(e0, P), :]).then_inc(s_ea[h], 16)

                        def after(w, end):
                            sp.wait_ge(s_read, 2 * end + 1)
                            sp.dma_start(counts_t[bass.ds(w, 1)].squeeze(0),
                                         turned[:, :, :].rearrange("p c n -> p (c n)")).then_inc(s_stored, 16)
                            sp.wait_ge(s_stored, w * 16 + 16)
                            sp.sem_inc(s_ctfree, 1)

                        loop_strips(sp, body, after=after)
                        sp.wait_ge(s_tail_read, 4)
                        sp.dma_start(counts_t[NW], turned[:, :, :].rearrange("p c n -> p (c n)")).then_inc(s_stored, 16)
                        sp.wait_ge(s_stored, 16 * (NW + 1))

                    @block.gpsimd
                    def _(pool):
                        pool.iota(node_ids[:, :], [[1, N]], base=-(N // 2), channel_multiplier=0,
                                  allow_small_or_imprecise_dtypes=True).then_inc(s_iota, 1)
                        pool.iota(place[:, :], [[1, QN]], base=0, channel_multiplier=0,
                                  allow_small_or_imprecise_dtypes=True).then_inc(s_iota, 1)
                        pool.iota(strip_start[:, :], [[WN, NW], [QN, Q]], base=0, channel_multiplier=0,
                                  allow_small_or_imprecise_dtypes=True).then_inc(s_iota, 1)

                        def body(w, tile, v):
                            for h in range(2):
                                pool.wait_ge(s_ctl, 2 * v + h + 1)
                                pool.sem_inc(s_seen_ctl, 1)
                                pool.tensor_copy(idx[:, h, :], ctl[:, h, :, 2]).then_inc(s_idx, 1)
                                pool.wait_ge(s_idx, 2 * v + h + 1)
                                pool.sem_inc(s_seen, 1)
                                for q in range(Q):
                                    pool.indirect_dma_start(rows[:, h, q, :], None, table0,
                                                            bass.IndirectOffsetOnAxis(ap=idx[:, h, q:q + 1], axis=0)).then_inc(s_rows[h], 16)

                        loop_strips(pool, body)

                    @block.scalar
                    def _(act):
                        act.sem_inc(s_free, 1)
                        act.sem_inc(s_read, 1)
                        act.sem_inc(s_side, 2)
                        act.preload_act_table(ACT.Silu)

                        def before(w):
                            act.wait_ge(s_ctfree, w + 1)

                        def body(w, tile, v):
                            m = act.snap(v - turn0[0])
                            for h in range(2):
                                k = 2 * v + h
                                act.wait_ge(s_into, k + 1)
                                act.copy(into16[:, h], into[:, h]).then_inc(s_into16, 1)
                                for q in range(Q):
                                    last = act.activation(into_w[:, h, q, :], into[:, h, q, :], ACT.Copy, scale=ctl[:, h, q, 1:2])
                                last.then_inc(s_into_w, 1)
                                g = least(act, v, NG) if h == 0 else g
                                c0 = least(act, THREE * (2 * m + h), NW - THREE)
                                act.wait_ge(s_side, k + 3)
                                act.copy(attr_t[:, h], side[:, 0:HID])
                                act.activation(hidden[:, 1 - h], side[:, HID:BIA], ACT.Silu, bias=b1[:, 0:1])
                                act.copy(bias[:, bass.ds(g, 1), h * H * HEADS2:(h + 1) * H * HEADS2].squeeze(1), side[:, BIA:TUR])
                                act.copy(turned[:, bass.ds(c0, THREE), :], side_t[:, :, 0:WN]).then_inc(s_read, 1)

                        def after(w, end):
                            act.wait_ge(s_half, 2 * end + 2)
                            act.copy(counts[:, :], acc[0:WN, 0:N])
                            act.copy(raw[:, bass.ds(w, 1), :].squeeze(1), acc[0:WN, TAIL:TAIL + RAW]).then_inc(s_free, 1)

                        act.wait_ge(s_zero, 7)
                        act.sem_inc(s_ctfree, 1)
                        loop_strips(act, body, before, after, turn0)
                        act.wait_ge(s_ctfree, NW + 1)
                        for b in range(4):
                            c0, c1 = 8 * b, min(8 * b + 8, NW)
                            act.wait_ge(s_tail, b + 1)
                            act.copy(turned[:, c0:c1, :], side_all[:, 0:c1 - c0, 0:WN]).then_inc(s_tail_read, 1)

                    @block.vector
                    def _(dve):
                        dve.memset(zeros[:, :], 0.0).then_inc(s_init, 1)
                        dve.wait_ge(s_iota, 3)

                        def body(w, tile, v):
                            for h in range(2):
                                k = 2 * v + h
                                t = [tile(q, h) for q in range(Q)]
                                dve.wait_ge(s_half, k + 1)
                                for q in range(Q):
                                    last = dve.tensor_copy(ctl[:, h, q, :], edge[:, bass.ds(t[q], 1), :].squeeze(1))
                                last.then_inc(s_ctl, 1)
                                dve.wait_ge(s_ctl, k + 1)
                                dve.tensor_tensor(rel[:, h, :], ctl[:, h, :, 0], strip_start[:, bass.ds(w * Q, Q)],
                                                  ALU.subtract).then_inc(s_rel, 1)

                                def starts_at(q, c0, c1):
                                    return dve.tensor_scalar(fro[:, h, q, c0:c1], node_ids[:, c0:c1], ctl[:, h, q, 3:4],
                                                             None, ALU.is_equal)

                                starts_at(0, 0, SPLIT)
                                dve.wait_ge(s_rel, k + 1)
                                dve.tensor_tensor(into[:, h], place[:, :].unsqueeze(1).broadcast_to([P, Q, QN]),
                                                  over(rel[:, h, :], QN), ALU.is_equal).then_inc(s_into, 1)
                                starts_at(1, 0, SPLIT)
                                starts_at(2, 0, SPLIT)
                                starts_at(3, 0, SPLIT).then_inc(s_fro, 1)
                                for q in range(Q):
                                    last = starts_at(q, SPLIT, N)
                                last.then_inc(s_fro, 1)

                        loop_strips(dve, body)

                    @block.tensor
                    def _(pe):
                        pe.sem_inc(s_half, 2)
                        pe.wait_ge(s_init, 1)
                        pe.wait_ge(s_zero, 7)

                        def before(w):
                            pe.wait_ge(s_free, w + 1)
                            for b in range(7):
                                nc.tensor.matmul(acc[:, b * BANK:(b + 1) * BANK], zeros[:, 0:P], zeros[:, :], start=True, stop=True)

                        def add(q, c0, c1, lhsT, rhs):
                            return nc.tensor.matmul(acc[q * QN:(q + 1) * QN, c0:c1], lhsT, rhs, start=False, stop=True,
                                                    skip_group_check=True, tile_position=(0, q * QN))

                        def body(w, tile, v):
                            m = pe.snap(v - turn0[0])
                            for h in range(2):
                                k = 2 * v + h
                                c0 = least(pe, THREE * (2 * m + h), NW - THREE)
                                pe.wait_ge(s_attr[h], 16 * (v + 1))
                                pe.wait_ge(s_read, k + 1)
                                pe.sem_inc(s_seen_pe, 1)
                                nc.tensor.transpose(side[:, 0:HID], attr[:, h].rearrange("p j f -> p (j f)"), ident[:, :])
                                nc.tensor.matmul(side[:, HID:BIA], w1[:, :], attr_t[:, 1 - h], start=True, stop=True)
                                nc.tensor.matmul(side[:, BIA:TUR], hidden[:, h], w2[:, :], start=True, stop=True)
                                for c in range(THREE):
                                    last = nc.tensor.transpose(side_t[:, c, 0:WN], counts[:, bass.ds((c0 + c) * WN, WN)],
                                                               ident16[0:WN, 0:WN])
                                last.then_inc(s_side, 1)
                                pe.wait_ge(s_into16, k + 1)
                                pe.wait_ge(s_fro, 2 * k + 1)
                                for c in range(0, N, BANK):
                                    if c == SPLIT:
                                        pe.wait_ge(s_fro, 2 * k + 2)
                                    for q in range(Q):
                                        add(q, c, min(c + BANK, N), into16[:, h, q, :], fro[:, h, q, c:min(c + BANK, N)])
                                pe.wait_ge(s_ea[h], 16 * Q * (v + 1))
                                for q in range(Q):
                                    add(q, TAIL + EA, TAIL + RAW, into[:, h, q, :], ea[:, h, q, :])
                                pe.wait_ge(s_rows[h], 16 * Q * (v + 1))
                                pe.wait_ge(s_into_w, k + 1)
                                for q in range(Q):
                                    last = add(q, TAIL, TAIL + ROW0, into_w[:, h, q, :], rows[:, h, q, :])
                                last.then_inc(s_half, 1)

                        loop_strips(pe, body, before, None, turn0)
                        pe.wait_ge(s_free, NW + 1)
                        for b in range(4):
                            c0, c1 = 8 * b, min(8 * b + 8, NW)
                            if b:
                                pe.wait_ge(s_tail_read, b)
                            for c in range(c0, c1):
                                last = nc.tensor.transpose(side_all[:, c - c0, 0:WN], counts[:, c * WN:(c + 1) * WN],
                                                           ident16[0:WN, 0:WN])
                            last.then_inc(s_tail, 1)

            y = first.sb("y", [WN, NW, F])
            mean = first.sb("mean", [WN, NW + 2, F])
            w_out = first.sb("w_out", [F, F])
            with Phase(nc, "heads0") as ph:
                whole_t = ph.sb("whole_t", [WN, NW, ROW0])
                parts = ph.sb("parts", [WN, NW, 3, ROW0], BF16)
                counts_w = ph.sb("counts_w", [WN, U, NW, WN], BF16)
                twice = ph.sb("twice", [WN, NW, F])
                rden = ph.sb("rden", [WN, U, 2, HEADS0])
                msg = ph.sb("msg", [WN, U, HEADS0 * F])
                tan = ph.sb("tan", [WN, HEADS0 * F])
                msg_t = ph.sb("msg_t", [P, 2, WN])
                deg_top = ph.sb("deg_top", [P, 2])
                flag_f = ph.sb("flag_f", [P, 2])
                s_deg, s_deg_all = ph.sem("s_deg"), ph.sem("s_deg_all")
                w_heads = ph.sb("w_heads", [P, 2, F])
                tan_ps = ph.ps("tan_ps", [WN, U, BANK])
                msg_ps = ph.ps("msg_ps", [P, 2, P])
                mean_ps = ph.ps("mean_ps", [WN, BANK])
                s_ld, s_ch, s_cast, s_rest, s_zero, s_twice = (
                    ph.sem(n) for n in ("s_ld", "s_ch", "s_cast", "s_rest", "s_zero", "s_twice"))
                s_sum, s_msg, s_dve, s_go, s_turned, s_turned_sb, s_mean_ps, s_mean = (
                    ph.sem(n) for n in ("s_sum", "s_msg", "s_dve", "s_go", "s_turned", "s_turned_sb", "s_mean_ps", "s_mean"))
                s_ct = [ph.sem(f"s_counts{u}") for u in range(U)]
                with nc.Block() as block:

                    @block.sync
                    def _(sp):
                        wh = a["L0_gnn_w_proj"].rearrange("h f g -> (h f) g").rearrange("(k p) g -> p k g", p=P)
                        sp.dma_start(w_heads[:, :, :], wh).then_inc(s_ld, 16)
                        sp.dma_start(w_out[:, :], a["L0_gnn_w_out"]).then_inc(s_ld, 16)
                        with nc.allow_non_contiguous_dma("rows"):
                            sp.dma_start(edge_sum, raw[:, :, EA:DEG]).then_inc(s_ld, 16)
                        sp.dma_start(bias_kept, bias[:, 1:NG + 1, :].rearrange("p g c -> p (g c)")).then_inc(s_ld, 16)
                        with sp.Fori(0, NW // U) as i:
                            for u in range(U):
                                w = i * U + u
                                sp.wait_ge(s_sum, w + 1)
                                sp.dma_start(counts_w[:, u].rearrange("p c n -> p (c n)"),
                                             counts_t[bass.ds(w + 1, 1)].squeeze(0)).then_inc(s_ct[u], 16)
                        sp.wait_ge(s_ld, 64)

                    @block.gpsimd
                    def _(pool):
                        pool.memset(msg[:, :, :], 0.0).then_inc(s_zero, 1)
                        pool.memset(msg_t[:, :, :], 0.0).then_inc(s_zero, 1)
                        pool.wait_ge(s_deg, 1)
                        pool.partition_all_reduce(deg_top[:, 1:2], deg_top[:, 0:1], P, RMAX).then_inc(s_deg_all, 1)

                    @block.vector
                    def _(dve):
                        step = Chain(dve, s_ch)
                        step(dve.tensor_copy(deg[:, :], raw[:, :, DEG:RAW].squeeze(2)))
                        step(dve.memset(deg_top[:, :], 0.0))
                        dve.tensor_reduce(deg_top[0:WN, 0:1], deg[:, :], AX, ALU.max).then_inc(s_deg, 1)
                        step(dve.tensor_scalar(stat[:, 0, :], deg[:, :], 1.0, 2.0, ALU.min, ALU.mult))
                        step(dve.tensor_tensor(twice[:, :, :], x[:, :, :], over(stat[:, 0, :], F), ALU.mult))
                        blocks = [slice(b * U, (b + 1) * U) for b in range(NW // U)]
                        for b in blocks:
                            for k in range(HEADS0):
                                dve.tensor_tensor(whole_t[:, b, k * F:(k + 1) * F], x[:, b, :], over(factor_t[:, b, k], F), ALU.mult)
                            dve.tensor_copy(whole_t[:, b, HEADS0 * F:ROW0], factor_t[:, b, :]).then_inc(s_rest, 1)
                        for n in range(2):
                            for m, b in enumerate(blocks):
                                dve.wait_ge(s_cast, n * len(blocks) + m + 1)
                                dve.tensor_tensor(whole_t[:, b, :], whole_t[:, b, :], parts[:, b, n, :], ALU.subtract).then_inc(s_rest, 1)
                        dve.wait_ge(s_deg_all, 1)
                        step(dve.tensor_scalar(flag_f[:, 1:2], deg_top[:, 1:2], MOST_EXACT, None, ALU.is_gt))
                        step(dve.tensor_scalar(flag_f[:, 0:1], wide0[:, :], WIDEST, None, ALU.is_gt))
                        step(dve.tensor_tensor(flag_f[:, 0:1], flag_f[:, 0:1], flag_f[:, 1:2], ALU.max))
                        step(dve.tensor_copy(flags[:, 0:2], flag_f[:, :]))
                        dve.sem_inc(s_msg, U)
                        dve.wait_ge(s_zero, 2)
                        with dve.Fori(0, NW // U) as i:
                            for u in range(U):
                                w = i * U + u
                                sums = raw[:, bass.ds(w, 1), 0:ROW0].squeeze(1)

                                def heads(ap):
                                    return ap.rearrange("p (h f) -> p h f", f=F)

                                n = 4 * (i * U + u)
                                dve.wait_ge(s_sum, w + U + 1)
                                dve.tensor_scalar(rden[:, u, 0, :], sums[:, DEN:ROW0], TINY, None, ALU.max)
                                dve.tensor_scalar(rden[:, u, 1, :], tan_ps[:, u, DEN:ROW0], TINY, None, ALU.max).then_inc(s_dve, 1)
                                dve.wait_ge(s_dve, n + 1)
                                dve.reciprocal(rden[:, u], rden[:, u]).then_inc(s_dve, 1)
                                dve.wait_ge(s_dve, n + 2)
                                dve.tensor_tensor(heads(msg[:, u, :]), heads(sums[:, 0:DEN]), over(rden[:, u, 0, :], F), ALU.mult)
                                dve.tensor_tensor(heads(tan[:, :]), heads(tan_ps[:, u, 0:DEN]), over(rden[:, u, 1, :], F),
                                                  ALU.mult).then_inc(s_dve, 1)
                                dve.wait_ge(s_dve, n + 3)
                                dve.tensor_tensor(msg[:, u, :], msg[:, u, :], tan[:, :], ALU.add).then_inc(s_dve, 1)
                                dve.wait_ge(s_dve, n + 4)
                                dve.tensor_tensor(heads(msg[:, u, :]), heads(msg[:, u, :]),
                                                  twice[:, bass.ds(w, 1), :].broadcast_to([WN, HEADS0, F]), ALU.subtract).then_inc(s_msg, 1)

                    @block.scalar
                    def _(act):
                        act.sem_inc(s_turned_sb, 1)
                        act.sem_inc(s_mean, 1)
                        blocks = [slice(b * U, (b + 1) * U) for b in range(NW // U)]
                        for n in range(3):
                            for m, b in enumerate(blocks):
                                act.wait_ge(s_rest, n * len(blocks) + m + 1)
                                act.copy(parts[:, b, n, :], whole_t[:, b, :]).then_inc(s_cast, 1)

                        def means(w, ap):
                            act.wait_ge(s_mean_ps, w + 1)
                            act.activation(ap, mean_ps[:, 0:F], ACT.Copy, scale=1.0 / HEADS0).then_inc(s_mean, 1)

                        def turns(w):
                            act.wait_ge(s_turned, w + 1)
                            act.copy(msg_t[:, :, :], msg_ps[:, :, 0:WN]).then_inc(s_turned_sb, 1)

                        with act.Fori(0, NW // U) as i:
                            for u in range(U):
                                w = i * U + u
                                means(w, mean[:, bass.ds(w, 1), :].squeeze(1))
                                turns(w)
                        means(NW, mean[:, NW, :])
                        turns(NW)
                        means(NW + 1, mean[:, NW + 1, :])

                    @block.tensor
                    def _(pe):
                        pe.sem_inc(s_sum, U)
                        pe.wait_ge(s_ld, 64)
                        pe.wait_ge(s_cast, 3 * (NW // U))
                        pe.wait_ge(s_zero, 2)

                        def mean_of(w):
                            pe.wait_ge(s_turned_sb, w + 1)
                            pe.wait_ge(s_mean, w + 1)
                            for k in range(2):
                                last = nc.tensor.matmul(mean_ps[:, 0:F], msg_t[:, k, :], w_heads[:, k, :], start=(k == 0), stop=(k == 1))
                            last.then_inc(s_mean_ps, 1)

                        def turn(w, u):
                            pe.wait_ge(s_msg, w + U)
                            pe.sem_inc(s_go, 1)
                            for k in range(2):
                                last = nc.tensor.transpose(msg_ps[:, k, 0:WN], msg[:, u, k * P:(k + 1) * P], ident[0:WN, 0:WN])
                            last.then_inc(s_turned, 1)

                        with pe.Fori(0, NW // U) as i:
                            for u in range(U):
                                w = i * U + u
                                pe.wait_ge(s_ct[u], 16 * (i + 1))
                                pe.wait_ge(s_msg, w + 1)
                                for c in range(NW):
                                    for k in range(3):
                                        last = nc.tensor.matmul(tan_ps[:, u, 0:ROW0], counts_w[:, u, c, :], parts[:, c, k, :],
                                                                start=(c == 0 and k == 0), stop=(c == NW - 1 and k == 2))
                                last.then_inc(s_sum, 1)
                                mean_of(w)
                                turn(w, (u - 1) % U)
                        mean_of(NW)
                        turn(NW, U - 1)
                        mean_of(NW + 1)

            with nc.If(nc.values_load(flags[0:1, 0:1], min_val=0, max_val=1) > 0):
                nc.all_engine_barrier()
                exact_first_layer()
                nc.all_engine_barrier()
            nc.end_ifs()
            nc.all_engine_barrier()

            with Phase(nc, "nodes0") as ph:
                means = mean[:, 2:NW + 2, :]
                tmp = ph.sb("tmp", [WN, NW, F])
                s_ch2, s_ch3 = ph.sem("s_ch2"), ph.sem("s_ch3")
                with nc.Block() as block:

                    @block.vector
                    def _(dve):
                        step = Chain(dve, s_ch2)
                        step(dve.tensor_tensor(tmp[:, :, :], means, means, ALU.is_equal))
                        step(dve.memset(y[:, :, :], 0.0))
                        step(dve.copy_predicated(y[:, :, :], tmp[:, :, :].bitcast(I32), means))
                        step(dve.tensor_scalar(means, y[:, :, :], 3.4028234e38, -3.4028234e38, ALU.min, ALU.max))

                node_linear(nc, "out0", means, [(0, F)], lambda k: w_out[:, :], F, None, y)
                norm = Norm(ph, "norm", stat, minus_half)
                with nc.Block() as block:

                    @block.gpsimd
                    def _(pool):
                        norm.on_gpsimd(pool)

                    @block.vector
                    def _(dve):
                        step = Chain(dve, s_ch3)
                        step(dve.tensor_tensor(y[:, :, :], y[:, :, :], x[:, :, :], ALU.add))
                        step(dve.tensor_tensor(y[:, :, :], y[:, :, :], x[:, :, :], ALU.add))
                        norm.on_vector(step, dve, y[:, :, :], x[:, :, :], tmp[:, :, :])

        def dense_sum(tag, counts_sb, parts, dst):
            with Phase(nc, tag) as ph:
                sum_ps = ph.ps("sum_ps", [WN, U, BANK])
                s_sum, s_out = ph.sem("s_sum"), ph.sem("s_out")
                with nc.Block() as block:

                    @block.tensor
                    def _(pe):
                        with pe.Fori(0, NW // U) as i:
                            for u in range(U):
                                w = i * U + u
                                pe.wait_ge(s_out, w + 1)
                                for c in range(NW):
                                    last = nc.tensor.matmul(sum_ps[:, u, 0:3 * F],
                                                            counts_sb[:, bass.ds(w, 1), c * WN:(c + 1) * WN].squeeze(1),
                                                            parts[:, c, :, :].rearrange("p k f -> p (k f)"),
                                                            start=(c == 0), stop=(c == NW - 1))
                                last.then_inc(s_sum, 1)

                    @block.vector
                    def _(dve):
                        dve.sem_inc(s_out, U)
                        with dve.Fori(0, NW // U) as i:
                            for u in range(U):
                                w = i * U + u
                                dve.wait_ge(s_sum, w + 1)
                                dve.tensor_reduce(dst[:, bass.ds(w, 1), 0:F].squeeze(1),
                                                  sum_ps[:, u, 0:3 * F].rearrange("p (k f) -> p f k", k=3),
                                                  AX, ALU.add).then_inc(s_out, 1)

        def sum_by_edge(tag, h, dst):
            with nc.If(nc.values_load(flags[0:1, 1:2], min_val=0, max_val=1) > 0):
                nc.all_engine_barrier()
                with Phase(nc, tag) as ph:
                    s_st = ph.sem("s_st")
                    with nc.Block() as block:

                        @block.sync
                        def _(sp):
                            with nc.allow_non_contiguous_dma("table rows"):
                                sp.dma_start(table_h.rearrange("(w p) f -> p w f", p=WN), h).then_inc(s_st, 16)
                            sp.wait_ge(s_st, 16)

                    edge_sums(tag + "_sums", table_h, None, dst)
                nc.all_engine_barrier()
            nc.end_ifs()
            nc.all_engine_barrier()

        def split3(step, dve, parts, rest, src):
            step(dve.tensor_copy(parts[:, :, 0, :], src))
            step(dve.tensor_tensor(rest, src, parts[:, :, 0, :], ALU.subtract))
            step(dve.tensor_copy(parts[:, :, 1, :], rest))
            step(dve.tensor_tensor(rest, rest, parts[:, :, 1, :], ALU.subtract))
            step(dve.tensor_copy(parts[:, :, 2, :], rest))

        with Phase(nc, "rounds") as ph:
            counts_sb = ph.sb("counts_sb", [WN, NW, N], BF16)
            parts = ph.sb("parts", [WN, NW, 3, F], BF16)
            cat = ph.sb("cat", [WN, NW, 2 * F])
            w_lr = ph.sb("w_lr", [P, 3, F])
            w_one = ph.sb("w_one", [F, 2, F])
            vecs = ph.sb("vecs", [WN, 11, F])
            inv_deg = ph.sb("inv_deg", [WN, NW])
            y = ph.sb("y", [WN, NW, F])
            h_in = cat[:, :, F:2 * F]
            s_ld, s_ct = ph.sem("s_ld"), ph.sem("s_ct")
            with nc.Block() as block:

                @block.sync
                def _(sp):
                    for w in range(NW):
                        sp.dma_start(counts_sb[:, w, :], counts_t[w + 1]).then_inc(s_ct, 16)
                    sp.wait_ge(s_ct, 16 * NW)

                @block.scalar
                def _(act):
                    with nc.allow_non_contiguous_dma("weights"):
                        act.dma_start(w_lr[0:F, :, :], a["L1_gnn_w_l"].rearrange("l f g -> f l g")).then_inc(s_ld, 16)
                        act.dma_start(w_lr[F:P, :, :], a["L1_gnn_w_r"].rearrange("l f g -> f l g")).then_inc(s_ld, 16)
                    act.dma_start(w_one[:, 0, :], a["L1_gnn_w_res"]).then_inc(s_ld, 16)
                    act.dma_start(w_one[:, 1, :], a["L1_gnn_w_fc"]).then_inc(s_ld, 16)
                    for n, name in enumerate(("L1_gnn_b_l", "L1_gnn_gamma", "L1_gnn_beta")):
                        act.dma_start(vecs[:, 3 * n:3 * n + 3, :], a[name].partition_broadcast(WN)).then_inc(s_ld, 16)
                    act.dma_start(vecs[:, 9, :], a["L1_gnn_b_res"].partition_broadcast(WN)).then_inc(s_ld, 16)
                    act.dma_start(vecs[:, 10, :], a["L1_gnn_b_fc"].partition_broadcast(WN)).then_inc(s_ld, 16)
                    act.wait_ge(s_ld, 16 * 9)

                s_ch = ph.sem("s_prep")

                @block.vector
                def _(dve):
                    step = Chain(dve, s_ch)
                    step(dve.tensor_scalar(inv_deg[:, :], deg[:, :], 1.0, None, ALU.max))
                    step(dve.reciprocal(inv_deg[:, :], inv_deg[:, :]))
                    step(dve.tensor_scalar(stat[:, 0, :], deg[:, :], 1.0, None, ALU.min))
                    step(dve.tensor_tensor(inv_deg[:, :], inv_deg[:, :], stat[:, 0, :], ALU.mult))
                    step(dve.tensor_copy(h_in, x[:, :, :]))
                    split3(step, dve, parts, y[:, :, :], x[:, :, :])

            for r in range(3):
                dense_sum(f"r{r}", counts_sb, parts, cat)
                sum_by_edge(f"edges_r{r}", h_in, cat)
                s_ch = ph.sem(f"s_mean{r}")
                with nc.Block() as block:

                    @block.vector
                    def _(dve):
                        step = Chain(dve, s_ch)
                        step(dve.tensor_tensor(cat[:, :, 0:F], cat[:, :, 0:F], over(inv_deg[:, :], F), ALU.mult))

                node_linear(nc, f"lr{r}", cat, [(0, P)], lambda k: w_lr[:, r, :], F, vecs[:, r, :], y)
                s_ch = ph.sem(f"s_round{r}")
                norm = Norm(ph, f"norm{r}", stat, minus_half)
                with nc.Block() as block:

                    @block.gpsimd
                    def _(pool):
                        norm.on_gpsimd(pool)

                    @block.vector
                    def _(dve):
                        def each(n):
                            return vecs[:, n, :].unsqueeze(1).broadcast_to([WN, NW, F])
                        step = Chain(dve, s_ch)
                        norm.on_vector(step, dve, y[:, :, :], y[:, :, :], cat[:, :, 0:F])
                        step(dve.tensor_tensor(y[:, :, :], y[:, :, :], each(3 + r), ALU.mult))
                        step(dve.tensor_tensor(y[:, :, :], y[:, :, :], each(6 + r), ALU.add))
                        step(dve.tensor_scalar(y[:, :, :], y[:, :, :], 0.0, None, ALU.max))

                residual = h_in
                if r == 0:
                    residual = cat[:, :, 0:F]
                    node_linear(nc, "res", x, [(0, F)], lambda k: w_one[:, 0, :], F, vecs[:, 9, :], cat)
                s_ch = ph.sem(f"s_sum{r}")
                with nc.Block() as block:

                    @block.vector
                    def _(dve):
                        step = Chain(dve, s_ch)
                        step(dve.tensor_tensor(h_in, y[:, :, :], residual, ALU.add))
                        if r < 2:
                            split3(step, dve, parts, y[:, :, :], h_in)

            node_linear(nc, "fc", h_in, [(0, F)], lambda k: w_one[:, 1, :], F, vecs[:, 10, :], y)
            s_ch = ph.sem("s_norm1")
            norm = Norm(ph, "norm", stat, minus_half)
            with nc.Block() as block:

                @block.gpsimd
                def _(pool):
                    norm.on_gpsimd(pool)

                @block.vector
                def _(dve):
                    step = Chain(dve, s_ch)
                    step(dve.tensor_tensor(y[:, :, :], y[:, :, :], x[:, :, :], ALU.add))
                    norm.on_vector(step, dve, y[:, :, :], x[:, :, :], cat[:, :, 0:F])

        with Phase(nc, "attention") as layer:
            bias = layer.sb("bias", [P, NG, T * HEADS2])
            q = layer.sb("q", [WN, NW + 1, F])
            attn = layer.sb("attn", [WN, NW, F + HEADS2])
            w_sq = layer.sb("w_sq", [F, 4, F])
            b_sq = layer.sb("b_sq", [WN, 4, F])
            b2 = layer.sb("b2", [P, HEADS2])
            with Phase(nc, "weights2") as ph:
                s_w = ph.sem("s_w")
                with nc.Block() as block:

                    @block.sync
                    def _(sp):
                        sp.dma_start(bias[:, :, :].rearrange("p g c -> p (g c)"), bias_kept).then_inc(s_w, 16)
                        sp.dma_start(b2[:, :], a["L2_gnn_be2"].partition_broadcast(P)).then_inc(s_w, 16)
                        for n, name in enumerate("QKVO"):
                            sp.dma_start(w_sq[:, n, :], a["L2_gnn_W" + name]).then_inc(s_w, 16)
                            sp.dma_start(b_sq[:, n, :], a["L2_gnn_b" + name].partition_broadcast(WN)).then_inc(s_w, 16)
                        sp.wait_ge(s_w, 160)

            with Phase(nc, "kvq") as ph:
                kv = ph.sb("kv", [WN, NW, 2 * F])
                sq = ph.sb("sq", [WN, NW, F])
                norms = ph.sb("norms", [WN, NW, HEADS2])
                top = ph.sb("top", [P, 3 * HEADS2])
                top_all = ph.sb("top_all", [P, 3 * HEADS2])
                bound = ph.sb("bound", [P, HEADS2])
                node_linear(nc, "q", x, [(0, F)], lambda k: w_sq[:, 0, :], F, b_sq[:, 0, :], q)
                node_linear(nc, "kv", x, [(0, F)], lambda k: w_sq[:, 1:3, :].rearrange("p a f -> p (a f)"), 2 * F,
                            b_sq[:, 1:3, :].rearrange("p a f -> p (a f)"), kv)
                s_st, s_ch, s_top, s_all = ph.sem("s_st"), ph.sem("s_ch"), ph.sem("s_top"), ph.sem("s_all")
                s_bound, s_root = ph.sem("s_bound"), ph.sem("s_root")
                with nc.Block() as block:

                    @block.sync
                    def _(sp):
                        with nc.allow_non_contiguous_dma("table rows"):
                            sp.dma_start(table_kv.rearrange("(w p) c -> p w c", p=WN), kv[:, :, :]).then_inc(s_st, 16)
                        sp.wait_ge(s_st, 16)

                    @block.gpsimd
                    def _(pool):
                        pool.wait_ge(s_top, 1)
                        pool.partition_all_reduce(top_all[:, :], top[:, :], P, RMAX).then_inc(s_all, 1)
                        pool.wait_ge(s_bound, 1)
                        pool.tensor_tensor(bound[:, :], bound[:, :], half[:, :], ALU.pow).then_inc(s_root, 1)

                    @block.vector
                    def _(dve):
                        step = Chain(dve, s_ch)
                        step(dve.memset(q[:, NW, :], 0.0))
                        step(dve.tensor_scalar(q[:, 0:NW, :], q[:, 0:NW, :], float(DK) ** -0.5, None, ALU.mult))
                        step(dve.memset(top[:, :], -3e38))
                        for n, of in enumerate((q[:, 0:NW, :], kv[:, :, 0:F])):
                            step(dve.tensor_tensor(sq[:, :, :], of, of, ALU.mult))
                            step(dve.tensor_reduce(norms[:, :, :], sq[:, :, :].rearrange("p w (h d) -> p w h d", d=DK), AX, ALU.add))
                            step(dve.tensor_reduce(top[0:WN, n * HEADS2:(n + 1) * HEADS2],
                                                   norms[:, :, :].rearrange("p w h -> p h w"), AX, ALU.max))
                        by_head = bias[:, :, :].rearrange("p g (j h) -> p (g j) h", h=HEADS2)
                        step(dve.tensor_tensor(by_head, by_head, b2[:, :].unsqueeze(1).broadcast_to([P, NG * T, HEADS2]), ALU.add))
                        dve.tensor_reduce(top[:, 2 * HEADS2:3 * HEADS2], by_head.rearrange("p e h -> p h e"), AX,
                                          ALU.max).then_inc(s_top, 1)
                        dve.wait_ge(s_all, 1)
                        dve.tensor_tensor(bound[:, :], top_all[:, 0:HEADS2], top_all[:, HEADS2:2 * HEADS2],
                                          ALU.mult).then_inc(s_bound, 1)
                        dve.wait_ge(s_root, 1)
                        step(dve.tensor_tensor(bound[:, :], bound[:, :], top_all[:, 2 * HEADS2:3 * HEADS2], ALU.add))
                        step(dve.tensor_tensor(by_head, by_head, bound[:, :].unsqueeze(1).broadcast_to([P, NG * T, HEADS2]),
                                               ALU.subtract))

            def attend(tag):
                with Phase(nc, tag) as ph:
                    zeros = ph.sb("zeros", [P, P])
                    idx = ph.sb("idx", [P, 2, H], I32)
                    rows = ph.sb("rows", [P, 2, H, 2 * F])
                    dst_rel = ph.sb("dst_rel", [P, 2, H])
                    dst_ahead = ph.sb("dst_ahead", [P, 2, H])
                    into = ph.sb("into", [P, 2, H, WN])
                    ahead = ph.sb("ahead", [P, 2, H, WN], BF16)
                    into_t = ph.sb("into_t", [WN, 2, H, P])
                    prod = ph.sb("prod", [P, 2, H, F])
                    score = ph.sb("score", [P, 2, H, HEADS2])
                    weighted = ph.sb("weighted", [P, 2, H, F + HEADS2])
                    t_ps = ph.ps("t_ps", [P, 2, 2 * H, P], BF16)
                    q_ps = ph.ps("q_ps", [P, 2, H, P])
                    acc = ph.ps("acc", [P, BANK])
                    s_idx, s_rel, s_into, s_t, s_tc, s_q, s_prod, s_score, s_sb, s_exp, s_m, s_half, s_free, s_seen, s_init = (
                        ph.sem(n) for n in ("s_idx", "s_rel", "s_into", "s_turned_ps", "s_turned", "s_query", "s_prod",
                                            "s_dot", "s_score", "s_exp", "s_weighted", "s_half_done", "s_acc_free", "s_seen", "s_init"))
                    s_rel2, s_ahead = ph.sem("s_rel_ahead"), ph.sem("s_ahead")
                    s_rows = [ph.sem(f"s_rows{h}") for h in range(2)]

                    def next_window(eng, w, v, end):
                        bit = END_BIT - CUM_BIT
                        last = in_range(eng.snap(1 - (((end - v - 2 + (1 << bit)) >> bit) & 1)), 0, 1, "one bit")
                        return last, in_range(eng.snap(w + last), 0, NW, "one past the last window at most")

                    with nc.Block() as block:

                        @block.gpsimd
                        def _(pool):
                            def body(w, g, v, end):
                                for h in range(2):
                                    pool.wait_ge(s_m, 2 * v + h + 1)
                                    pool.tensor_copy(idx[:, h, :], src_i[:, bass.ds(g, 1), h * H:(h + 1) * H].squeeze(1)).then_inc(s_idx, 1)
                                    pool.wait_ge(s_idx, 2 * v + h + 1)
                                    pool.sem_inc(s_seen, 1)
                                    for j in range(H):
                                        pool.indirect_dma_start(rows[:, h, j, :], None, table_kv,
                                                                bass.IndirectOffsetOnAxis(ap=idx[:, h, j:j + 1], axis=0)).then_inc(s_rows[h], 16)

                            loop_windows(pool, body)

                        @block.vector
                        def _(dve):
                            dve.memset(zeros[:, :], 0.0).then_inc(s_init, 1)
                            dve.sem_inc(s_m, 2)
                            dve.sem_inc(s_prod, 2)

                            def match(to, rel, s_rel, s_to, w, g, h, k):
                                dve.tensor_scalar(rel[:, h], dst_f[:, bass.ds(g, 1), h * H:(h + 1) * H].squeeze(1),
                                                  window_start[:, bass.ds(w, 1)], None, ALU.subtract).then_inc(s_rel, 1)
                                dve.wait_ge(s_rel, k)
                                dve.tensor_tensor(to[:, h], iota_n[:, :].unsqueeze(1).broadcast_to([P, H, WN]),
                                                  over(rel[:, h], WN), ALU.is_equal).then_inc(s_to, 1)

                            def match_ahead(w, g, h, k):
                                dve.wait_ge(s_t, k)
                                match(ahead, dst_ahead, s_rel2, s_ahead, w, g, h, k)

                            def match_into(w, g, h, k):
                                dve.wait_ge(s_half, k)
                                match(into, dst_rel, s_rel, s_into, w, g, h, k)

                            def scores(g, v, h, k):
                                dve.wait_ge(s_rows[h], 16 * H * (v + 1))
                                dve.wait_ge(s_q, 2 + k)
                                dve.tensor_tensor(prod[:, h], rows[:, h, :, 0:F], q_ps[:, h, :, 0:F], ALU.mult).then_inc(s_prod, 1)
                                dve.wait_ge(s_prod, 2 + k)
                                dve.tensor_reduce(score[:, h], prod[:, h].rearrange("p j (h d) -> p j h d", d=DK), AX,
                                                  ALU.add).then_inc(s_score, 1)
                                dve.wait_ge(s_score, k)
                                dve.tensor_tensor(score[:, h], score[:, h],
                                                  bias[:, bass.ds(g, 1), h * H * HEADS2:(h + 1) * H * HEADS2].squeeze(1)
                                                  .rearrange("p (j h) -> p j h", h=HEADS2), ALU.add).then_inc(s_sb, 1)

                            def weigh(h, k):
                                dve.wait_ge(s_exp, k)
                                dve.tensor_tensor(weighted[:, h, :, 0:F].rearrange("p j (h d) -> p j h d", d=DK),
                                                  rows[:, h, :, F:2 * F].rearrange("p j (h d) -> p j h d", d=DK),
                                                  weighted[:, h, :, F:F + HEADS2].unsqueeze(3).broadcast_to([P, H, HEADS2, DK]),
                                                  ALU.mult).then_inc(s_m, 1)

                            def body(w, g, v, end):
                                k = 2 * v + 1
                                last, w_next = next_window(dve, w, v, end)
                                g_next = dve.snap(g + 1 + last * (lo_next[0] - g - 1))
                                g_next = in_range(g_next, 0, NG - 1, "visits go to groups that exist")
                                match_ahead(w_next, g_next, 0, k + 2)
                                scores(g, v, 0, k)
                                weigh(0, k)
                                match_into(w, g, 1, k + 1)
                                match_ahead(w_next, g_next, 1, k + 3)
                                scores(g, v, 1, k + 1)
                                weigh(1, k + 1)
                                match_into(w_next, g_next, 0, k + 2)

                            def before(w):
                                lo_next[0] = dve.value_load(visits[0:1, 1, bass.ds(w + 1, 1)], min_val=0, max_val=NG - 1)

                            lo_next = [None]
                            g0 = dve.value_load(visits[0:1, 1, 0:1], min_val=0, max_val=NG - 1)
                            match_ahead(0, g0, 0, 1)
                            match_ahead(0, g0, 1, 2)
                            match_into(0, g0, 0, 1)
                            loop_windows(dve, body, before)

                        @block.scalar
                        def _(act):
                            act.sem_inc(s_free, 1)
                            act.sem_inc(s_tc, 2)
                            act.preload_act_table(ACT.Exp)

                            def copy_turned(h, k):
                                act.wait_ge(s_t, k + 2)
                                act.wait_ge(s_q, k)
                                act.copy(into_t[:, h], t_ps[0:WN, h, 0:H, :]).then_inc(s_tc, 1)

                            def exps(h, k):
                                act.wait_ge(s_sb, k)
                                act.activation(weighted[:, h, :, F:F + HEADS2], score[:, h], ACT.Exp).then_inc(s_exp, 1)

                            def body(w, g, v, end):
                                k = 2 * v + 1
                                exps(0, k)
                                copy_turned(0, k + 2)
                                exps(1, k + 1)
                                copy_turned(1, k + 3)

                            def after(w, end):
                                act.wait_ge(s_half, 2 * end + 2)
                                act.copy(attn[:, bass.ds(w, 1), :].squeeze(1), acc[0:WN, 0:F + HEADS2]).then_inc(s_free, 1)

                            copy_turned(0, 1)
                            copy_turned(1, 2)
                            loop_windows(act, body, after=after)

                        @block.tensor
                        def _(pe):
                            for s in (s_half, s_t, s_q):
                                pe.sem_inc(s, 2)
                            pe.wait_ge(s_init, 1)

                            def before(w):
                                pe.wait_ge(s_free, w + 1)
                                nc.tensor.matmul(acc[0:WN, 0:P], zeros[:, 0:WN], zeros[:, :], start=True, stop=True)

                            def spread(w, h, k):
                                pe.wait_ge(s_ahead, k)
                                pe.wait_ge(s_tc, k)
                                for j in range(H):
                                    last = nc.tensor.transpose(t_ps[0:WN, h, j, :], ahead[:, h, j, :], ident16[:, :])
                                last.then_inc(s_t, 1)
                                pe.wait_ge(s_tc, 2 + k)
                                pe.wait_ge(s_prod, k)
                                for j in range(H):
                                    last = nc.tensor.matmul(q_ps[:, h, j, 0:F], into_t[:, h, j, :],
                                                            q[:, bass.ds(w, 1), :].squeeze(1), start=True, stop=True)
                                last.then_inc(s_q, 1)

                            def add(h, k):
                                pe.wait_ge(s_m, 2 + k)
                                for j in range(H):
                                    last = nc.tensor.matmul(acc[0:WN, 0:F + HEADS2], into[:, h, j, :], weighted[:, h, j, :],
                                                            start=False, stop=True, skip_group_check=True)
                                last.then_inc(s_half, 1)

                            def body(w, g, v, end):
                                k = 2 * v + 1
                                _, w_next = next_window(pe, w, v, end)
                                for h in range(2):
                                    spread(w_next, h, k + h + 2)
                                    add(h, k + h)

                            spread(0, 0, 1)
                            spread(0, 1, 2)
                            loop_windows(pe, body, before)

            def exact_shift():
                with Phase(nc, "exact2") as ph:
                    score = ph.sb("score", [P, NG, T, HEADS2])
                    idx = ph.sb("idx", [P, 2], I32)
                    dst_in = ph.sb("dst_in", [P, NG, T])
                    k_row = ph.sb("k_row", [P, 2 * F])
                    q_row = ph.sb("q_row", [P, F])
                    prod = ph.sb("prod", [P, F])
                    s_st, s_dst, s_idx, s_seen, s_k, s_q, s_used, s_steps = (
                        ph.sem(n) for n in ("s_st", "s_dst", "s_idx", "s_seen", "s_k", "s_q", "s_used", "s_steps"))
                    with nc.Block() as block:

                        @block.sync
                        def _(sp):
                            with nc.allow_non_contiguous_dma("table rows"):
                                sp.dma_start(table_q.rearrange("(w p) f -> p w f", p=WN), q[:, 0:NW, :]).then_inc(s_st, 16)
                            sp.wait_ge(s_st, 16)

                        @block.gpsimd
                        def _(pool):
                            pool.sem_inc(s_used, 1)
                            pool.wait_ge(s_dst, 1)
                            pool.wait_ge(s_st, 16)
                            with pool.Fori(0, NG) as g:
                                for j in range(T):
                                    pool.wait_ge(s_used, g * T + j + 1)
                                    pool.sem_inc(s_seen, 1)
                                    pool.tensor_copy(idx[:, 0:1], src_i[:, bass.ds(g, 1), j:j + 1].squeeze(1))
                                    pool.tensor_copy(idx[:, 1:2], dst_in[:, bass.ds(g, 1), j:j + 1].squeeze(1)).then_inc(s_idx, 1)
                                    pool.wait_ge(s_idx, g * T + j + 1)
                                    pool.sem_inc(s_seen, 1)
                                    pool.indirect_dma_start(k_row[:, :], None, table_kv,
                                                            bass.IndirectOffsetOnAxis(ap=idx[:, 0:1], axis=0)).then_inc(s_k, 16)
                                    pool.indirect_dma_start(q_row[:, :], None, table_q,
                                                            bass.IndirectOffsetOnAxis(ap=idx[:, 1:2], axis=0)).then_inc(s_q, 16)

                        @block.vector
                        def _(dve):
                            dve.tensor_scalar(dst_in[:, :, :], dst_f[:, :, :], 0.0, None, ALU.max).then_inc(s_dst, 1)
                            with dve.Fori(0, NG) as g:
                                for j in range(T):
                                    n = 2 * (g * T + j)
                                    dve.wait_ge(s_k, 16 * (g * T + j + 1))
                                    dve.wait_ge(s_q, 16 * (g * T + j + 1))
                                    of = score[:, bass.ds(g, 1), j, :].squeeze(1)
                                    dve.tensor_tensor(prod[:, :], k_row[:, 0:F], q_row[:, :], ALU.mult).then_inc(s_steps, 1)
                                    dve.wait_ge(s_steps, n + 1)
                                    dve.tensor_reduce(of, prod[:, :].rearrange("p (h d) -> p h d", d=DK), AX, ALU.add).then_inc(s_steps, 1)
                                    dve.wait_ge(s_steps, n + 2)
                                    dve.tensor_tensor(of, of, bias[:, bass.ds(g, 1), j * HEADS2:(j + 1) * HEADS2].squeeze(1),
                                                      ALU.add).then_inc(s_used, 1)

                    subtract_largest("largest2", score, bias[:, :, :].rearrange("p g (j h) -> p g j h", h=HEADS2))

            attend("edges2")
            with Phase(nc, "sums_seen") as ph:
                seen = ph.sb("seen", [WN, NW, HEADS2])
                low = ph.sb("low", [P, 3])
                s_ch, s_low, s_all = ph.sem("s_ch"), ph.sem("s_low"), ph.sem("s_all")
                with nc.Block() as block:

                    @block.gpsimd
                    def _(pool):
                        pool.wait_ge(s_low, 1)
                        pool.partition_all_reduce(low[:, 1:2], low[:, 0:1], P, RMAX).then_inc(s_all, 1)

                    @block.vector
                    def _(dve):
                        step = Chain(dve, s_ch)
                        step(dve.memset(low[:, :], 0.0))
                        step(dve.tensor_scalar(seen[:, :, :], attn[:, :, F:F + HEADS2], SMALLEST, None, ALU.is_lt))
                        step(dve.tensor_tensor(seen[:, :, :], seen[:, :, :], over(deg[:, :], HEADS2), ALU.mult))
                        dve.tensor_reduce(low[0:WN, 0:1], seen[:, :, :].rearrange("p w h -> p (w h)"), AX, ALU.max).then_inc(s_low, 1)
                        dve.wait_ge(s_all, 1)
                        step(dve.tensor_scalar(low[:, 2:3], low[:, 1:2], 0.0, None, ALU.is_gt))
                        step(dve.tensor_copy(flags[:, 2:3], low[:, 2:3]))

            with nc.If(nc.values_load(flags[0:1, 2:3], min_val=0, max_val=1) > 0):
                nc.all_engine_barrier()
                exact_shift()
                attend("edges2_exact")
                nc.all_engine_barrier()
            nc.end_ifs()
            nc.all_engine_barrier()

            with Phase(nc, "nodes2") as ph:
                rden = ph.sb("rden", [WN, NW, HEADS2])
                y = ph.sb("y", [WN, NW, F])
                tmp = ph.sb("tmp", [WN, NW, F])
                s_ch, s_ch2 = ph.sem("s_ch"), ph.sem("s_ch2")
                with nc.Block() as block:

                    @block.vector
                    def _(dve):
                        step = Chain(dve, s_ch)
                        step(dve.tensor_scalar(rden[:, :, :], attn[:, :, F:F + HEADS2], TINY, None, ALU.max))
                        step(dve.reciprocal(rden[:, :, :], rden[:, :, :]))
                        for h in range(HEADS2):
                            part = attn[:, :, h * DK:(h + 1) * DK]
                            step(dve.tensor_tensor(part, part, over(rden[:, :, h], DK), ALU.mult))

                node_linear(nc, "wo", attn, [(0, F)], lambda k: w_sq[:, 3, :], F, b_sq[:, 3, :], y)
                norm = Norm(ph, "norm", stat, minus_half)
                with nc.Block() as block:

                    @block.gpsimd
                    def _(pool):
                        norm.on_gpsimd(pool)

                    @block.vector
                    def _(dve):
                        step = Chain(dve, s_ch2)
                        step(dve.tensor_tensor(y[:, :, :], y[:, :, :], x[:, :, :], ALU.add))
                        norm.on_vector(step, dve, y[:, :, :], x[:, :, :], tmp[:, :, :])

        with Phase(nc, "last") as ph:
            counts_sb = ph.sb("counts_sb", [WN, NW, N], BF16)
            parts = ph.sb("parts", [WN, NW, 3, F], BF16)
            y = ph.sb("y", [WN, NW, F])
            tmp = ph.sb("tmp", [WN, NW, F])
            sums = ph.sb("sums", [WN, NW, F])
            s_ct, s_ch, s_ch2, s_out = ph.sem("s_ct"), ph.sem("s_ch"), ph.sem("s_ch2"), ph.sem("s_out")
            with nc.Block() as block:

                @block.sync
                def _(sp):
                    for w in range(NW):
                        sp.dma_start(counts_sb[:, w, :], counts_t[w + 1]).then_inc(s_ct, 16)
                    sp.dma_start(sums[:, :, :], edge_sum).then_inc(s_ct, 16)
                    sp.wait_ge(s_ct, 16 * NW + 16)

                @block.vector
                def _(dve):
                    step = Chain(dve, s_ch)
                    split3(step, dve, parts, y[:, :, :], x[:, :, :])

            dense_sum("neighbours", counts_sb, parts, y)
            sum_by_edge("edges_last", x[:, :, :], y)
            s_res = ph.sem("s_res")
            norm = Norm(ph, "norm", stat, minus_half)
            with nc.Block() as block:

                @block.gpsimd
                def _(pool):
                    norm.on_gpsimd(pool)

                @block.vector
                def _(dve):
                    step = Chain(dve, s_ch2)
                    step(dve.tensor_tensor(y[:, :, :], y[:, :, :], sums[:, :, :], ALU.add))
                    step(dve.tensor_tensor(tmp[:, :, :], x[:, :, :], over(deg[:, :], F), ALU.mult))
                    step(dve.tensor_tensor(y[:, :, :], y[:, :, :], tmp[:, :, :], ALU.add))
                    step(dve.tensor_tensor(y[:, :, :], y[:, :, :], x[:, :, :], ALU.add))
                    norm.on_vector(step, dve, y[:, :, :], x[:, :, :], tmp[:, :, :])
                    dve.sem_inc(s_res, 1)

                @block.sync
                def _(sp):
                    sp.wait_ge(s_res, 1)
                    with nc.allow_non_contiguous_dma("rows"):
                        sp.dma_start(out.rearrange("(w p) f -> p w f", p=WN), x[:, :, :]).then_inc(s_out, 16)
                    sp.wait_ge(s_out, 16)


def kernel(**inputs):
    import numpy as np
    import concourse.bacc as bacc
    from concourse.bass_utils import run_bass_kernel_spmd

    nc = bacc.Bacc("TRN2", target_bir_lowering=False, num_devices=1)
    arrays, args = {}, {}
    for name in inputs:
        if name == "edge_attr_3":
            continue
        arr = np.ascontiguousarray(inputs[name])
        if arr.ndim == 0:
            arr = arr.reshape(1)
        arrays["in_" + name] = arr
        args[name] = nc.dram_tensor("in_" + name, arr.shape, mybir.dt.from_np(arr.dtype), kind="ExternalInput").ap()
    out = nc.dram_tensor("out", (N, F), F32, kind="ExternalOutput").ap()
    build(nc, args, out)
    got = run_bass_kernel_spmd(nc, [arrays], core_ids=[0])
    return got.results[0]["out"]
```
